# Optimizing a Trainium2 kernel written in Bass

```python
import numpy as np
import jax
import jax.numpy as jnp

def _softmax(x, axis=-1):
    return jax.nn.softmax(x, axis=axis)

def _gelu(x):
    return jax.nn.gelu(x, approximate=True)

def _silu(x):
    return jax.nn.silu(x)

def _sigmoid(x):
    return jax.nn.sigmoid(x)

def _layernorm(x, axis=-1, eps=1e-05):
    m = jnp.mean(x, axis=axis, keepdims=True)
    v = jnp.var(x, axis=axis, keepdims=True)
    return (x - m) / jnp.sqrt(v + eps)

def _scatter_add(tgt, idx, src, axis=0):
    return tgt.at[idx].add(src)

def _segment_sum(src, seg, n):
    return jax.ops.segment_sum(src, seg, n)
kernel_name = 'mk_sandwich_d1_jaxref_r4_33d79a'

def setup_inputs(seed: int=0):
    np.random.seed(seed)
    _w = jnp.asarray

    def _L0_attn_setup():
        import jax, jax.numpy as jnp
        import numpy as np
        N_EMBED = 256
        N_HEAD = 16
        N_GROUP = 4
        NUM_KV_HEAD = N_HEAD // N_GROUP
        HEAD_DIM = N_EMBED // N_HEAD
        B, T = (2, 512)
        key = jax.random.key(seed)
        ks = jax.random.split(key, 9)
        s = 0.02
        kv_dim = NUM_KV_HEAD * HEAD_DIM
        return {'x': jax.random.normal(ks[0], (B, T, N_EMBED), dtype=jnp.float32), 'w_q': jax.random.normal(ks[1], (N_EMBED, N_EMBED), dtype=jnp.float32) * s, 'b_q': jnp.zeros((N_EMBED,), dtype=jnp.float32), 'w_k': jax.random.normal(ks[2], (N_EMBED, kv_dim), dtype=jnp.float32) * s, 'b_k': jnp.zeros((kv_dim,), dtype=jnp.float32), 'w_v': jax.random.normal(ks[3], (N_EMBED, kv_dim), dtype=jnp.float32) * s, 'b_v': jnp.zeros((kv_dim,), dtype=jnp.float32), 'w_o': jax.random.normal(ks[4], (N_EMBED, N_EMBED), dtype=jnp.float32) * s, 'b_o': jnp.zeros((N_EMBED,), dtype=jnp.float32)}
    _L0_attn_in = _L0_attn_setup()

    def _L0_ffn_setup():
        import jax, jax.numpy as jnp
        import numpy as np
        DIM = 256
        H = 8
        DH = 64
        W = 64
        NQ = 128
        NKV = 256
        EPS = 1.0
        NITERS = 50
        FETCH = 9.0 / 8.0
        SCALE = DH ** (-0.5)

        def _ln(x, w, b):
            m = x.mean(-1, keepdims=True)
            v = ((x - m) ** 2).mean(-1, keepdims=True)
            return (x - m) * jax.lax.rsqrt(v + 1e-05) * w + b

        def _rms(x, g):
            n = jnp.maximum(jnp.linalg.norm(x, axis=-1, keepdims=True), 1e-12)
            return x / n * np.sqrt(DIM).astype(np.float32) * g

        def local_attn(x, Wqkv, Wout):
            b, n, _ = x.shape
            nw = n // W
            qkv = x @ Wqkv.T
            q, k, v = jnp.split(qkv, 3, axis=-1)

            def towin(t):
                return t.reshape(b, nw, W, H, DH).transpose(0, 3, 1, 2, 4)
            q, k, v = map(towin, (q, k, v))

            def expand(t):
                tp = jnp.pad(t, ((0, 0), (0, 0), (1, 1), (0, 0), (0, 0)))
                return jnp.concatenate([tp[:, :, :-2], tp[:, :, 1:-1], tp[:, :, 2:]], axis=3)
            ke, ve = (expand(k), expand(v))
            sim = jnp.einsum('bhnid,bhnjd->bhnij', q, ke) * SCALE
            win = jnp.arange(nw)
            valid = jnp.concatenate([jnp.repeat((win > 0)[:, None], W, 1), jnp.ones((nw, W), bool), jnp.repeat((win < nw - 1)[:, None], W, 1)], axis=1)
            sim = jnp.where(valid[None, None, :, None, :], sim, -1000000000.0)
            attn = jax.nn.softmax(sim, axis=-1)
            o = jnp.einsum('bhnij,bhnjd->bhnid', attn, ve)
            o = o.transpose(0, 2, 3, 1, 4).reshape(b, n, H * DH)
            return o @ Wout.T

        def route(x, routing_token, num_tokens):
            s = jnp.einsum('bnd,rd->brn', x, routing_token).reshape(x.shape[0], x.shape[1])
            n = s.shape[-1]
            logk = jnp.log(jnp.asarray(min(num_tokens * FETCH, float(n)), s.dtype))

            def body(ab, _):
                a, bb = ab
                a = EPS * (logk - jax.nn.logsumexp((s + bb) / EPS, axis=-1, keepdims=True))
                bb = -jax.nn.relu(s + a)
                return ((a, bb), None)
            (a, bb), _ = jax.lax.scan(body, (jnp.zeros((s.shape[0], 1), s.dtype), -s), None, length=NITERS)
            scores = jnp.exp((s + a + bb) / EPS)
            sel_scores, sel_idx = jax.lax.top_k(scores, num_tokens)
            sel_scores = sel_scores + jax.lax.stop_gradient(1.0 - sel_scores)
            return (sel_scores, sel_idx)

        def heavy_attn(xq, ctx, scores_kv, gamma, Wq, Wkv, Wout, null_kv):
            b = xq.shape[0]
            xq = _rms(xq, gamma)
            ctx = _rms(ctx, gamma)
            q = (xq @ Wq.T).reshape(b, -1, H, DH).transpose(0, 2, 1, 3)
            kv = (ctx @ Wkv.T).reshape(b, -1, H, 2 * DH).transpose(0, 2, 1, 3)
            k, v = (kv[..., :DH], kv[..., DH:])
            v = v * scores_kv[:, None, :, None]
            nk = jnp.broadcast_to(null_kv[0][None, :, None, :], (b, H, 1, DH))
            nv = jnp.broadcast_to(null_kv[1][None, :, None, :], (b, H, 1, DH))
            k = jnp.concatenate([nk, k], axis=2)
            v = jnp.concatenate([nv, v], axis=2)
            sim = jnp.einsum('bhid,bhjd->bhij', q, k) * SCALE
            attn = jax.nn.softmax(sim, axis=-1)
            o = jnp.einsum('bhij,bhjd->bhid', attn, v)
            o = o.transpose(0, 2, 1, 3).reshape(b, -1, H * DH)
            return o @ Wout.T
        key = jax.random.key(seed)
        ks = jax.random.split(key, 12)
        D, IN = (DIM, H * DH)
        w = lambda k, shape: jax.random.normal(k, shape, jnp.float32) * 0.02
        return {'x': jax.random.normal(ks[0], (4, 1024, D), jnp.float32), 'ln_w': jnp.ones((D,), jnp.float32), 'ln_b': jnp.zeros((D,), jnp.float32), 'Wqkv': w(ks[1], (3 * IN, D)), 'Wout_l': w(ks[2], (D, IN)), 'rt_q': jax.random.normal(ks[3], (1, D), jnp.float32), 'rt_kv': jax.random.normal(ks[4], (1, D), jnp.float32), 'gamma': jnp.ones((D,), jnp.float32), 'Wq': w(ks[5], (IN, D)), 'Wkv': w(ks[6], (2 * IN, D)), 'Wout_h': w(ks[7], (D, IN)), 'null_kv': jax.random.normal(ks[8], (2, H, DH), jnp.float32), 'null_q': jax.random.normal(ks[9], (D,), jnp.float32)}
    _L0_ffn_in = _L0_ffn_setup()
    _d = {'L0_attn_x': _L0_attn_in['x'], 'L0_attn_w_q': _L0_attn_in['w_q'], 'L0_attn_b_q': _L0_attn_in['b_q'], 'L0_attn_w_k': _L0_attn_in['w_k'], 'L0_attn_b_k': _L0_attn_in['b_k'], 'L0_attn_w_v': _L0_attn_in['w_v'], 'L0_attn_b_v': _L0_attn_in['b_v'], 'L0_attn_w_o': _L0_attn_in['w_o'], 'L0_attn_b_o': _L0_attn_in['b_o'], 'L0_ffn_ln_w': _L0_ffn_in['ln_w'], 'L0_ffn_ln_b': _L0_ffn_in['ln_b'], 'L0_ffn_Wqkv': _L0_ffn_in['Wqkv'], 'L0_ffn_Wout_l': _L0_ffn_in['Wout_l'], 'L0_ffn_rt_q': _L0_ffn_in['rt_q'], 'L0_ffn_rt_kv': _L0_ffn_in['rt_kv'], 'L0_ffn_gamma': _L0_ffn_in['gamma'], 'L0_ffn_Wq': _L0_ffn_in['Wq'], 'L0_ffn_Wkv': _L0_ffn_in['Wkv'], 'L0_ffn_Wout_h': _L0_ffn_in['Wout_h'], 'L0_ffn_null_kv': _L0_ffn_in['null_kv'], 'L0_ffn_null_q': _L0_ffn_in['null_q']}
    _x0 = _d['L0_attn_x']
    _d['L0_attn_x'] = jax.random.normal(jax.random.fold_in(jax.random.key(seed), 1), (4, 2048, 256), dtype=_x0.dtype)
    del _x0
    return _d

def reference(L0_attn_x, L0_attn_w_q, L0_attn_b_q, L0_attn_w_k, L0_attn_b_k, L0_attn_w_v, L0_attn_b_v, L0_attn_w_o, L0_attn_b_o, L0_ffn_ln_w, L0_ffn_ln_b, L0_ffn_Wqkv, L0_ffn_Wout_l, L0_ffn_rt_q, L0_ffn_rt_kv, L0_ffn_gamma, L0_ffn_Wq, L0_ffn_Wkv, L0_ffn_Wout_h, L0_ffn_null_kv, L0_ffn_null_q):

    def _L0_attn_ref(x, w_q, b_q, w_k, b_k, w_v, b_v, w_o, b_o):
        import jax, jax.numpy as jnp
        import numpy as np
        N_EMBED = 256
        N_HEAD = 16
        N_GROUP = 4
        NUM_KV_HEAD = N_HEAD // N_GROUP
        HEAD_DIM = N_EMBED // N_HEAD
        B, T = (2, 512)
        Bq, Tq, C = x.shape
        q = x @ w_q + b_q
        k = x @ w_k + b_k
        v = x @ w_v + b_v
        q = q.reshape(Bq, Tq, NUM_KV_HEAD, N_GROUP, HEAD_DIM)
        k = k.reshape(Bq, Tq, NUM_KV_HEAD, HEAD_DIM)
        v = v.reshape(Bq, Tq, NUM_KV_HEAD, HEAD_DIM)
        scale = 1.0 / np.sqrt(HEAD_DIM).astype(np.float32)
        attn = jnp.einsum('btkgd,bskd->bkgts', q, k) * scale
        causal = jnp.tril(jnp.ones((Tq, Tq), dtype=bool))
        attn = jnp.where(causal, attn, -jnp.inf)
        attn = jax.nn.softmax(attn, axis=-1)
        out = jnp.einsum('bkgts,bskd->btkgd', attn, v)
        out = out.reshape(Bq, Tq, C)
        return out @ w_o + b_o

    def _L0_ffn_ref(x, ln_w, ln_b, Wqkv, Wout_l, rt_q, rt_kv, gamma, Wq, Wkv, Wout_h, null_kv, null_q):
        import jax, jax.numpy as jnp
        import numpy as np
        DIM = 256
        H = 8
        DH = 64
        W = 64
        NQ = 128
        NKV = 256
        EPS = 1.0
        NITERS = 50
        FETCH = 9.0 / 8.0
        SCALE = DH ** (-0.5)

        def _ln(x, w, b):
            m = x.mean(-1, keepdims=True)
            v = ((x - m) ** 2).mean(-1, keepdims=True)
            return (x - m) * jax.lax.rsqrt(v + 1e-05) * w + b

        def _rms(x, g):
            n = jnp.maximum(jnp.linalg.norm(x, axis=-1, keepdims=True), 1e-12)
            return x / n * np.sqrt(DIM).astype(np.float32) * g

        def local_attn(x, Wqkv, Wout):
            b, n, _ = x.shape
            nw = n // W
            qkv = x @ Wqkv.T
            q, k, v = jnp.split(qkv, 3, axis=-1)

            def towin(t):
                return t.reshape(b, nw, W, H, DH).transpose(0, 3, 1, 2, 4)
            q, k, v = map(towin, (q, k, v))

            def expand(t):
                tp = jnp.pad(t, ((0, 0), (0, 0), (1, 1), (0, 0), (0, 0)))
                return jnp.concatenate([tp[:, :, :-2], tp[:, :, 1:-1], tp[:, :, 2:]], axis=3)
            ke, ve = (expand(k), expand(v))
            sim = jnp.einsum('bhnid,bhnjd->bhnij', q, ke) * SCALE
            win = jnp.arange(nw)
            valid = jnp.concatenate([jnp.repeat((win > 0)[:, None], W, 1), jnp.ones((nw, W), bool), jnp.repeat((win < nw - 1)[:, None], W, 1)], axis=1)
            sim = jnp.where(valid[None, None, :, None, :], sim, -1000000000.0)
            attn = jax.nn.softmax(sim, axis=-1)
            o = jnp.einsum('bhnij,bhnjd->bhnid', attn, ve)
            o = o.transpose(0, 2, 3, 1, 4).reshape(b, n, H * DH)
            return o @ Wout.T

        def route(x, routing_token, num_tokens):
            s = jnp.einsum('bnd,rd->brn', x, routing_token).reshape(x.shape[0], x.shape[1])
            n = s.shape[-1]
            logk = jnp.log(jnp.asarray(min(num_tokens * FETCH, float(n)), s.dtype))

            def body(ab, _):
                a, bb = ab
                a = EPS * (logk - jax.nn.logsumexp((s + bb) / EPS, axis=-1, keepdims=True))
                bb = -jax.nn.relu(s + a)
                return ((a, bb), None)
            (a, bb), _ = jax.lax.scan(body, (jnp.zeros((s.shape[0], 1), s.dtype), -s), None, length=NITERS)
            scores = jnp.exp((s + a + bb) / EPS)
            sel_scores, sel_idx = jax.lax.top_k(scores, num_tokens)
            sel_scores = sel_scores + jax.lax.stop_gradient(1.0 - sel_scores)
            return (sel_scores, sel_idx)

        def heavy_attn(xq, ctx, scores_kv, gamma, Wq, Wkv, Wout, null_kv):
            b = xq.shape[0]
            xq = _rms(xq, gamma)
            ctx = _rms(ctx, gamma)
            q = (xq @ Wq.T).reshape(b, -1, H, DH).transpose(0, 2, 1, 3)
            kv = (ctx @ Wkv.T).reshape(b, -1, H, 2 * DH).transpose(0, 2, 1, 3)
            k, v = (kv[..., :DH], kv[..., DH:])
            v = v * scores_kv[:, None, :, None]
            nk = jnp.broadcast_to(null_kv[0][None, :, None, :], (b, H, 1, DH))
            nv = jnp.broadcast_to(null_kv[1][None, :, None, :], (b, H, 1, DH))
            k = jnp.concatenate([nk, k], axis=2)
            v = jnp.concatenate([nv, v], axis=2)
            sim = jnp.einsum('bhid,bhjd->bhij', q, k) * SCALE
            attn = jax.nn.softmax(sim, axis=-1)
            o = jnp.einsum('bhij,bhjd->bhid', attn, v)
            o = o.transpose(0, 2, 1, 3).reshape(b, -1, H * DH)
            return o @ Wout.T
        b, n, d = x.shape
        light = local_attn(_ln(x, ln_w, ln_b), Wqkv, Wout_l)
        sq, iq = route(x, rt_q, NQ)
        skv, ikv = route(x, rt_kv, NKV)
        br = jnp.arange(b)[:, None]
        xq = x[br, iq]
        xkv = x[br, ikv]
        heavy = heavy_attn(xq, xkv, skv, gamma, Wq, Wkv, Wout_h, null_kv)
        heavy = heavy * sq[..., None]
        out = jnp.broadcast_to(null_q[None, None, :], (b, n, d))
        out = out.at[br, iq].set(heavy)
        return out + light
    x = L0_attn_x
    x = x + _layernorm(_L0_attn_ref(_layernorm(x, axis=-1), L0_attn_w_q, L0_attn_b_q, L0_attn_w_k, L0_attn_b_k, L0_attn_w_v, L0_attn_b_v, L0_attn_w_o, L0_attn_b_o), axis=-1)
    x = x + _layernorm(_L0_ffn_ref(_layernorm(x, axis=-1), L0_ffn_ln_w, L0_ffn_ln_b, L0_ffn_Wqkv, L0_ffn_Wout_l, L0_ffn_rt_q, L0_ffn_rt_kv, L0_ffn_gamma, L0_ffn_Wq, L0_ffn_Wkv, L0_ffn_Wout_h, L0_ffn_null_kv, L0_ffn_null_q), axis=-1)
    return x

_drawn_inputs = setup_inputs


def setup_inputs(seed=0):
    import zlib

    import numpy as np

    out = dict(_drawn_inputs(seed))
    spreads = {'L0_attn_b_q': (0.0, 0.644),
     'L0_attn_b_k': (0.0, 2.0),
     'L0_attn_b_v': (0.0, 0.1),
     'L0_attn_b_o': (0.0, 0.1),
     'L0_ffn_ln_w': (1.0, 0.6),
     'L0_ffn_ln_b': (0.0, 0.533),
     'L0_ffn_gamma': (1.0, 0.6)}
    factors = {'L0_attn_w_q': 3.13,
     'L0_attn_w_k': 3.109,
     'L0_ffn_rt_kv': 39.52,
     'L0_ffn_Wq': 8.0,
     'L0_ffn_null_kv': 8.0,
     'L0_ffn_Wkv': 4.245}
    for name, (base, spread) in spreads.items():
        noise = np.random.default_rng([zlib.crc32(name.encode()), seed]).standard_normal(out[name].shape)
        drawn = base * np.exp(spread * noise) if base else spread * noise
        out[name] = jnp.asarray(drawn.astype(out[name].dtype))
    for name, factor in factors.items():
        out[name] = (out[name] * factor).astype(out[name].dtype)
    return out
```

```python
import concourse.bass as bass
import numpy as np
from concourse import mybir
from contextlib import ExitStack

fp32 = mybir.dt.float32
bf16 = mybir.dt.bfloat16
i32 = mybir.dt.int32
ALU = mybir.AluOpType
ACT = mybir.ActivationFunctionType
AX = mybir.AxisListType

BATCH, SEQ, DIM = 4, 2048, 256
TOKENS = BATCH * SEQ
P = 128
TILES = TOKENS // P
TILES_B = SEQ // P
BLOCK = 512
BT = BLOCK // P
BLOCKS_B = SEQ // BLOCK
HALVES = DIM // P
EPS = 1e-5
HEADS, KV, GROUP, HD = 16, 4, 4, 16
KVD = KV * HD
PARTS = 3
Q_PART = (0, 0, 1, 1, 0, 2)
K_PART = (0, 1, 0, 1, 2, 0)
SLOTS = len(Q_PART)
STACK = SLOTS * HD
ROWS = STACK + 2
A_SCALE = 1.0 / float(HD) ** 0.5
FAR = -1e38
GUARD = 50.0


class Steps:

    def __init__(self, sem, per=1, lead=2):
        self.sem, self.per, self.lead = sem, per, lead

    def open(self, eng):
        eng.sem_inc(self.sem, self.lead * self.per)

    def after(self, step):
        return (step + 1 + self.lead) * self.per


def apart(engine, s):
    engine.sem_inc(s.passed[engine.engine], 1)


def inverse_root(pool, s, out, var, power, inverted, step):
    apart(pool, s)
    pool.tensor_scalar(out, var, EPS, None, ALU.add).then_inc(inverted.sem, 1)
    pool.wait_ge(inverted.sem, inverted.after(step - 1) + 1)
    pool.tensor_tensor(out, out, power, ALU.pow).then_inc(inverted.sem, 1)


def constants(nc, s):
    with nc.semaphore("const_filled") as const_filled, nc.semaphore("const_zero_out") as zero_out, \
            nc.semaphore("const_loaded") as loaded, nc.semaphore("rows_filled") as rows_filled, nc.Block() as block:

        @block.gpsimd
        def _(pool):
            pool.memset(s.ident[:], 0.0).then_inc(const_filled, 1)
            pool.memset(s.heads_of[:], 1.0).then_inc(const_filled, 1)
            pool.wait_ge(const_filled, 2)
            pool.affine_select(out=s.ident[:], in_=s.ident[:], compare_op=ALU.not_equal, fill=1.0,
                               base=0, pattern=[[-1, P]], channel_multiplier=1).then_inc(const_filled, 1)
            pool.affine_select(out=s.heads_of[:], in_=s.heads_of[:], compare_op=ALU.is_ge, fill=0.0,
                               base=0, pattern=[[-HD, 8]], channel_multiplier=1).then_inc(const_filled, 1)
            pool.wait_ge(const_filled, 4)
            pool.affine_select(out=s.heads_of[:], in_=s.heads_of[:], compare_op=ALU.is_ge, fill=0.0,
                               base=HD - 1, pattern=[[HD, 8]], channel_multiplier=-1).then_inc(const_filled, 1)
            pool.wait_ge(const_filled, 5)
            pool.memset(s.norm_sel[:], 0.0).then_inc(const_filled, 1)
            pool.wait_ge(const_filled, 6)
            pool.tensor_copy(s.norm_sel[:, 0, 0:8], s.heads_of[:]).then_inc(const_filled, 1)
            pool.tensor_copy(s.norm_sel[:, 1, 8:16], s.heads_of[:]).then_inc(const_filled, 1)
            pool.tensor_copy(s.norm_sel[0:KVD, 2, 16:20], s.heads_of[0:KVD, 0:KV]).then_inc(const_filled, 1)

        @block.vector
        def _(dve):
            dve.memset(s.v_all[:, :, :, HD:], 1.0).then_inc(rows_filled, 1)
            dve.memset(s.k_stack[STACK:ROWS, :, :], 1.0).then_inc(rows_filled, 1)
            dve.memset(s.zero_row[:], 0.0).then_inc(rows_filled, 1)
            dve.memset(s.power[:], -0.5).then_inc(rows_filled, 1)
            dve.memset(s.half[:], 0.5).then_inc(rows_filled, 1)

        @block.sync
        def _(sp):
            sp.dma_start(s.w_q[:], s.d_w_q.rearrange("(k p) n -> p k n", p=P)).then_inc(loaded, 16)
            sp.dma_start(s.w_k[:], s.d_w_k.rearrange("(k p) n -> p k n", p=P)).then_inc(loaded, 16)
            sp.dma_start(s.w_v[:], s.d_w_v.rearrange("(k p) n -> p k n", p=P)).then_inc(loaded, 16)
            sp.dma_start(s.b_q[:], s.d_b_q.rearrange("(k p) -> p k", p=P), allow_slow_non_contiguous=True).then_inc(loaded, 16)
            sp.dma_start(s.b_k[:], s.d_b_k.rearrange("(p k) -> p k", k=1), allow_slow_non_contiguous=True).then_inc(loaded, 16)
            sp.dma_start(s.b_v[:], s.d_b_v.rearrange("(a n) -> a n", a=1).broadcast_to([P, KVD]))\
              .then_inc(loaded, 16)
            sp.wait_ge(rows_filled, 3)
            sp.dma_start(s.d_shift, s.zero_row[:]).then_inc(zero_out, 16)
            sp.wait_ge(loaded, 6 * 16)
            sp.wait_ge(zero_out, 16)


def project(nc, s):
    with ExitStack() as ctx:
        def sb(name, shape, dt=fp32):
            return ctx.enter_context(nc.sbuf_tensor(name, shape, dt))

        def ps(name, shape):
            return ctx.enter_context(nc.psum_tensor(name, shape, fp32))

        def sem(name):
            return ctx.enter_context(nc.semaphore(name))

        x_in = sb("x_in", [P, 2, BT, DIM])
        stats = sb("stats", [P, BT, 6])
        mean_var = sb("mean_var", [P, BT, 2])
        inv = sb("inv", [P, BT])
        x_n = sb("x_n", [P, 2, BT, DIM])
        x_t = sb("x_t", [P, 2, HALVES, BLOCK])
        q_f = sb("q_f", [P, 2, HALVES, BLOCK])
        k_f = sb("k_f", [KVD, 2, BLOCK])
        q_sq = sb("q_sq", [P, HALVES, BLOCK], bf16)
        k_sq = sb("k_sq", [KVD, BLOCK], bf16)
        q_p = sb("q_p", [P, 2, PARTS, HALVES, BLOCK], bf16)
        k_p = sb("k_p", [KVD, 2, PARTS, BLOCK], bf16)
        q_rest = sb("q_rest", [P, HALVES, BLOCK])
        k_rest = sb("k_rest", [KVD, BLOCK])
        p_t = ps("p_t", [P, HALVES, BLOCK])
        p_q = ps("p_q", [P, HALVES, BLOCK])
        p_k = ps("p_k", [P, BLOCK])
        p_v = ps("p_v", [P, BLOCK])
        p_norm = ps("p_norm", [P, BLOCK])

        def steps(name, per=1):
            return Steps(sem(name), per)

        x_loaded = [steps(f"x_loaded_{u}", 16) for u in range(2)]
        normed, norm_step, inverted = steps("normed"), steps("norm_step", 2), steps("inverted", 2)
        transposed, x_t_ready = steps("transposed"), steps("x_t_ready")
        projected, biased, v_ready = steps("projected"), steps("biased"), steps("v_ready")
        q_split, k_split = steps("q_split", 4), steps("k_split", 4)
        q_out = [steps(f"q_out_{u}", 32) for u in range(2)]
        k_out = [steps(f"k_out_{u}", 16) for u in range(2)]
        squared, norms, norms_read = steps("squared"), steps("norms"), steps("norms_read")
        block = ctx.enter_context(nc.Block())

        @block.sync
        def _(sp):
            for made in (*x_loaded, *q_out, *k_out):
                made.open(sp)

            def store(g, b, c):
                u = c % 2
                sp.wait_ge(q_split.sem, q_split.after(g))
                for m in range(HALVES):
                    sp.dma_start(s.d_q_parts[:, bass.ds(b * 2 + m, 1), :, bass.ts(c, BLOCK)]
                                 .rearrange("r a p n -> p r (a n)"), q_p[:, u, :, m, :]).then_inc(q_out[u].sem, 16)
                sp.wait_ge(k_split.sem, k_split.after(g))
                sp.dma_start(s.d_k_parts[:, bass.ds(b, 1), :, bass.ts(c, BLOCK)]
                             .rearrange("r a p n -> p r (a n)"), k_p[:, u, :, :]).then_inc(k_out[u].sem, 16)

            with sp.Fori(0, BATCH) as b:
                for c in range(BLOCKS_B):
                    g = b * BLOCKS_B + c
                    sp.wait_ge(normed.sem, normed.after(g - 2))
                    sp.dma_start(x_in[:, c % 2], s.d_x[bass.ds(b * TILES_B + BT * c, BT)].rearrange("t p d -> p t d"))\
                      .then_inc(x_loaded[c % 2].sem, 16)
                    if c > 0:
                        store(g - 1, b, c - 1)
                store(b * BLOCKS_B + BLOCKS_B - 1, b, BLOCKS_B - 1)
            for u in range(2):
                sp.wait_ge(q_out[u].sem, q_out[u].after(BATCH * BLOCKS_B // 2 - 1))
                sp.wait_ge(k_out[u].sem, k_out[u].after(BATCH * BLOCKS_B // 2 - 1))

        @block.vector
        def _(dve):
            for made in (normed, norm_step, v_ready, q_split, norms_read):
                made.open(dve)
            with dve.Fori(0, BATCH) as b:
                for c in range(BLOCKS_B):
                    g = b * BLOCKS_B + c
                    u = c % 2
                    v = b * (BLOCKS_B // 2) + c // 2
                    dve.wait_ge(x_loaded[u].sem, x_loaded[u].after(v))
                    for t in range(BT):
                        last = dve.bn_stats(stats[:, t], x_in[:, u, t])
                    last.then_inc(norm_step.sem, 1)
                    dve.wait_ge(norm_step.sem, norm_step.after(g - 1) + 1)
                    apart(dve, s)
                    for t in range(BT):
                        last = dve.bn_aggr(mean_var[:, t], stats[:, t])
                    last.then_inc(norm_step.sem, 1)
                    dve.wait_ge(inverted.sem, inverted.after(g))
                    dve.wait_ge(transposed.sem, transposed.after(g - 2))
                    for t in range(BT):
                        last = dve.tensor_scalar(x_n[:, u, t], x_in[:, u, t], mean_var[:, t, 0:1], inv[:, t:t + 1],
                                                 ALU.subtract, ALU.mult)
                    last.then_inc(normed.sem, 1)
                    dve.wait_ge(projected.sem, projected.after(g))
                    for t in range(BT):
                        out = s.v_all[:, bass.ds(b * KV, KV), BT * c + t, 0:HD]
                        last = dve.tensor_tensor(out, p_v[:, KVD * t:KVD * t + KVD].rearrange("p (k d) -> p k d", k=KV),
                                                 s.b_v[:].rearrange("p (k d) -> p k d", k=KV), ALU.add)
                    last.then_inc(v_ready.sem, 1)
                    dve.wait_ge(biased.sem, biased.after(g))
                    dve.wait_ge(q_out[u].sem, q_out[u].after(v - 1))
                    dve.tensor_copy(q_p[:, u, 0], q_f[:, u]).then_inc(q_split.sem, 1)
                    dve.wait_ge(q_split.sem, q_split.after(g - 1) + 1)
                    dve.tensor_tensor(q_rest[:], q_f[:, u], q_p[:, u, 0], ALU.subtract).then_inc(q_split.sem, 1)
                    dve.wait_ge(q_split.sem, q_split.after(g - 1) + 2)
                    dve.tensor_copy(q_p[:, u, 1], q_rest[:]).then_inc(q_split.sem, 1)
                    dve.wait_ge(q_split.sem, q_split.after(g - 1) + 3)
                    dve.tensor_tensor(q_p[:, u, 2], q_rest[:], q_p[:, u, 1], ALU.subtract).then_inc(q_split.sem, 1)
                    dve.wait_ge(norms.sem, norms.after(g))
                    dve.tensor_reduce(s.norm_max[:, bass.ds(g, 1)], p_norm[0:20, :], AX.X, ALU.max)\
                       .then_inc(norms_read.sem, 1)

        @block.gpsimd
        def _(pool):
            k_split.open(pool)
            inverted.open(pool)
            with pool.Fori(0, BATCH) as b:
                for c in range(BLOCKS_B):
                    g = b * BLOCKS_B + c
                    u = c % 2
                    pool.wait_ge(norm_step.sem, norm_step.after(g))
                    pool.wait_ge(normed.sem, normed.after(g - 1))
                    inverse_root(pool, s, inv[:], mean_var[:, :, 1], s.power[:, 0:BT], inverted, g)
                    pool.wait_ge(biased.sem, biased.after(g))
                    pool.wait_ge(k_out[u].sem, k_out[u].after(b * (BLOCKS_B // 2) + c // 2 - 1))
                    apart(pool, s)
                    pool.tensor_copy(k_p[:, u, 0], k_f[:, u]).then_inc(k_split.sem, 1)
                    pool.wait_ge(k_split.sem, k_split.after(g - 1) + 1)
                    pool.tensor_tensor(k_rest[:], k_f[:, u], k_p[:, u, 0], ALU.subtract).then_inc(k_split.sem, 1)
                    pool.wait_ge(k_split.sem, k_split.after(g - 1) + 2)
                    apart(pool, s)
                    pool.tensor_copy(k_p[:, u, 1], k_rest[:]).then_inc(k_split.sem, 1)
                    pool.wait_ge(k_split.sem, k_split.after(g - 1) + 3)
                    pool.tensor_tensor(k_p[:, u, 2], k_rest[:], k_p[:, u, 1], ALU.subtract).then_inc(k_split.sem, 1)

        @block.scalar
        def _(act):
            for made in (x_t_ready, biased, squared):
                made.open(act)
            with act.Fori(0, BATCH) as b:
                for c in range(BLOCKS_B):
                    g = b * BLOCKS_B + c
                    u = c % 2
                    act.wait_ge(transposed.sem, transposed.after(g))
                    act.wait_ge(projected.sem, projected.after(g - 2))
                    act.activation(x_t[:, u], p_t[:], ACT.Copy).then_inc(x_t_ready.sem, 1)
                    act.wait_ge(projected.sem, projected.after(g))
                    act.wait_ge(q_split.sem, q_split.after(g - 2))
                    act.wait_ge(k_split.sem, k_split.after(g - 2))
                    for m in range(HALVES):
                        act.activation(q_f[:, u, m], p_q[:, m, :], ACT.Identity, bias=s.b_q[:, m:m + 1])
                    act.activation(k_f[:, u], p_k[0:KVD, :], ACT.Identity, bias=s.b_k[:]).then_inc(biased.sem, 1)
                    act.wait_ge(biased.sem, biased.after(g))
                    act.wait_ge(norms.sem, norms.after(g - 1))
                    act.activation(q_sq[:], q_f[:, u], ACT.Square)
                    act.activation(k_sq[:], k_f[:, u], ACT.Square).then_inc(squared.sem, 1)

        @block.tensor
        def _(pe):
            for made in (transposed, projected, norms):
                made.open(pe)
            with pe.Fori(0, BATCH) as b:
                for c in range(BLOCKS_B):
                    g = b * BLOCKS_B + c
                    u = c % 2
                    pe.wait_ge(normed.sem, normed.after(g))
                    pe.wait_ge(x_t_ready.sem, x_t_ready.after(g - 1))
                    for t in range(BT):
                        for h in range(HALVES):
                            last = nc.tensor.transpose(p_t[:, h, P * t:P * t + P], x_n[:, u, t, P * h:P * h + P], s.ident[:])
                    last.then_inc(transposed.sem, 1)
                    pe.wait_ge(x_t_ready.sem, x_t_ready.after(g))
                    pe.wait_ge(biased.sem, biased.after(g - 1))
                    for m in range(HALVES):
                        for k in range(HALVES):
                            nc.tensor.matmul(p_q[:, m, :], s.w_q[:, k, P * m:P * m + P], x_t[:, u, k, :],
                                             start=(k == 0), stop=(k == HALVES - 1))
                    for k in range(HALVES):
                        nc.tensor.matmul(p_k[0:KVD, :], s.w_k[:, k, :], x_t[:, u, k, :],
                                         start=(k == 0), stop=(k == HALVES - 1))
                    pe.wait_ge(v_ready.sem, v_ready.after(g - 1))
                    for t in range(BT):
                        for k in range(HALVES):
                            last = nc.tensor.matmul(p_v[:, KVD * t:KVD * t + KVD], x_t[:, u, k, P * t:P * t + P],
                                                    s.w_v[:, k, :], start=(k == 0), stop=(k == HALVES - 1))
                    last.then_inc(projected.sem, 1)
                    pe.wait_ge(squared.sem, squared.after(g))
                    pe.wait_ge(norms_read.sem, norms_read.after(g - 1))
                    nc.tensor.matmul(p_norm[0:20, :], s.norm_sel[:, 0, :], q_sq[:, 0, :], start=True, stop=False)
                    nc.tensor.matmul(p_norm[0:20, :], s.norm_sel[:, 1, :], q_sq[:, 1, :], start=False, stop=False)
                    nc.tensor.matmul(p_norm[0:20, :], s.norm_sel[0:KVD, 2, :], k_sq[:], start=False, stop=True)\
                      .then_inc(norms.sem, 1)


def bound_scores(nc, s):
    with nc.sbuf_tensor("norm_all", [20, 1], fp32) as norm_all, nc.sbuf_tensor("norm_top", [1, 4], fp32) as norm_top, \
            nc.psum_tensor("norm_row", [1, 20], fp32) as norm_row, nc.semaphore("bounded") as bounded, \
            nc.semaphore("norm_turned") as turned, nc.Block() as block:

        @block.tensor
        def _(pe):
            pe.wait_ge(bounded, 1)
            nc.tensor.matmul(norm_row[:], norm_all[:], s.ident[0:20, 0:20], start=True, stop=True).then_inc(turned, 1)

        @block.vector
        def _(dve):
            dve.tensor_reduce(norm_all[:], s.norm_max[:], AX.X, ALU.max).then_inc(bounded, 1)
            dve.wait_ge(turned, 1)
            dve.tensor_reduce(norm_top[:, 0:1], norm_row[:, 0:HEADS], AX.X, ALU.max)
            dve.tensor_reduce(norm_top[:, 1:2], norm_row[:, HEADS:], AX.X, ALU.max).then_inc(bounded, 1)
            dve.wait_ge(bounded, 2)
            dve.tensor_tensor(norm_top[:, 2:3], norm_top[:, 0:1], norm_top[:, 1:2], ALU.mult).then_inc(bounded, 1)
            dve.wait_ge(bounded, 3)
            dve.tensor_scalar(norm_top[:, 3:4], norm_top[:, 2:3], (GUARD / A_SCALE) ** 2, None, ALU.is_le).then_inc(bounded, 1)
            dve.wait_ge(bounded, 4)
            dve.tensor_scalar(s.loose[:], norm_top[:, 3:4], -1.0, 1.0, ALU.mult, ALU.add).then_inc(bounded, 1)
            dve.wait_ge(bounded, 5)


def largest_scores(nc, s):
    PAIRS = BATCH * KV
    with ExitStack() as ctx:
        def sb(name, shape, dt=fp32):
            return ctx.enter_context(nc.sbuf_tensor(name, shape, dt))

        def steps(name, per=1, lead=2):
            return Steps(ctx.enter_context(nc.semaphore(name)), per, lead)

        q_stack = sb("m_q_stack", [STACK, GROUP, SEQ], bf16)
        ahead, masked = sb("ahead", [P, P]), sb("m_masked", [P, P])
        found = sb("found", [P, 2, GROUP, TILES_B])
        least = sb("least", [P, GROUP * TILES_B])
        rest = sb("m_rest", [GROUP * TILES_B, P])
        parts = sb("m_parts", [GROUP * TILES_B, 2, P], bf16)
        scores = ctx.enter_context(nc.psum_tensor("m_scores", [P, SEQ], fp32))
        turned = ctx.enter_context(nc.psum_tensor("m_turned", [GROUP * TILES_B, P], fp32))
        jobs = [(h, t) for h in range(GROUP) for t in range(TILES_B)]
        filled = ctx.enter_context(nc.semaphore("m_filled"))
        loaded, stored = steps("m_loaded", 16 * 2 * SLOTS), steps("m_stored", 16)
        scored, masked_done, taken = steps("m_scored"), steps("m_masked_done"), steps("m_taken")
        joined, split, flipped = steps("m_joined", 2), steps("m_split", 3), steps("m_flipped")
        block = ctx.enter_context(nc.Block())

        @block.gpsimd
        def _(pool):
            with pool.If(pool.value_load(s.loose[:], min_val=0, max_val=1) > 0):
                pool.memset(ahead[:], 0.0).then_inc(filled, 1)
                pool.wait_ge(filled, 1)
                pool.affine_select(out=ahead[:], in_=ahead[:], compare_op=ALU.is_ge, fill=FAR, base=0, pattern=[[-1, P]],
                                   channel_multiplier=1).then_inc(filled, 1)
            with pool.Else():
                pass

        @block.sync
        def _(sp):
            with sp.If(sp.value_load(s.loose[:], min_val=0, max_val=1) > 0):
                loaded.open(sp)
                stored.open(sp)
                with sp.Fori(0, PAIRS) as j:
                    sp.wait_ge(joined.sem, joined.after(j - 1))
                    for n in range(SLOTS):
                        rows = slice(HD * n, HD * n + HD)
                        sp.dma_start(s.k_stack[rows, 0, :], s.k_rows[K_PART[n], bass.ds(j, 1)].rearrange("a p n -> p (a n)"))\
                          .then_inc(loaded.sem, 16)
                        sp.dma_start(q_stack[rows], s.q_rows[Q_PART[n], bass.ds(j * GROUP, GROUP)].rearrange("h p n -> p h n"))\
                          .then_inc(loaded.sem, 16)
                    sp.wait_ge(split.sem, split.after(j))
                    sp.dma_start(s.d_shift[:, bass.ds(j * GROUP, GROUP)].rearrange("r h (t n) -> (h t) r n", n=P), parts[:])\
                      .then_inc(stored.sem, 16)
                sp.wait_ge(stored.sem, stored.after(PAIRS - 1))
            with sp.Else():
                pass

        @block.tensor
        def _(pe):
            with pe.If(pe.value_load(s.loose[:], min_val=0, max_val=1) > 0):
                scored.open(pe)
                flipped.open(pe)
                with pe.Fori(0, PAIRS) as j:
                    pe.wait_ge(loaded.sem, loaded.after(j))
                    for n, (h, t) in enumerate(jobs):
                        pe.wait_ge(taken.sem, taken.after(j * len(jobs) + n - 1))
                        keys = P * (t + 1)
                        for at in range(0, keys, BLOCK):
                            width = min(BLOCK, keys - at)
                            last = nc.tensor.matmul(scores[:, at:at + width], q_stack[:, h, P * t:P * t + P],
                                                    s.k_stack[0:STACK, 0, at:at + width], start=True, stop=True)
                        last.then_inc(scored.sem, 1)
                    pe.wait_ge(joined.sem, joined.after(j))
                    pe.wait_ge(split.sem, split.after(j - 1))
                    apart(pe, s)
                    nc.tensor.transpose(turned[:], least[:], s.ident[:]).then_inc(flipped.sem, 1)
            with pe.Else():
                pass

        @block.vector
        def _(dve):
            with dve.If(dve.value_load(s.loose[:], min_val=0, max_val=1) > 0):
                for made in (masked_done, taken, joined, split):
                    made.open(dve)
                dve.wait_ge(filled, 2)
                dve.memset(found[:], FAR).then_inc(filled, 1)
                dve.wait_ge(filled, 3)
                with dve.Fori(0, PAIRS) as j:
                    for n, (h, t) in enumerate(jobs):
                        job = j * len(jobs) + n
                        own = P * t
                        dve.wait_ge(scored.sem, scored.after(job))
                        dve.wait_ge(taken.sem, taken.after(job - 1))
                        dve.tensor_tensor(masked[:], scores[:, own:own + P], ahead[:], ALU.add).then_inc(masked_done.sem, 1)
                        dve.wait_ge(masked_done.sem, masked_done.after(job))
                        if t:
                            dve.tensor_reduce(found[:, 1, h, t:t + 1], scores[:, 0:own], AX.X, ALU.max)
                        dve.tensor_reduce(found[:, 0, h, t:t + 1], masked[:], AX.X, ALU.max).then_inc(taken.sem, 1)
                    dve.wait_ge(taken.sem, taken.after(j * len(jobs) + len(jobs) - 1))
                    dve.wait_ge(flipped.sem, flipped.after(j - 1))
                    dve.tensor_tensor(least[:], found[:, 0].rearrange("p h t -> p (h t)"), found[:, 1].rearrange("p h t -> p (h t)"), ALU.max)\
                       .then_inc(joined.sem, 1)
                    dve.wait_ge(joined.sem, joined.after(j - 1) + 1)
                    dve.tensor_scalar(least[:], least[:], -1.0, None, ALU.mult).then_inc(joined.sem, 1)
                    dve.wait_ge(flipped.sem, flipped.after(j))
                    dve.wait_ge(stored.sem, stored.after(j - 1))
                    dve.tensor_copy(parts[:, 0], turned[:]).then_inc(split.sem, 1)
                    dve.wait_ge(split.sem, split.after(j - 1) + 1)
                    dve.tensor_tensor(rest[:], turned[:], parts[:, 0], ALU.subtract).then_inc(split.sem, 1)
                    dve.wait_ge(split.sem, split.after(j - 1) + 2)
                    dve.tensor_copy(parts[:, 1], rest[:]).then_inc(split.sem, 1)
            with dve.Else():
                pass


def attend(nc, s):
    PAIRS = BATCH * KV
    chunks = [(t, c) for t in reversed(range(BLOCKS_B)) for c in range(BT * t + BT)]
    PER_PAIR = len(chunks)
    BODY = 2 * PER_PAIR
    UNITS = 2 * BODY
    diagonal = {}
    for n in range(BODY):
        t, c = chunks[n % PER_PAIR]
        if c >= BT * t:
            diagonal[n] = len(diagonal)
    DIAGONALS = len(diagonal)
    with ExitStack() as ctx:
        def sb(name, shape, dt=fp32):
            return ctx.enter_context(nc.sbuf_tensor(name, shape, dt))

        def steps(name, per=1, lead=2):
            return Steps(ctx.enter_context(nc.semaphore(name)), per, lead)

        q_stack = sb("q_stack", [P, 2, GROUP, SEQ], bf16)
        values = sb("values", [P, 2, TILES_B, 2 * HD])
        probs = sb("probs", [P, 4, 2, BLOCK])
        den = sb("den", [P, 2, BLOCK])
        o_n = sb("o_n", [P, 2, BLOCK])
        scores = ctx.enter_context(nc.psum_tensor("scores", [P, 3, 2, BLOCK], fp32))
        sums = ctx.enter_context(nc.psum_tensor("sums", [P, 2, BLOCK], fp32))

        loaded = [steps(f"pair_loaded_{u}", 16 * (2 * SLOTS + 2)) for u in range(2)]
        scored, exped = steps("scored"), steps("exped", lead=4)
        masked, summed = steps("masked"), steps("summed", lead=BODY)
        divided = steps("divided", 3)
        a_out = [steps(f"a_out_{u}", 16 * GROUP) for u in range(2)]
        block = ctx.enter_context(nc.Block())

        def body():
            for u in range(2):
                for k, (t, c) in enumerate(chunks):
                    yield u * PER_PAIR + k, u, t, c, P * max(0, c - BT * t)

        @block.sync
        def _(sp):
            for made in (*loaded, *a_out):
                made.open(sp)

            def store(i, u):
                for t in reversed(range(BLOCKS_B)):
                    sp.wait_ge(divided.sem, divided.after(i * 2 * BLOCKS_B + u * BLOCKS_B + (BLOCKS_B - 1 - t)))
                    apart(sp, s)
                    for h in range(GROUP):
                        sp.dma_start(s.a_rows[bass.ds(i * 2 + u, 1), h, :, BLOCK * t:BLOCK * t + BLOCK].rearrange("a p n -> p (a n)"),
                                     o_n[2 * HD * h:2 * HD * h + HD, t % 2]).then_inc(a_out[t % 2].sem, 16)

            def load(i, u):
                j = i * 2 + u
                sp.wait_ge(summed.sem, summed.after(i * BODY + (u - 1) * PER_PAIR - 1))
                for n in range(SLOTS):
                    rows = slice(HD * n, HD * n + HD)
                    sp.dma_start(s.k_stack[rows, u, :], s.k_rows[K_PART[n], bass.ds(j, 1)].rearrange("a p n -> p (a n)"))\
                      .then_inc(loaded[u].sem, 16)
                    sp.dma_start(q_stack[rows, u], s.q_rows[Q_PART[n], bass.ds(j * GROUP, GROUP)].rearrange("h p n -> p h n"))\
                      .then_inc(loaded[u].sem, 16)
                sp.dma_start(q_stack[STACK:ROWS, u], s.d_shift[:, bass.ds(j * GROUP, GROUP), :]).then_inc(loaded[u].sem, 16)
                sp.dma_start(values[:, u], s.v_all[:, bass.ds(j, 1)].rearrange("p a t d -> p (a t) d"))\
                  .then_inc(loaded[u].sem, 16)

            load(0, 0)
            with sp.Fori(0, PAIRS // 2 - 1) as i:
                load(i, 1)
                store(i, 0)
                load(i + 1, 0)
                store(i, 1)
            load(PAIRS // 2 - 1, 1)
            store(PAIRS // 2 - 1, 0)
            store(PAIRS // 2 - 1, 1)
            for u in range(2):
                sp.wait_ge(a_out[u].sem, a_out[u].after(PAIRS * BLOCKS_B // 2 - 1))

        @block.tensor
        def _(pe):
            summed.open(pe)
            scored.open(pe)

            def score(i, n, u, t, c, n0):
                if n % PER_PAIR == 0:
                    pe.wait_ge(loaded[u].sem, loaded[u].after(i))
                for half in range(2):
                    e = 2 * n + half
                    before = e - 3 if e >= 3 else max(x for x in range(UNITS - 3, UNITS) if x % 3 == e) - UNITS
                    pe.wait_ge(exped.sem, exped.after(i * UNITS + before))
                    for h in range(2):
                        last = nc.tensor.matmul(scores[:, e % 3, h, n0:], s.k_stack[0:ROWS, u, P * c:P * c + P],
                                                q_stack[0:ROWS, u, 2 * half + h, BLOCK * t + n0:BLOCK * t + BLOCK],
                                                start=True, stop=True)
                    last.then_inc(scored.sem, 1)

            def weigh(i, n, u, t, c, n0):
                pe.wait_ge(exped.sem, exped.after(i * UNITS + 2 * n + 1))
                if c >= BT * t:
                    pe.wait_ge(masked.sem, masked.after(i * DIAGONALS + diagonal[n]))
                if c == 0:
                    pe.wait_ge(divided.sem, divided.after(i * 2 * BLOCKS_B + u * BLOCKS_B + (BLOCKS_B - 1 - t) - 2))
                for h in range(GROUP):
                    last = nc.tensor.matmul(sums[2 * HD * h:2 * HD * h + 2 * HD, t % 2, n0:], values[:, u, c, :],
                                            probs[:, (2 * n + h // 2) % 4, h % 2, n0:],
                                            start=(c == 0), stop=(c == BT * t + BT - 1), tile_position=(0, 2 * HD * h))
                last.then_inc(summed.sem, 1)

            with pe.Fori(0, PAIRS // 2) as i:
                before = None
                for chunk in body():
                    score(i, *chunk)
                    if before:
                        weigh(i, *before)
                    before = chunk
                weigh(i, *before)

        @block.scalar
        def _(act):
            exped.open(act)
            with act.Fori(0, PAIRS // 2) as i:
                for n, u, t, c, n0 in body():
                    act.wait_ge(summed.sem, summed.after(i * BODY + n - 2))
                    for e in (2 * n, 2 * n + 1):
                        act.wait_ge(scored.sem, scored.after(i * UNITS + e))
                        act.activation(probs[:, e % 4, :, n0:], scores[:, e % 3, :, n0:], ACT.Exp, scale=A_SCALE)\
                           .then_inc(exped.sem, 1)

        @block.gpsimd
        def _(pool):
            masked.open(pool)
            with pool.Fori(0, PAIRS // 2) as i:
                for n, u, t, c, n0 in body():
                    if c < BT * t:
                        continue
                    for e in (2 * n, 2 * n + 1):
                        pool.wait_ge(exped.sem, exped.after(i * UNITS + e))
                        own = probs[:, e % 4, :, n0:n0 + P]
                        apart(pool, s)
                        last = pool.affine_select(out=own, in_=own, compare_op=ALU.is_ge, fill=0.0, base=0,
                                                  pattern=[[0, 2], [1, P]], channel_multiplier=-1)
                    last.then_inc(masked.sem, 1)

        @block.vector
        def _(dve):
            divided.open(dve)
            spread = [HD + r % HD for r in range(2 * HD)]
            with dve.Fori(0, PAIRS // 2) as i:
                for n, u, t, c, n0 in body():
                    if c < BT * t + BT - 1:
                        continue
                    tile = i * 2 * BLOCKS_B + u * BLOCKS_B + (BLOCKS_B - 1 - t)
                    dve.wait_ge(summed.sem, summed.after(i * BODY + n))
                    apart(dve, s)
                    dve.stream_shuffle(den[:, 0], sums[:, t % 2], spread).then_inc(divided.sem, 1)
                    dve.wait_ge(divided.sem, divided.after(tile - 1) + 1)
                    dve.reciprocal(den[:, 1], den[:, 0]).then_inc(divided.sem, 1)
                    dve.wait_ge(divided.sem, divided.after(tile - 1) + 2)
                    dve.wait_ge(a_out[t % 2].sem, a_out[t % 2].after(i * BLOCKS_B + (u * BLOCKS_B + BLOCKS_B - 1 - t) // 2 - 1))
                    dve.tensor_tensor(o_n[:, t % 2], sums[:, t % 2], den[:, 1], ALU.mult).then_inc(divided.sem, 1)



def transpose_weights(nc, s):
    jobs = [(source, target, source.shape[0] // P, source.shape[1] // P) for source, target in (
        (s.d_wqkv, s.w_qkv_t), (s.d_wq_h, s.wq_h_t), (s.d_wkv_h, s.wkv_h_t),
        (s.d_wout_l, s.wout_l_t), (s.d_wout_h, s.wout_h_t))]
    rows = sum(n for _, _, n, _ in jobs)
    with nc.sbuf_tensor("w_rows", [P, rows, 4 * P], fp32) as w_rows, \
            nc.psum_tensor("w_turned", [P, 2, 4, P], fp32) as w_turned, \
            nc.semaphore("w_loaded") as loaded, nc.semaphore("w_turned_done") as turned, \
            nc.semaphore("w_copied") as copied, nc.Block() as block:
        turns, at = [], 0
        for source, target, n, m in jobs:
            for r in range(n):
                turns.append((at, target, r, m))
                at += 1

        @block.sync
        def _(sp):
            at = 0
            for source, _, n, m in jobs:
                sp.dma_start(w_rows[:, at:at + n, 0:m * P], source.rearrange("(r p) n -> p r n", p=P)).then_inc(loaded, 16)
                at += n

        @block.tensor
        def _(pe):
            pe.wait_ge(loaded, 16 * len(jobs))
            for k, (at, _, r, m) in enumerate(turns):
                if k >= 2:
                    pe.wait_ge(copied, k - 1)
                for c in range(m):
                    last = nc.tensor.transpose(w_turned[:, k % 2, c], w_rows[:, at, P * c:P * c + P], s.ident[:])
                last.then_inc(turned, 1)

        @block.vector
        def _(dve):
            for k, (_, target, r, m) in enumerate(turns):
                dve.wait_ge(turned, k + 1)
                if target is s.wkv_h_t:
                    dve.tensor_copy(target[:, :, :, r], w_turned[:, k % 2, 0:m].rearrange("p c (a d) -> p c a d", a=2)).then_inc(copied, 1)
                else:
                    dve.tensor_copy(target[:, :, P * r:P * r + P], w_turned[:, k % 2, 0:m]).then_inc(copied, 1)


def normalise_tiles(dve, out, mean_var, inv, x):
    for t in range(BT):
        last = dve.tensor_scalar(out[:, t], x[:, t], mean_var[:, t, 0:1], inv[:, t:t + 1], ALU.subtract, ALU.mult)
    return last


def merge(nc, s):
    with ExitStack() as ctx:
        def sb(name, shape, dt=fp32):
            return ctx.enter_context(nc.sbuf_tensor(name, shape, dt))

        def steps(name, per=1, lead=2):
            return Steps(ctx.enter_context(nc.semaphore(name)), per, lead)

        a_t = sb("a_t", [P, 2, HALVES, BLOCK])
        x_in = sb("x_in2", [P, 2, BT, DIM])
        y = sb("y", [P, BT, DIM])
        x_1 = sb("x_1", [P, 2, BT, DIM])
        h_n = sb("h_n", [P, 2, BT, DIM])
        u_n = sb("u_n", [P, BT, DIM])
        u_t = sb("u_turned", [P, 2, HALVES, BLOCK])
        stats = sb("stats2", [P, BT, 6])
        mean_var = sb("mean_var2", [P, BT, 2])
        inv = sb("inv2", [P, BT])
        scratch, block_s = sb("route_product", [P, BT, 2, DIM]), sb("block_s", [P, 2, BT])
        w_o, b_o = sb("w_o", [P, HALVES, DIM]), sb("b_o", [P, DIM])
        ln_w, ln_b = sb("ln_w", [P, HALVES]), sb("ln_b", [P, HALVES])
        rt = sb("rt", [P, 2, DIM])
        p_y = ctx.enter_context(nc.psum_tensor("p_y", [P, BT, DIM], fp32))
        p_u = ctx.enter_context(nc.psum_tensor("p_u", [P, HALVES, BLOCK], fp32))

        w_loaded = ctx.enter_context(nc.semaphore("merge_weights"))
        loaded = [steps(f"block_loaded_{u}", 32) for u in range(2)]
        x1_out = [steps(f"x1_out_{u}", 32) for u in range(2)]
        u_out = [steps(f"u_out_{u}", 16) for u in range(2)]
        DVE_STEPS = 11
        made, multiplied = steps("made", DVE_STEPS), steps("multiplied")
        inverted = steps("inverted2", 6)
        projected, turned, u_ready = steps("o_projected"), steps("u_turned_done"), steps("u_ready")
        routed = steps("routed")
        block = ctx.enter_context(nc.Block())

        @block.sync
        def _(sp):
            for m in (*loaded, *x1_out, *u_out):
                m.open(sp)
            sp.dma_start(w_o[:], s.d_w_o.rearrange("(k p) n -> p k n", p=P)).then_inc(w_loaded, 16)
            sp.dma_start(b_o[:], s.d_b_o.rearrange("(a n) -> a n", a=1).broadcast_to([P, DIM])).then_inc(w_loaded, 16)
            sp.dma_start(rt[:, 0], s.d_rt_q.broadcast_to([P, DIM])).then_inc(w_loaded, 16)
            sp.dma_start(rt[:, 1], s.d_rt_kv.broadcast_to([P, DIM])).then_inc(w_loaded, 16)
            sp.dma_start(ln_w[:], s.d_ln_w.rearrange("(k p) -> p k", p=P), allow_slow_non_contiguous=True).then_inc(w_loaded, 16)
            sp.dma_start(ln_b[:], s.d_ln_b.rearrange("(k p) -> p k", p=P), allow_slow_non_contiguous=True).then_inc(w_loaded, 16)

            def store(g, v, b, c):
                u = c % 2
                tiles = bass.ds(b * TILES_B + BT * c, BT)
                sp.wait_ge(made.sem, made.after(g - 1) + 8)
                sp.dma_start(s.d_x1[tiles].rearrange("t p d -> p t d"), x_1[:, u]).then_inc(x1_out[u].sem, 16)
                sp.dma_start(s.d_h[tiles].rearrange("t p d -> p t d"), h_n[:, u]).then_inc(x1_out[u].sem, 16)
                sp.wait_ge(u_ready.sem, u_ready.after(g))
                sp.dma_start(s.d_u_t[:, :, bass.ds(b * SEQ + BLOCK * c, BLOCK)], u_t[:, u]).then_inc(u_out[u].sem, 16)

            with sp.Fori(0, BATCH) as b:
                for c in range(BLOCKS_B):
                    g, u = b * BLOCKS_B + c, c % 2
                    sp.wait_ge(made.sem, made.after(g - 2))
                    sp.dma_start(a_t[:, u], s.d_attended[bass.ds(b * HALVES, HALVES), :, BLOCK * c:BLOCK * c + BLOCK]
                                 .rearrange("k p n -> p k n")).then_inc(loaded[u].sem, 16)
                    sp.dma_start(x_in[:, u], s.d_x[bass.ds(b * TILES_B + BT * c, BT)].rearrange("t p d -> p t d"))\
                      .then_inc(loaded[u].sem, 16)
                    if c > 0:
                        store(g - 1, 0, b, c - 1)
                store(b * BLOCKS_B + BLOCKS_B - 1, 0, b, BLOCKS_B - 1)
            for u in range(2):
                sp.wait_ge(x1_out[u].sem, x1_out[u].after(BATCH * BLOCKS_B // 2 - 1))
                sp.wait_ge(u_out[u].sem, u_out[u].after(BATCH * BLOCKS_B // 2 - 1))

        @block.tensor
        def _(pe):
            projected.open(pe)
            turned.open(pe)
            pe.wait_ge(w_loaded, 6 * 16)
            with pe.Fori(0, BATCH) as b:
                for c in range(BLOCKS_B):
                    g, u, v = b * BLOCKS_B + c, c % 2, b * (BLOCKS_B // 2) + c // 2
                    pe.wait_ge(loaded[u].sem, loaded[u].after(v))
                    pe.wait_ge(made.sem, made.after(g - 2) + 1)
                    for t in range(BT):
                        for k in range(HALVES):
                            last = nc.tensor.matmul(p_y[:, t], a_t[:, u, k, P * t:P * t + P], w_o[:, k],
                                                    start=(k == 0), stop=(k == HALVES - 1))
                    last.then_inc(projected.sem, 1)
                    pe.wait_ge(made.sem, made.after(g))
                    pe.wait_ge(u_ready.sem, u_ready.after(g - 1))
                    for t in range(BT):
                        for k in range(HALVES):
                            last = nc.tensor.transpose(p_u[:, k, P * t:P * t + P], u_n[:, t, P * k:P * k + P], s.ident[:])
                    last.then_inc(turned.sem, 1)

        @block.scalar
        def _(act):
            u_ready.open(act)
            with act.Fori(0, BATCH) as b:
                for c in range(BLOCKS_B):
                    g, u, v = b * BLOCKS_B + c, c % 2, b * (BLOCKS_B // 2) + c // 2
                    act.wait_ge(turned.sem, turned.after(g))
                    act.wait_ge(u_out[u].sem, u_out[u].after(v - 1))
                    for k in range(HALVES):
                        last = act.activation(u_t[:, u, k], p_u[:, k], ACT.Identity, scale=ln_w[:, k:k + 1], bias=ln_b[:, k:k + 1])
                    last.then_inc(u_ready.sem, 1)

        @block.gpsimd
        def _(pool):
            inverted.open(pool)
            with pool.Fori(0, BATCH) as b:
                for c in range(BLOCKS_B):
                    g = b * BLOCKS_B + c
                    for n, ready in enumerate((3, 7, 10)):
                        pool.wait_ge(made.sem, made.after(g - 1) + ready)
                        apart(pool, s)
                        pool.tensor_scalar(inv[:], mean_var[:, :, 1], EPS, None, ALU.add).then_inc(inverted.sem, 1)
                        pool.wait_ge(inverted.sem, inverted.after(g - 1) + 2 * n + 1)
                        pool.tensor_tensor(inv[:], inv[:], s.power[:, 0:BT], ALU.pow).then_inc(inverted.sem, 1)

        @block.vector
        def _(dve):
            for one in (made, multiplied, routed):
                one.open(dve)
            dve.wait_ge(w_loaded, 6 * 16)
            with dve.Fori(0, BATCH) as b:
                for c in range(BLOCKS_B):
                    g, u, v = b * BLOCKS_B + c, c % 2, b * (BLOCKS_B // 2) + c // 2
                    done = [0]

                    def step(instruction):
                        instruction.then_inc(made.sem, 1)
                        done[0] += 1
                        dve.wait_ge(made.sem, made.after(g - 1) + done[0])

                    def statistics(x, n):
                        for t in range(BT):
                            last = dve.bn_stats(stats[:, t], x[:, t])
                        step(last)
                        apart(dve, s)
                        for t in range(BT):
                            last = dve.bn_aggr(mean_var[:, t], stats[:, t])
                        step(last)
                        dve.wait_ge(inverted.sem, inverted.after(g - 1) + 2 * n + 2)

                    dve.wait_ge(projected.sem, projected.after(g))
                    step(dve.tensor_tensor(y[:], p_y[:], b_o[:].rearrange("p (a n) -> p a n", a=1).broadcast_to([P, BT, DIM]), ALU.add))
                    statistics(y, 0)
                    step(normalise_tiles(dve, y, mean_var, inv, y))
                    dve.wait_ge(x1_out[u].sem, x1_out[u].after(v - 1))
                    dve.wait_ge(loaded[u].sem, loaded[u].after(v))
                    step(dve.tensor_tensor(x_1[:, u], x_in[:, u], y[:], ALU.add))
                    statistics(x_1[:, u], 1)
                    step(normalise_tiles(dve, h_n[:, u], mean_var, inv, x_1[:, u]))
                    statistics(h_n[:, u], 2)
                    dve.wait_ge(turned.sem, turned.after(g - 1))
                    step(normalise_tiles(dve, u_n, mean_var, inv, h_n[:, u]))
                    dve.wait_ge(routed.sem, routed.after(g - 1))
                    for t in range(BT):
                        for r in range(2):
                            last = dve.tensor_tensor_reduce(out=scratch[:, t, r], in0=h_n[:, u, t], in1=rt[:, r], scale=1.0, scalar=0.0,
                                                            op0=ALU.mult, op1=ALU.add,
                                                            accum_out=block_s[:, r, t:t + 1])
                    last.then_inc(multiplied.sem, 1)
                    dve.wait_ge(multiplied.sem, multiplied.after(g))
                    dve.tensor_copy(s.route_s[:, :, bass.ds(g * BT, BT)], block_s[:]).then_inc(routed.sem, 1)
            dve.wait_ge(routed.sem, routed.after(BATCH * BLOCKS_B - 1))


WINDOW, L_HEADS, L_HD = 64, 8, 64
L_INNER = L_HEADS * L_HD
L_SCALE = L_HD ** -0.5
PAIR_CHUNKS = L_INNER // P
HALF_HEADS = L_HEADS // 2
OUTSIDE = -1e30


def local(nc, s):
    with ExitStack() as ctx:
        def sb(name, shape, dt=fp32):
            return ctx.enter_context(nc.sbuf_tensor(name, shape, dt))

        def ps(name, shape):
            return ctx.enter_context(nc.psum_tensor(name, shape, fp32))

        def steps(name, per=1, lead=4):
            return Steps(ctx.enter_context(nc.semaphore(name)), per, lead)

        SLOTS4 = 4
        EVEN, ODD = slice(0, WINDOW), slice(WINDOW, P)
        u_in = sb("u_in", [P, SLOTS4, HALVES, P])
        x1_in = sb("x1_in", [P, SLOTS4, DIM])
        q_pad = sb("q_pad", [P, SLOTS4, L_HEADS, P])
        k_window = sb("k_window", [P, SLOTS4, PAIR_CHUNKS, 2 * P])
        v_main = sb("v_main", [P, SLOTS4, L_HEADS, L_HD + 1])
        v_side = sb("v_side", [P, SLOTS4, L_HEADS, L_HD + 1])
        edge = sb("edge", [P, TILES])
        m_main, m_side = sb("m_main", [P, HALF_HEADS]), sb("m_side", [P, HALF_HEADS])
        m_all, m_edge = sb("m_all", [P, HALF_HEADS]), sb("m_edge", [P, HALF_HEADS])
        z = sb("z", [P, 2, HALF_HEADS, 2 * P])
        probs = sb("l_probs", [P, 2, HALF_HEADS, 2 * P])
        probs_t = sb("probs_t", [P, 2, HALF_HEADS, 2, P])
        den = sb("l_den", [P, HALF_HEADS])
        o_n = sb("l_o_n", [P, L_HEADS, L_HD])
        o_t = sb("o_t", [P, PAIR_CHUNKS, P])
        light = sb("light_rows", [P, 2, DIM])
        y = sb("l_y", [P, DIM])
        stats, mean_var, inv = sb("stats3", [P, 6]), sb("mean_var3", [P, 2]), sb("inv3", [P, 1])
        rows = sb("out_rows", [P, 2, DIM])
        null_q = sb("null_q", [P, DIM])
        p_q, p_k, p_v = ps("p_q3", [P, BLOCK]), ps("p_k3", [P, BLOCK]), ps("p_v3", [P, BLOCK])
        p_s = ps("p_s", [P, HALF_HEADS, 2 * P])
        p_p = ps("p_p", [P, HALF_HEADS, 2, P])
        p_o = ps("p_o", [P, BLOCK])
        sums = p_o[:, 0:HALF_HEADS * (L_HD + 1)].rearrange("p (h d) -> p h d", h=HALF_HEADS)
        p_ot, p_y = p_q, p_k[:, 0:DIM]

        filled = ctx.enter_context(nc.semaphore("l_filled"))
        null_loaded = ctx.enter_context(nc.semaphore("null_loaded"))
        u_loaded = [steps(f"u_loaded_{k}", 16, 1) for k in range(SLOTS4)]
        x1_loaded = [steps(f"x1_loaded_{k}", 16, 1) for k in range(SLOTS4)]
        light_out = [steps(f"light_out_{k}", 16, 1) for k in range(2)]
        out_out = [steps(f"out_out_{k}", 16, 1) for k in range(2)]
        qk_done, v_done = steps("qk_done"), steps("v_done")
        q_ready, k_main, k_sides = steps("q_ready"), steps("k_main"), steps("k_sides")
        v_ready, v_sides = steps("v_main_ready"), steps("v_sides_ready")
        scored, z_ready, exped = steps("l_scored"), steps("z_ready"), steps("l_exped")
        p_turned, p_ready, summed = steps("p_turned"), steps("p_ready"), steps("l_summed")
        o_ready, o_turned, o_t_ready = steps("o_ready"), steps("o_turned"), steps("o_t_ready")
        y_done, light_ready = steps("y_done"), steps("light_ready")
        G_STEPS, F_STEPS = 4, 4
        g_chain = steps("g_chain", G_STEPS)
        f_chain = steps("f_chain", F_STEPS)
        inverted, rows_ready = steps("inverted3", 2), steps("rows_ready")
        r_chain = steps("r_chain")
        FILLS = 8
        block = ctx.enter_context(nc.Block())
        LAST = TILES // SLOTS4 - 1

        def loop(eng, before, turn):
            before()
            with eng.Fori(0, LAST) as i:
                for k in range(SLOTS4):
                    turn(i, k, True)
            for k in range(SLOTS4):
                turn(LAST, k, k < 2)

        @block.sync
        def _(sp):
            for made in (*u_loaded, *x1_loaded, *light_out, *out_out):
                made.open(sp)
            sp.dma_start(null_q[:], s.d_null_q.rearrange("(a n) -> a n", a=1).broadcast_to([P, DIM])).then_inc(null_loaded, 16)

            def load(n, k):
                sp.wait_ge(v_done.sem, v_done.after(n - SLOTS4))
                sp.dma_start(u_in[:, k], s.d_u_t[:, :, bass.ds(n * P, P)]).then_inc(u_loaded[k].sem, 16)
                sp.wait_ge(rows_ready.sem, rows_ready.after(n - SLOTS4))
                sp.dma_start(x1_in[:, k], s.d_x1[bass.ds(n, 1)].rearrange("a p d -> p (a d)")).then_inc(x1_loaded[k].sem, 16)

            def turn(i, k, more):
                m = i * SLOTS4 + k
                if more:
                    load(m + 2, (k + 2) % SLOTS4)
                sp.wait_ge(light_ready.sem, light_ready.after(m))
                sp.dma_start(s.d_light[bass.ds(m, 1)].rearrange("a p d -> p (a d)"), light[:, k % 2]).then_inc(light_out[k % 2].sem, 16)
                sp.wait_ge(rows_ready.sem, rows_ready.after(m))
                sp.dma_start(s.d_out[bass.ds(m, 1)].rearrange("a p d -> p (a d)"), rows[:, k % 2]).then_inc(out_out[k % 2].sem, 16)

            def before():
                load(0, 0)
                load(1, 1)

            loop(sp, before, turn)
            for k in range(2):
                sp.wait_ge(light_out[k].sem, light_out[k].after(TILES // 2 - 1))
                sp.wait_ge(out_out[k].sem, out_out[k].after(TILES // 2 - 1))

        @block.tensor
        def _(pe):
            for made in (qk_done, v_done, scored, p_turned, summed, o_turned, y_done):
                made.open(pe)
            pe.wait_ge(filled, FILLS)

            def project_qk(i, k):
                n = i * SLOTS4 + k
                slot, turn = k % SLOTS4, i + k // SLOTS4
                pe.wait_ge(u_loaded[slot].sem, u_loaded[slot].after(turn))
                pe.wait_ge(o_t_ready.sem, o_t_ready.after(n - 3))
                pe.wait_ge(q_ready.sem, q_ready.after(n - 1))
                pe.wait_ge(light_ready.sem, light_ready.after(n - 3))
                pe.wait_ge(k_main.sem, k_main.after(n - 1))
                for out, first in ((p_q, 0), (p_k, L_INNER)):
                    for c in range(PAIR_CHUNKS):
                        for h in range(HALVES):
                            last = nc.tensor.matmul(out[:, P * c:P * c + P], s.w_qkv_t[:, h, first + P * c:first + P * c + P],
                                                    u_in[:, slot, h], start=(h == 0), stop=(h == HALVES - 1))
                last.then_inc(qk_done.sem, 1)

            def project_v(i, k):
                n = i * SLOTS4 + k
                pe.wait_ge(v_ready.sem, v_ready.after(n - 1))
                pe.wait_ge(v_sides.sem, v_sides.after(n - 1))
                for h in range(HALVES):
                    last = nc.tensor.matmul(p_v[:], u_in[:, k % SLOTS4, h], s.w_qkv_t[:, h, 2 * L_INNER:],
                                            start=(h == 0), stop=(h == HALVES - 1))
                last.then_inc(v_done.sem, 1)

            def score(e, k, g):
                pe.wait_ge(z_ready.sem, z_ready.after(e - 1))
                for j in range(HALF_HEADS):
                    h = g * HALF_HEADS + j
                    last = nc.tensor.matmul(p_s[:, j], q_pad[:, k, h], k_window[:, k, h // 2], start=True, stop=True)
                last.then_inc(scored.sem, 1)

            def turn_probs(e, g):
                pe.wait_ge(exped.sem, exped.after(e))
                pe.wait_ge(p_ready.sem, p_ready.after(e - 1))
                for j in range(HALF_HEADS):
                    for side in range(2):
                        last = nc.tensor.transpose(p_p[:, j, side], probs[:, g, j, P * side:P * side + P], s.ident[:])
                last.then_inc(p_turned.sem, 1)

            def weigh(e, k, g):
                pe.wait_ge(p_ready.sem, p_ready.after(e))
                pe.wait_ge(o_ready.sem, o_ready.after(e - 1))
                for j in range(HALF_HEADS):
                    h = g * HALF_HEADS + j
                    nc.tensor.matmul(sums[:, j], probs_t[:, g, j, 0], v_main[:, k, h], start=True, stop=False)
                    last = nc.tensor.matmul(sums[:, j], probs_t[:, g, j, 1], v_side[:, k, h], start=False, stop=True)
                last.then_inc(summed.sem, 1)

            def turn(i, k, more):
                m = i * SLOTS4 + k
                ahead = 1 if more or k < 3 else 0
                pe.wait_ge(q_ready.sem, q_ready.after(m))
                pe.wait_ge(k_sides.sem, k_sides.after(m + ahead))
                score(2 * m, k, 0)
                if more:
                    project_qk(i, k + 2)
                score(2 * m + 1, k, 1)
                turn_probs(2 * m, 0)
                if more:
                    project_v(i, k + 2)
                pe.wait_ge(v_sides.sem, v_sides.after(m + ahead))
                weigh(2 * m, k, 0)
                turn_probs(2 * m + 1, 1)
                weigh(2 * m + 1, k, 1)
                pe.wait_ge(o_ready.sem, o_ready.after(2 * m + 1))
                pe.wait_ge(q_ready.sem, q_ready.after(m + 2 if more else m + (1 if k == 2 else 0)))
                for c in range(PAIR_CHUNKS):
                    last = nc.tensor.transpose(p_ot[:, P * c:P * c + P], o_n[:, 2 * c:2 * c + 2].rearrange("p h d -> p (h d)"),
                                               s.ident[:])
                last.then_inc(o_turned.sem, 1)
                pe.wait_ge(o_t_ready.sem, o_t_ready.after(m))
                pe.wait_ge(k_main.sem, k_main.after(m + 2 if more else m + (1 if k == 2 else 0)))
                for c in range(PAIR_CHUNKS):
                    last = nc.tensor.matmul(p_y, o_t[:, c], s.wout_l_t[:, c], start=(c == 0), stop=(c == PAIR_CHUNKS - 1))
                last.then_inc(y_done.sem, 1)

            def before():
                for k in range(2):
                    project_qk(0, k)
                    project_v(0, k)

            loop(pe, before, turn)

        @block.scalar
        def _(act):
            for made in (q_ready, k_main, v_sides, exped, p_ready, o_t_ready, light_ready):
                made.open(act)
            act.wait_ge(filled, FILLS)

            def take_qk(i, k):
                n, slot = i * SLOTS4 + k, k % SLOTS4
                act.wait_ge(qk_done.sem, qk_done.after(n))
                q = p_q[:].rearrange("p (c n) -> p c n", c=PAIR_CHUNKS)
                pairs = q_pad[:, slot].rearrange("p (c a) n -> p c a n", a=2)
                act.activation(pairs[EVEN, :, 0], q[EVEN], ACT.Copy)
                act.activation(pairs[ODD, :, 1], q[ODD], ACT.Copy).then_inc(q_ready.sem, 1)
                act.activation(k_window[:, slot, :, 0:P], p_k[:].rearrange("p (c n) -> p c n", c=PAIR_CHUNKS), ACT.Copy)\
                   .then_inc(k_main.sem, 1)

            def take_v_sides(i, k):
                act.wait_ge(v_ready.sem, v_ready.after(i * SLOTS4 + k))
                v = p_v[:].rearrange("p (h d) -> p h d", h=L_HEADS)
                act.activation(v_side[EVEN, (k - 1) % SLOTS4, :, 0:L_HD], v[EVEN], ACT.Copy)
                act.activation(v_side[ODD, (k + 1) % SLOTS4, :, 0:L_HD], v[ODD], ACT.Copy).then_inc(v_sides.sem, 1)

            def exps(e, g):
                act.wait_ge(z_ready.sem, z_ready.after(e))
                act.wait_ge(p_turned.sem, p_turned.after(e - 2))
                act.activation(probs[:, g], z[:, g], ACT.Exp, scale=L_SCALE).then_inc(exped.sem, 1)

            def take_probs(e, g):
                act.wait_ge(p_turned.sem, p_turned.after(e))
                act.wait_ge(summed.sem, summed.after(e - 2))
                act.activation(probs_t[:, g], p_p[:], ACT.Copy).then_inc(p_ready.sem, 1)

            def turn(i, k, more):
                m = i * SLOTS4 + k
                exps(2 * m, 0)
                if more:
                    take_qk(i, k + 2)
                take_probs(2 * m, 0)
                exps(2 * m + 1, 1)
                if more:
                    take_v_sides(i, k + 2)
                take_probs(2 * m + 1, 1)
                act.wait_ge(o_turned.sem, o_turned.after(m))
                act.activation(o_t[:], p_ot[:].rearrange("p (c n) -> p c n", c=PAIR_CHUNKS), ACT.Copy).then_inc(o_t_ready.sem, 1)
                act.wait_ge(y_done.sem, y_done.after(m))
                act.wait_ge(light_out[k % 2].sem, light_out[k % 2].after(i * 2 + k // 2 - 1))
                act.wait_ge(f_chain.sem, f_chain.after(m - 2))
                act.activation(light[:, k % 2], p_y, ACT.Copy).then_inc(light_ready.sem, 1)

            def before():
                for k in range(2):
                    take_qk(0, k)
                    take_v_sides(0, k)

            loop(act, before, turn)

        @block.gpsimd
        def _(pool):
            for made in (k_sides, inverted, rows_ready):
                made.open(pool)
            pool.wait_ge(filled, FILLS)

            def sides(i, k):
                n, slot, prior, following = i * SLOTS4 + k, k % SLOTS4, (k - 1) % SLOTS4, (k + 1) % SLOTS4
                pool.wait_ge(k_main.sem, k_main.after(n))
                apart(pool, s)
                pool.tensor_copy(k_window[:, prior, :, P:P + WINDOW], k_window[:, slot, :, 0:WINDOW])
                pool.tensor_copy(k_window[:, following, :, P + WINDOW:], k_window[:, slot, :, WINDOW:P]).then_inc(k_sides.sem, 1)

            def turn(i, k, more):
                m = i * SLOTS4 + k
                if more:
                    sides(i, k + 2)
                pool.wait_ge(f_chain.sem, f_chain.after(m - 1) + 3)
                apart(pool, s)
                pool.tensor_scalar(inv[:], mean_var[:, 1:2], EPS, None, ALU.add).then_inc(inverted.sem, 1)
                pool.wait_ge(inverted.sem, inverted.after(m - 1) + 1)
                pool.tensor_tensor(inv[:], inv[:], s.power[:, 0:1], ALU.pow).then_inc(inverted.sem, 1)
                pool.wait_ge(f_chain.sem, f_chain.after(m))
                pool.wait_ge(x1_loaded[k].sem, x1_loaded[k].after(i))
                pool.wait_ge(out_out[k % 2].sem, out_out[k % 2].after(i * 2 + k // 2 - 1))
                pool.tensor_tensor(rows[:, k % 2], y[:], x1_in[:, k], ALU.add).then_inc(rows_ready.sem, 1)

            def before():
                sides(0, 0)
                sides(0, 1)

            loop(pool, before, turn)

        @block.vector
        def _(dve):
            for made in (v_ready, z_ready, o_ready, g_chain, f_chain):
                made.open(dve)
            fills = [(q_pad[:], 0.0), (k_window[:], 0.0), (v_side[:], 1.0), (v_main[:], 1.0), (z[:], OUTSIDE), (edge[:], 0.0)]
            for out, value in fills:
                dve.memset(out, value).then_inc(filled, 1)
            dve.wait_ge(filled, len(fills))
            by_batch = edge[:].rearrange("p (b t) -> p b t", b=BATCH)
            dve.memset(by_batch[EVEN, :, 0:1], OUTSIDE).then_inc(filled, 1)
            dve.memset(by_batch[ODD, :, TILES_B - 1:TILES_B], OUTSIDE).then_inc(filled, 1)
            dve.wait_ge(filled, FILLS)
            dve.wait_ge(null_loaded, 16)

            def take_v(i, k):
                n = i * SLOTS4 + k
                dve.wait_ge(v_done.sem, v_done.after(n))
                dve.tensor_copy(v_main[:, k % SLOTS4, :, 0:L_HD], p_v[:].rearrange("p (h d) -> p h d", h=L_HEADS)).then_inc(v_ready.sem, 1)

            def wide(x, rows, n):
                return x[rows].rearrange("p (h a) -> p h a", a=1).broadcast_to([rows.stop - rows.start, HALF_HEADS, n])

            def maxima(e, m, g):
                base = g_chain.after(e - 1)
                out_of = edge[:, bass.ds(m, 1)]
                dve.wait_ge(scored.sem, scored.after(e))
                dve.wait_ge(exped.sem, exped.after(e - 2))
                dve.wait_ge(z_ready.sem, z_ready.after(e - 1))
                dve.tensor_reduce(m_main[:], p_s[:, :, 0:P], AX.X, ALU.max)
                dve.tensor_reduce(m_side[EVEN], p_s[EVEN, :, P + WINDOW:], AX.X, ALU.max)
                dve.tensor_reduce(m_side[ODD], p_s[ODD, :, P:P + WINDOW], AX.X, ALU.max).then_inc(g_chain.sem, 1)
                dve.wait_ge(g_chain.sem, base + 1)
                dve.tensor_scalar(m_side[:], m_side[:], out_of, None, ALU.add).then_inc(g_chain.sem, 1)
                dve.wait_ge(g_chain.sem, base + 2)
                dve.tensor_tensor(m_all[:], m_side[:], m_main[:], ALU.max).then_inc(g_chain.sem, 1)
                dve.wait_ge(g_chain.sem, base + 3)
                dve.tensor_scalar(m_edge[:], m_all[:], out_of, None, ALU.subtract).then_inc(g_chain.sem, 1)
                dve.wait_ge(g_chain.sem, base + 4)
                dve.tensor_tensor(z[:, g, :, 0:P], p_s[:, :, 0:P], wide(m_all, slice(0, P), P), ALU.subtract)
                dve.tensor_tensor(z[EVEN, g, :, P + WINDOW:], p_s[EVEN, :, P + WINDOW:], wide(m_edge, EVEN, WINDOW), ALU.subtract)
                dve.tensor_tensor(z[ODD, g, :, P:P + WINDOW], p_s[ODD, :, P:P + WINDOW], wide(m_edge, ODD, WINDOW), ALU.subtract)\
                   .then_inc(z_ready.sem, 1)

            def finish(m, k):
                base = f_chain.after(m - 1)
                dve.wait_ge(light_ready.sem, light_ready.after(m))
                dve.wait_ge(rows_ready.sem, rows_ready.after(m - 1))
                dve.tensor_tensor(y[:], light[:, k % 2], null_q[:], ALU.add).then_inc(f_chain.sem, 1)
                dve.wait_ge(f_chain.sem, base + 1)
                dve.bn_stats(stats[:], y[:]).then_inc(f_chain.sem, 1)
                dve.wait_ge(f_chain.sem, base + 2)
                apart(dve, s)
                dve.bn_aggr(mean_var[:], stats[:]).then_inc(f_chain.sem, 1)
                dve.wait_ge(inverted.sem, inverted.after(m))
                dve.tensor_scalar(y[:], y[:], mean_var[:, 0:1], inv[:, 0:1], ALU.subtract, ALU.mult).then_inc(f_chain.sem, 1)

            def turn(i, k, more):
                m = i * SLOTS4 + k
                maxima(2 * m, m, 0)
                maxima(2 * m + 1, m, 1)
                if more:
                    take_v(i, k + 2)
                divide(m, 0)
                divide(m, 1)
                finish(m, k)

            def divide(m, g):
                e = 2 * m + g
                dve.wait_ge(summed.sem, summed.after(e))
                dve.wait_ge(o_turned.sem, o_turned.after(m - 1))
                dve.wait_ge(o_ready.sem, o_ready.after(e - 1))
                dve.reciprocal(den[:], sums[:, :, L_HD]).then_inc(r_chain.sem, 1)
                dve.wait_ge(r_chain.sem, r_chain.after(e))
                dve.tensor_tensor(o_n[:, g * HALF_HEADS:(g + 1) * HALF_HEADS], sums[:, :, 0:L_HD], wide(den, slice(0, P), L_HD), ALU.mult)\
                   .then_inc(o_ready.sem, 1)

            def before():
                r_chain.open(dve)
                take_v(0, 0)
                take_v(0, 1)

            loop(dve, before, turn)




N_Q, N_KV = 128, 256
ITERATIONS = 50
FETCH = 9.0 / 8.0
ROUTES = 2 * BATCH
DRAWN = (N_Q,) * BATCH + (N_KV,) * BATCH
LOWEST = 104.0
FLOAT_BITS = 31
ROW_TILES = 3


def route(nc, s):
    with ExitStack() as ctx:
        def sb(name, shape, dt=fp32):
            return ctx.enter_context(nc.sbuf_tensor(name, shape, dt))

        def ps(name, shape):
            return ctx.enter_context(nc.psum_tensor(name, shape, fp32))

        def steps(name, per=1, lead=2):
            return Steps(ctx.enter_context(nc.semaphore(name)), per, lead)

        T = TILES_B
        s17 = sb("s17", [P, ROUTES, T + 1])
        top = sb("top", [P, ROUTES])
        top8, top_diag = sb("top8", [ROUTES, 1]), sb("top_diag", [ROUTES, ROUTES])
        ones, tri, reset = sb("ones", [P, P]), sb("tri", [P, P], bf16), sb("reset", [P, ROUTES, T])
        ones_b = sb("ones_b", [P, P], bf16)
        log_k, k_of = sb("log_k", [P, ROUTES]), sb("k_of", [P, ROUTES])
        a, c = sb("route_a", [P, ROUTES]), sb("route_c", [P, ROUTES])
        t17, nz17, w17 = sb("t17", [P, ROUTES, T + 1]), sb("nz17", [P, ROUTES, T + 1]), sb("w17", [P, ROUTES, T + 1])
        e, part, log_sum = sb("route_e", [P, ROUTES, T]), sb("route_part", [P, ROUTES]), sb("log_sum", [P, ROUTES])
        x, x_clamped, sc = sb("route_x", [P, ROUTES, T]), sb("x_clamped", [P, ROUTES, T]), sb("route_sc", [P, ROUTES, T])
        bit_f, bit_i = sb("bit_f", [P, 1]), sb("bit_i", [P, 1], i32)
        limit, trial, kept = sb("limit", [P, ROUTES], i32), sb("trial", [P, ROUTES], i32), sb("kept", [P, ROUTES], i32)
        below, tie = sb("below", [P, ROUTES, T]), sb("tie", [P, ROUTES, T], bf16)
        count, few = sb("count", [P, ROUTES]), sb("few", [P, ROUTES])
        scan, order = sb("scan", [P, ROUTES, T]), sb("order", [P, ROUTES, T])
        chosen, chosen_b, place = sb("chosen", [P, ROUTES, T]), sb("chosen_b", [P, ROUTES, T], bf16), sb("place", [P, ROUTES, T])
        number_i, number = sb("number_i", [P, 2, ROUTES, T], i32), sb("number", [P, ROUTES, T, 3], bf16)
        slot_i, slot = sb("slot_i", [P, N_KV], i32), sb("slot", [P, N_KV])
        one_hot = sb("one_hot", [P, 2, T, N_KV], bf16)
        token = sb("token", [P, BATCH, ROW_TILES])
        p_sum, p_tri, p_all = ps("p_sum", [P, 512]), ps("p_tri", [P, 512]), ps("p_all", [P, 512])
        p_number = ps("p_number", [P, BATCH, ROW_TILES, 3])

        d = steps("route_step", lead=2)
        exped, summed, logged = steps("r_exped"), steps("r_summed"), steps("r_logged")
        constants_made = ctx.enter_context(nc.semaphore("r_constants"))
        hot, gathered = steps("hot"), steps("hot_used")
        block = ctx.enter_context(nc.Block())

        def wide(v, n):
            return v.rearrange("p (r a) -> p r a", a=1).broadcast_to([P, ROUTES, n])

        TURN = 6
        BIT_TURN = 8
        START = 5
        SEARCH = START + TURN * (ITERATIONS - 1)
        PREPARE = 4
        SELECT = SEARCH + PREPARE + BIT_TURN * FLOAT_BITS
        SUM_BITS = 2 + ITERATIONS - 1
        SUM_LAST = SUM_BITS + FLOAT_BITS
        numbered = [(b, r, problem) for b in range(BATCH) for r, problem in ((0, BATCH + b), (2, b))]

        @block.gpsimd
        def _(pool):
            pool.memset(ones[:], 1.0).then_inc(constants_made, 1)
            pool.memset(ones_b[:], 1.0).then_inc(constants_made, 1)
            pool.memset(tri[:], 1.0).then_inc(constants_made, 1)
            pool.memset(reset[:], 1.0).then_inc(constants_made, 1)
            pool.iota(number_i[:, 0], pattern=[[0, 2], [T, BATCH], [1, T]], base=0, channel_multiplier=0).then_inc(constants_made, 1)
            pool.iota(number_i[:, 1], pattern=[[0, ROUTES], [0, T]], base=0, channel_multiplier=1).then_inc(constants_made, 1)
            pool.iota(slot_i[:], pattern=[[1, N_KV]], base=0, channel_multiplier=0).then_inc(constants_made, 1)
            pool.wait_ge(constants_made, 7)
            pool.affine_select(out=tri[:], in_=tri[:], compare_op=ALU.is_gt, fill=0.0, base=0, pattern=[[1, P]],
                               channel_multiplier=-1).then_inc(constants_made, 1)
            pool.memset(reset[:, :, 0:1], 0.0).then_inc(constants_made, 1)
            pool.tensor_copy(number[:, :, :, 0], number_i[:, 0]).then_inc(constants_made, 1)
            pool.tensor_copy(number[:, :, :, 1], number_i[:, 1]).then_inc(constants_made, 1)
            pool.tensor_copy(slot[:], slot_i[:]).then_inc(constants_made, 1)

        @block.tensor
        def _(pe):
            summed.open(pe)
            gathered.open(pe)
            pe.wait_ge(constants_made, 12)
            pe.wait_ge(d.sem, d.after(1))
            nc.tensor.transpose(p_sum[0:ROUTES, 0:P], top[:], s.ident[:]).then_inc(summed.sem, 1)
            pe.wait_ge(d.sem, d.after(3))
            nc.tensor.matmul(p_sum[:, 0:ROUTES], ones[0:ROUTES, :], top_diag[:], start=True, stop=True).then_inc(summed.sem, 1)

            def total(step):
                pe.wait_ge(d.sem, d.after(step))
                nc.tensor.matmul(p_sum[:, 0:ROUTES], ones[:], part[:], start=True, stop=True).then_inc(summed.sem, 1)

            with pe.Fori(0, ITERATIONS - 1) as i:
                total(START + i * TURN + 4)
            with pe.Fori(0, FLOAT_BITS) as i:
                total(SEARCH + PREPARE + i * BIT_TURN + 3)
            total(SELECT + 1)
            for n, (step, what) in enumerate(((SELECT + 3, tie), (SELECT + 12, chosen_b))):
                pe.wait_ge(d.sem, d.after(step))
                flat = what[:].rearrange("p r t -> p (r t)")
                nc.tensor.matmul(p_tri[:, 0:ROUTES * T], tri[:], flat, start=True, stop=True)
                nc.tensor.matmul(p_all[:, 0:ROUTES * T], ones_b[:], flat, start=True, stop=True).then_inc(summed.sem, 1)
            for n, (b, r, problem) in enumerate(numbered):
                pe.wait_ge(hot.sem, hot.after(n))
                for j in range(DRAWN[problem] // P):
                    for t in range(T):
                        last = nc.tensor.matmul(p_number[:, b, r + j], one_hot[:, n % 2, t, P * j:P * j + P],
                                                number[:, problem, t], start=(t == 0), stop=(t == T - 1))
                last.then_inc(gathered.sem, 1)

        @block.scalar
        def _(act):
            exped.open(act)
            logged.open(act)
            with act.Fori(0, ITERATIONS - 1) as i:
                act.wait_ge(d.sem, d.after(START + i * TURN + 2))
                act.activation(e[:], w17[:, :, 0:T], ACT.Exp, scale=-1.0).then_inc(exped.sem, 1)
                act.wait_ge(summed.sem, summed.after(2 + i))
                act.activation(log_sum[:], p_sum[:, 0:ROUTES], ACT.Ln).then_inc(logged.sem, 1)
            act.wait_ge(d.sem, d.after(SEARCH + 1))
            act.activation(sc[:], x[:], ACT.Exp, scale=-1.0).then_inc(exped.sem, 1)

        @block.vector
        def _(dve):
            d.open(dve)
            hot.open(dve)

            def step(instruction, at):
                instruction.then_inc(d.sem, 1)
                dve.wait_ge(d.sem, d.after(at))

            scores = s17[:, :, 0:T]
            step(dve.tensor_copy(scores, s.route_s[:].rearrange("p r (b t) -> p (r b) t", b=BATCH)), 0)
            step(dve.tensor_reduce(top[:], scores, AX.X, ALU.max), 1)
            dve.wait_ge(summed.sem, summed.after(0))
            step(dve.tensor_reduce(top8[:], p_sum[0:ROUTES, 0:P], AX.X, ALU.max), 2)
            step(dve.tensor_scalar(top_diag[:], s.ident[0:ROUTES, 0:ROUTES], top8[:], None, ALU.mult), 3)
            dve.wait_ge(summed.sem, summed.after(1))
            for r, k in ((0, N_Q), (1, N_KV)):
                some = slice(r * BATCH, (r + 1) * BATCH)
                log = float(np.log(np.float32(min(k * FETCH, float(SEQ)))))
                dve.memset(log_k[:, some], log)
                dve.memset(k_of[:, some], float(k))
                dve.memset(a[:, some], float(np.float32(log) - np.log(np.float32(SEQ))))
            step(dve.tensor_copy(s17[:, :, T:T + 1], p_sum[:, 0:ROUTES].rearrange("p (r a) -> p r a", a=1)), 4)
            with dve.Fori(0, ITERATIONS - 1) as i:
                base = START + i * TURN
                step(dve.tensor_tensor(t17[:], s17[:], wide(a[:], T + 1), ALU.add), base)
                step(dve.scalar_tensor_tensor(nz17[:], t17[:], 0.0, s17[:], ALU.max, ALU.subtract), base + 1)
                step(dve.tensor_tensor(w17[:], nz17[:], nz17[:, :, T:T + 1].broadcast_to([P, ROUTES, T + 1]), ALU.subtract), base + 2)
                step(dve.tensor_tensor(c[:], log_k[:], nz17[:, :, T], ALU.add), base + 3)
                dve.wait_ge(exped.sem, exped.after(i))
                step(dve.tensor_reduce(part[:], e[:], AX.X, ALU.add), base + 4)
                dve.wait_ge(logged.sem, logged.after(i))
                step(dve.tensor_tensor(a[:], c[:], log_sum[:], ALU.subtract), base + 5)
            step(dve.tensor_tensor(t17[:], s17[:], wide(a[:], T + 1), ALU.add), SEARCH)
            step(dve.tensor_scalar(x[:], t17[:, :, 0:T], -1.0, 0.0, ALU.mult, ALU.max), SEARCH + 1)
            dve.memset(limit[:], 0)
            dve.memset(bit_f[:], float(2 ** (FLOAT_BITS - 1)))
            step(dve.tensor_scalar(x_clamped[:], x[:], LOWEST, None, ALU.min), SEARCH + 2)
            step(dve.tensor_copy(bit_i[:], bit_f[:]), SEARCH + 3)
            with dve.Fori(0, FLOAT_BITS) as i:
                base = SEARCH + PREPARE + i * BIT_TURN
                step(dve.tensor_copy(bit_i[:], bit_f[:]), base)
                step(dve.tensor_tensor(trial[:], limit[:], bit_i[:].broadcast_to([P, ROUTES]), ALU.bitwise_or), base + 1)
                step(dve.tensor_tensor(below[:], x_clamped[:], wide(trial[:].bitcast(fp32), T), ALU.is_lt), base + 2)
                step(dve.tensor_reduce(part[:], below[:], AX.X, ALU.add), base + 3)
                dve.wait_ge(summed.sem, summed.after(SUM_BITS + i))
                step(dve.tensor_tensor(few[:], p_sum[:, 0:ROUTES], k_of[:], ALU.is_lt), base + 4)
                step(dve.tensor_scalar(kept[:], few[:], bit_f[:], None, ALU.mult), base + 5)
                step(dve.tensor_tensor(limit[:], limit[:], kept[:], ALU.bitwise_or), base + 6)
                step(dve.tensor_scalar(bit_f[:], bit_f[:], 0.5, None, ALU.mult), base + 7)
            limit_f = wide(limit[:].bitcast(fp32), T)
            step(dve.tensor_tensor(below[:], x_clamped[:], limit_f, ALU.is_lt), SELECT)
            step(dve.tensor_reduce(part[:], below[:], AX.X, ALU.add), SELECT + 1)
            dve.wait_ge(summed.sem, summed.after(SUM_LAST))
            step(dve.tensor_tensor(count[:], k_of[:], p_sum[:, 0:ROUTES], ALU.subtract), SELECT + 2)
            step(dve.tensor_tensor(tie[:], x_clamped[:], limit_f, ALU.is_equal), SELECT + 3)
            dve.wait_ge(summed.sem, summed.after(SUM_LAST + 1))

            def before(at):
                flat = "p r t -> p (r t)"
                every = p_all[:, 0:ROUTES * T]
                step(dve.tensor_tensor_scan(scan[:].rearrange(flat), reset[:].rearrange(flat), every, 0.0, ALU.mult, ALU.add), at)
                step(dve.tensor_tensor(scan[:].rearrange(flat), scan[:].rearrange(flat), every, ALU.subtract), at + 1)
                step(dve.tensor_tensor(order[:].rearrange(flat), scan[:].rearrange(flat), p_tri[:, 0:ROUTES * T], ALU.add), at + 2)

            dve.wait_ge(constants_made, 12)
            before(SELECT + 4)
            step(dve.tensor_tensor(order[:], order[:], wide(count[:], T), ALU.is_lt), SELECT + 7)
            step(dve.tensor_tensor(order[:], order[:], tie[:], ALU.mult), SELECT + 8)
            step(dve.tensor_tensor(chosen[:], order[:], below[:], ALU.add), SELECT + 9)
            dve.wait_ge(exped.sem, exped.after(ITERATIONS - 1))
            step(dve.tensor_scalar(x[:], sc[:], -1.0, 1.0, ALU.mult, ALU.add), SELECT + 10)
            step(dve.tensor_tensor(sc[:], sc[:], x[:], ALU.add), SELECT + 11)
            step(dve.tensor_copy(chosen_b[:], chosen[:]), SELECT + 12)
            step(dve.tensor_scalar(number[:, :, :, 2], sc[:], -1.0, None, ALU.add), SELECT + 13)
            dve.wait_ge(summed.sem, summed.after(SUM_LAST + 2))
            before(SELECT + 14)
            step(dve.scalar_tensor_tensor(place[:], order[:], 1.0, chosen[:], ALU.add, ALU.mult), SELECT + 17)
            step(dve.tensor_scalar(place[:], place[:], -1.0, None, ALU.add), SELECT + 18)
            for n, (b, r, problem) in enumerate(numbered):
                dve.wait_ge(gathered.sem, gathered.after(n - 2))
                k = DRAWN[problem]
                for t in range(T):
                    last = dve.tensor_scalar(one_hot[:, n % 2, t, 0:k], slot[:, 0:k], place[:, problem, t:t + 1], None, ALU.is_equal)
                last.then_inc(hot.sem, 1)
            dve.wait_ge(gathered.sem, gathered.after(len(numbered) - 1))
            step(dve.tensor_scalar(token[:], p_number[:, :, :, 0], float(P), None, ALU.mult), SELECT + 19)
            step(dve.tensor_tensor(token[:], token[:], p_number[:, :, :, 1], ALU.add), SELECT + 20)
            step(dve.tensor_copy(s.token_i[:], token[:]), SELECT + 21)
            step(dve.tensor_scalar(s.weight[:], p_number[:, :, :, 2], 1.0, None, ALU.add), SELECT + 22)


def heavy(nc, s):
    with ExitStack() as ctx:
        def sb(name, shape, dt=fp32):
            return ctx.enter_context(nc.sbuf_tensor(name, shape, dt))

        def ps(name, shape):
            return ctx.enter_context(nc.psum_tensor(name, shape, fp32))

        def steps(name, per=1, lead=2):
            return Steps(ctx.enter_context(nc.semaphore(name)), per, lead)

        EVEN, ODD = slice(0, L_HD), slice(L_HD, P)
        KEYS, ALL_ROWS = N_KV, N_KV + N_Q
        rows_in = sb("rows_in", [P, BATCH, ROW_TILES, DIM])
        x1_rows, light_rows = sb("x1_rows", [P, BATCH, DIM]), sb("h_light_rows", [P, BATCH, DIM])
        out_rows = sb("h_out_rows", [P, BATCH, DIM])
        gamma = sb("gamma", [P, HALVES])
        null_k, null_v = sb("null_k", [P, PAIR_CHUNKS]), sb("null_v", [P, L_HEADS, L_HD + 1])
        own_rows = sb("own_rows", [P, ROW_TILES, DIM])
        squares, square_sum = sb("squares", [P, ROW_TILES, DIM]), sb("square_sum", [P, ROW_TILES])
        norm, inv_norm = sb("norm", [P, ROW_TILES]), sb("inv_norm", [P, ROW_TILES])
        rms = sb("rms", [P, ROW_TILES, DIM])
        rms_t = sb("rms_t", [P, HALVES, ALL_ROWS])
        q_pad = sb("h_q_pad", [P, L_HEADS, P])
        keys, vals = sb("h_keys", [P, PAIR_CHUNKS, KEYS]), sb("h_vals", [P, 2, L_HEADS, L_HD + 1])
        m, m_null = sb("h_m", [P, HALF_HEADS]), sb("h_m_null", [P, L_HEADS])
        z, z_null = sb("h_z", [P, HALF_HEADS, KEYS]), sb("h_z_null", [P, HALF_HEADS])
        probs, p_null = sb("h_probs", [P, HALF_HEADS, KEYS]), sb("h_p_null", [P, HALF_HEADS])
        probs_t = sb("h_probs_t", [P, HALF_HEADS, 2, P])
        o_null, o_all, den = sb("o_null", [P, HALF_HEADS, L_HD + 1]), sb("o_all", [P, HALF_HEADS, L_HD + 1]), sb("h_den", [P, HALF_HEADS])
        o_n, o_t = sb("h_o_n", [P, L_HEADS, L_HD]), sb("h_o_t", [P, PAIR_CHUNKS, P])
        y = sb("h_y", [P, DIM])
        stats, mean_var, inv = sb("stats4", [P, 6]), sb("mean_var4", [P, 2]), sb("inv4", [P, 1])
        p_rms = ps("p_rms", [P, HALVES, 512])
        p_keys = ps("p_keys", [P, PAIR_CHUNKS, KEYS])
        p_probs = ps("p_probs", [P, HALF_HEADS, 2, P])
        p_q, p_o = ps("h_p_q", [P, 512]), ps("h_p_o", [P, 512])
        p_null_s = p_o[:, 384:384 + L_HEADS]
        sums = p_o[:, 0:HALF_HEADS * (L_HD + 1)].rearrange("p (h d) -> p h d", h=HALF_HEADS)

        loaded, filled = ctx.enter_context(nc.semaphore("h_loaded")), ctx.enter_context(nc.semaphore("h_filled"))
        rows_loaded = ctx.enter_context(nc.semaphore("rows_loaded"))
        scattered = ctx.enter_context(nc.semaphore("scattered"))
        copied = steps("own_copied")
        squared, rooted, rms_chain = steps("squared2"), steps("rooted", 2), steps("rms_chain", 2)
        rms_turned, rms_t_ready, projected, vals_done = steps("rms_turned"), steps("rms_t_ready"), steps("h_projected"), steps("vals_done")
        qk_ready, vals_ready, null_scored = steps("h_qk_ready"), steps("h_vals_ready"), steps("null_scored")
        scored, z_chain, z_ready, exped = steps("h_scored"), steps("z_chain", 3), steps("h_z_ready"), steps("h_exped")
        p_turned, p_ready, summed = steps("h_p_turned"), steps("h_p_ready"), steps("h_summed")
        null_added, o_chain, o_ready = steps("null_weighed"), steps("o_chain", 2), steps("h_o_ready")
        o_turned, o_t_ready, y_done = steps("h_o_turned"), steps("h_o_t_ready"), steps("h_y_done")
        y_chain, inverted, rows_ready = steps("y_chain", 5), steps("inverted4", 2), steps("h_rows_ready")
        m_null_ready = steps("m_null_ready")
        block = ctx.enter_context(nc.Block())

        @block.sync
        def _(sp):
            sp.dma_start(gamma[:], s.d_gamma.rearrange("(k p) -> p k", p=P), allow_slow_non_contiguous=True).then_inc(loaded, 16)
            sp.dma_start(null_k[:], s.d_null_kv[0].rearrange("(c a) d -> (a d) c", a=2), allow_slow_non_contiguous=True).then_inc(loaded, 16)
            sp.wait_ge(filled, 3)
            sp.dma_start(null_v[:, :, 0:L_HD], s.d_null_kv[1:2].broadcast_to([P, L_HEADS, L_HD])).then_inc(loaded, 16)

        @block.gpsimd
        def _(pool):
            for made in (rooted, inverted, rows_ready):
                made.open(pool)
            flat = "t p d -> (t p) d"
            for b in range(BATCH):
                sources = [(rows_in[:, b, r], s.d_h, r) for r in range(ROW_TILES)]
                sources += [(x1_rows[:, b], s.d_x1, 2), (light_rows[:, b], s.d_light, 2)]
                for target, source, r in sources:
                    pool.indirect_dma_start(out=target, out_offset=None, in_=source.rearrange(flat),
                                            in_offset=bass.IndirectOffsetOnAxis(ap=s.token_i[:, b, r:r + 1], axis=0))\
                        .then_inc(rows_loaded, 16)
            with pool.Fori(0, BATCH) as b:
                pool.wait_ge(squared.sem, squared.after(b))
                pool.tensor_tensor(norm[:], square_sum[:], s.half[:, 0:ROW_TILES], ALU.pow).then_inc(rooted.sem, 1)
                pool.wait_ge(rooted.sem, rooted.after(b - 1) + 1)
                apart(pool, s)
                pool.tensor_scalar(norm[:], norm[:], 1e-12, None, ALU.max).then_inc(rooted.sem, 1)
                pool.wait_ge(y_chain.sem, y_chain.after(b - 1) + 4)
                apart(pool, s)
                pool.tensor_scalar(inv[:], mean_var[:, 1:2], EPS, None, ALU.add).then_inc(inverted.sem, 1)
                pool.wait_ge(inverted.sem, inverted.after(b - 1) + 1)
                pool.tensor_tensor(inv[:], inv[:], s.power[:, 0:1], ALU.pow).then_inc(inverted.sem, 1)
                pool.wait_ge(y_chain.sem, y_chain.after(b))
                pool.tensor_tensor(out_rows[:, bass.ds(b, 1)].rearrange("p a d -> p (a d)"), y[:],
                                   x1_rows[:, bass.ds(b, 1)].rearrange("p a d -> p (a d)"), ALU.add).then_inc(rows_ready.sem, 1)
            pool.wait_ge(rows_ready.sem, rows_ready.after(BATCH - 1))
            for b in range(BATCH):
                pool.indirect_dma_start(out=s.d_out.rearrange(flat), out_offset=bass.IndirectOffsetOnAxis(ap=s.token_i[:, b, 2:3], axis=0),
                                        in_=out_rows[:, b], in_offset=None).then_inc(scattered, 16)
            pool.wait_ge(scattered, 16 * BATCH)

        @block.tensor
        def _(pe):
            for made in (rms_turned, projected, vals_done, null_scored, scored, p_turned, summed, o_turned, y_done):
                made.open(pe)
            pe.wait_ge(filled, 3)
            pe.wait_ge(loaded, 48)
            with pe.Fori(0, BATCH) as b:
                pe.wait_ge(rms_chain.sem, rms_chain.after(b))
                pe.wait_ge(y_chain.sem, y_chain.after(b - 2) + 1)
                for r in range(ROW_TILES):
                    for k in range(HALVES):
                        last = nc.tensor.transpose(p_rms[:, k, P * r:P * r + P], rms[:, r, P * k:P * k + P], s.ident[:])
                last.then_inc(rms_turned.sem, 1)
                pe.wait_ge(rms_t_ready.sem, rms_t_ready.after(b))
                for c in range(PAIR_CHUNKS):
                    for k in range(HALVES):
                        nc.tensor.matmul(p_q[:, P * c:P * c + P], s.wq_h_t[:, k, P * c:P * c + P], rms_t[:, k, KEYS:ALL_ROWS],
                                         start=(k == 0), stop=(k == HALVES - 1))
                for c in range(PAIR_CHUNKS):
                    for k in range(HALVES):
                        w = s.wkv_h_t[:, k, 0, 2 * c:2 * c + 2].rearrange("p h d -> p (h d)")
                        last = nc.tensor.matmul(p_keys[:, c], w, rms_t[:, k, 0:KEYS], start=(k == 0), stop=(k == HALVES - 1))
                last.then_inc(projected.sem, 1)
                for r in range(2):
                    for k in range(HALVES):
                        w = s.wkv_h_t[:, k, 1].rearrange("p h d -> p (h d)")
                        last = nc.tensor.matmul(p_rms[:, r], rms_t[:, k, P * r:P * r + P], w, start=(k == 0), stop=(k == HALVES - 1))
                last.then_inc(vals_done.sem, 1)
                pe.wait_ge(qk_ready.sem, qk_ready.after(b))
                for h in range(L_HEADS):
                    last = nc.tensor.matmul(p_null_s[:, h:h + 1], q_pad[:, h], null_k[:, h // 2:h // 2 + 1], start=True, stop=True)
                last.then_inc(null_scored.sem, 1)
                for g in range(2):
                    e = b * 2 + g
                    pe.wait_ge(z_ready.sem, z_ready.after(e - 1))
                    for j in range(HALF_HEADS):
                        h = g * HALF_HEADS + j
                        last = nc.tensor.matmul(p_keys[:, j], q_pad[:, h], keys[:, h // 2], start=True, stop=True)
                    last.then_inc(scored.sem, 1)
                    pe.wait_ge(exped.sem, exped.after(e))
                    pe.wait_ge(p_ready.sem, p_ready.after(e - 1))
                    for j in range(HALF_HEADS):
                        for r in range(2):
                            last = nc.tensor.transpose(p_probs[:, j, r], probs[:, j, P * r:P * r + P], s.ident[:])
                    last.then_inc(p_turned.sem, 1)
                    pe.wait_ge(p_ready.sem, p_ready.after(e))
                    pe.wait_ge(vals_ready.sem, vals_ready.after(b))
                    pe.wait_ge(o_chain.sem, o_chain.after(e - 1))
                    pe.wait_ge(m_null_ready.sem, m_null_ready.after(b))
                    for j in range(HALF_HEADS):
                        h = g * HALF_HEADS + j
                        for r in range(2):
                            last = nc.tensor.matmul(sums[:, j], probs_t[:, j, r], vals[:, r, h], start=(r == 0), stop=(r == 1))
                    last.then_inc(summed.sem, 1)
                pe.wait_ge(o_ready.sem, o_ready.after(b * 2 + 1))
                for c in range(PAIR_CHUNKS):
                    last = nc.tensor.transpose(p_q[:, P * c:P * c + P], o_n[:, 2 * c:2 * c + 2].rearrange("p h d -> p (h d)"), s.ident[:])
                last.then_inc(o_turned.sem, 1)
                pe.wait_ge(o_t_ready.sem, o_t_ready.after(b))
                for c in range(PAIR_CHUNKS):
                    last = nc.tensor.matmul(p_rms[:, 0, 0:DIM], o_t[:, c], s.wout_h_t[:, c], start=(c == 0), stop=(c == PAIR_CHUNKS - 1))
                last.then_inc(y_done.sem, 1)

        @block.scalar
        def _(act):
            for made in (rms_t_ready, qk_ready, exped, p_ready, o_t_ready):
                made.open(act)
            act.wait_ge(loaded, 48)
            act.wait_ge(filled, 3)
            with act.Fori(0, BATCH) as b:
                act.wait_ge(rms_turned.sem, rms_turned.after(b))
                for k in range(HALVES):
                    last = act.activation(rms_t[:, k], p_rms[:, k, 0:ALL_ROWS], ACT.Copy, scale=gamma[:, k:k + 1])
                last.then_inc(rms_t_ready.sem, 1)
                act.wait_ge(projected.sem, projected.after(b))
                q = p_q[:].rearrange("p (c n) -> p c n", c=PAIR_CHUNKS)
                pairs = q_pad[:].rearrange("p (c a) n -> p c a n", a=2)
                act.activation(pairs[EVEN, :, 0], q[EVEN], ACT.Copy)
                act.activation(pairs[ODD, :, 1], q[ODD], ACT.Copy)
                act.activation(keys[:], p_keys[:], ACT.Copy).then_inc(qk_ready.sem, 1)
                for g in range(2):
                    e = b * 2 + g
                    act.wait_ge(z_ready.sem, z_ready.after(e))
                    act.wait_ge(null_added.sem, null_added.after(e - 1))
                    act.activation(p_null[:], z_null[:], ACT.Exp, scale=L_SCALE)
                    act.activation(probs[:], z[:], ACT.Exp, scale=L_SCALE).then_inc(exped.sem, 1)
                    act.wait_ge(p_turned.sem, p_turned.after(e))
                    act.activation(probs_t[:], p_probs[:], ACT.Copy).then_inc(p_ready.sem, 1)
                act.wait_ge(o_turned.sem, o_turned.after(b))
                act.activation(o_t[:], p_q[:].rearrange("p (c n) -> p c n", c=PAIR_CHUNKS), ACT.Copy).then_inc(o_t_ready.sem, 1)

        @block.vector
        def _(dve):
            for made in (copied, squared, rms_chain, vals_ready, m_null_ready, z_chain, z_ready, null_added, o_chain, o_ready, y_chain):
                made.open(dve)
            dve.memset(q_pad[:], 0.0).then_inc(filled, 1)
            dve.memset(vals[:], 1.0).then_inc(filled, 1)
            dve.memset(null_v[:], 1.0).then_inc(filled, 1)
            dve.wait_ge(loaded, 48)
            dve.wait_ge(rows_loaded, 16 * BATCH * 5)

            def wide(x, n):
                return x.rearrange("p (h a) -> p h a", a=1).broadcast_to([P, HALF_HEADS, n])

            with dve.Fori(0, BATCH) as b:
                rows = rows_in[:, bass.ds(b, 1)].rearrange("p a r d -> p (a r) d")
                dve.tensor_copy(own_rows[:], rows).then_inc(copied.sem, 1)
                dve.wait_ge(copied.sem, copied.after(b))
                for r in range(ROW_TILES):
                    last = dve.tensor_tensor_reduce(out=squares[:, r], in0=own_rows[:, r], in1=own_rows[:, r], scale=1.0, scalar=0.0,
                                                    op0=ALU.mult, op1=ALU.add, accum_out=square_sum[:, r:r + 1])
                last.then_inc(squared.sem, 1)
                dve.wait_ge(rooted.sem, rooted.after(b))
                dve.reciprocal(inv_norm[:], norm[:]).then_inc(rms_chain.sem, 1)
                dve.wait_ge(rms_chain.sem, rms_chain.after(b - 1) + 1)
                for r in range(ROW_TILES):
                    last = dve.tensor_scalar(rms[:, r], rows[:, r], inv_norm[:, r:r + 1], float(DIM) ** 0.5, ALU.mult, ALU.mult)
                last.then_inc(rms_chain.sem, 1)
                dve.wait_ge(vals_done.sem, vals_done.after(b))
                for r in range(2):
                    last = dve.tensor_scalar(vals[:, r, :, 0:L_HD], p_rms[:, r].rearrange("p (h d) -> p h d", h=L_HEADS),
                                             s.weight[:, bass.ds(b, 1), r], None, ALU.mult)
                last.then_inc(vals_ready.sem, 1)
                dve.wait_ge(null_scored.sem, null_scored.after(b))
                dve.tensor_copy(m_null[:], p_null_s).then_inc(m_null_ready.sem, 1)
                dve.wait_ge(m_null_ready.sem, m_null_ready.after(b))
                for g in range(2):
                    e = b * 2 + g
                    null_s = m_null[:, HALF_HEADS * g:HALF_HEADS * (g + 1)]
                    dve.wait_ge(scored.sem, scored.after(e))
                    dve.tensor_reduce(m[:], p_keys[:], AX.X, ALU.max).then_inc(z_chain.sem, 1)
                    dve.wait_ge(z_chain.sem, z_chain.after(e - 1) + 1)
                    dve.tensor_tensor(m[:], m[:], null_s, ALU.max).then_inc(z_chain.sem, 1)
                    dve.wait_ge(z_chain.sem, z_chain.after(e - 1) + 2)
                    dve.wait_ge(exped.sem, exped.after(e - 1))
                    dve.tensor_tensor(z_null[:], null_s, m[:], ALU.subtract).then_inc(z_chain.sem, 1)
                    dve.tensor_tensor(z[:], p_keys[:], wide(m[:], KEYS), ALU.subtract).then_inc(z_ready.sem, 1)
                    dve.wait_ge(exped.sem, exped.after(e))
                    dve.tensor_tensor(o_null[:], null_v[:, HALF_HEADS * g:HALF_HEADS * (g + 1)], wide(p_null[:], L_HD + 1), ALU.mult)\
                       .then_inc(null_added.sem, 1)
                    dve.wait_ge(null_added.sem, null_added.after(e))
                    dve.wait_ge(summed.sem, summed.after(e))
                    dve.tensor_tensor(o_all[:], sums, o_null[:], ALU.add).then_inc(o_chain.sem, 1)
                    dve.wait_ge(o_chain.sem, o_chain.after(e - 1) + 1)
                    dve.reciprocal(den[:], o_all[:, :, L_HD]).then_inc(o_chain.sem, 1)
                    dve.wait_ge(o_chain.sem, o_chain.after(e))
                    dve.tensor_tensor(o_n[:, HALF_HEADS * g:HALF_HEADS * (g + 1)], o_all[:, :, 0:L_HD], wide(den[:], L_HD), ALU.mult)\
                       .then_inc(o_ready.sem, 1)
                base = y_chain.after(b - 1)
                dve.wait_ge(y_done.sem, y_done.after(b))
                dve.wait_ge(rows_ready.sem, rows_ready.after(b - 1))
                dve.tensor_scalar(y[:], p_rms[:, 0, 0:DIM], s.weight[:, bass.ds(b, 1), 2], None, ALU.mult).then_inc(y_chain.sem, 1)
                dve.wait_ge(y_chain.sem, base + 1)
                dve.tensor_tensor(y[:], y[:], light_rows[:, bass.ds(b, 1)].rearrange("p a d -> p (a d)"), ALU.add).then_inc(y_chain.sem, 1)
                dve.wait_ge(y_chain.sem, base + 2)
                dve.bn_stats(stats[:], y[:]).then_inc(y_chain.sem, 1)
                dve.wait_ge(y_chain.sem, base + 3)
                apart(dve, s)
                dve.bn_aggr(mean_var[:], stats[:]).then_inc(y_chain.sem, 1)
                dve.wait_ge(inverted.sem, inverted.after(b))
                dve.tensor_scalar(y[:], y[:], mean_var[:, 0:1], inv[:, 0:1], ALU.subtract, ALU.mult).then_inc(y_chain.sem, 1)


class Memory:
    pass


def build(nc, ins, out, debug=None):
    with ExitStack() as ctx:
        s = Memory()
        kind = "ExternalOutput" if debug else "Internal"

        def dram(name, shape, dt=fp32):
            return nc.dram_tensor(name, shape, dt, kind=kind).ap()

        def sb(name, shape, dt=fp32):
            return ctx.enter_context(nc.sbuf_tensor(name, shape, dt))

        (x, s.d_w_q, s.d_b_q, s.d_w_k, s.d_b_k, s.d_w_v, s.d_b_v, s.d_w_o, s.d_b_o, s.d_ln_w, s.d_ln_b, s.d_wqkv,
         s.d_wout_l, s.d_rt_q, s.d_rt_kv, s.d_gamma, s.d_wq_h, s.d_wkv_h, s.d_wout_h, s.d_null_kv, s.d_null_q) = ins
        s.d_x = x.rearrange("b (t p) d -> (b t) p d", p=P)
        q_parts = dram("q_parts", [PARTS, BATCH * HALVES, P, SEQ], bf16)
        k_parts = dram("k_parts", [PARTS, BATCH, KVD, SEQ], bf16)
        shift = dram("shift", [2, BATCH * HEADS, SEQ], bf16)
        attended = dram("attended", [BATCH * HALVES, P, SEQ])
        s.d_q_parts, s.d_k_parts, s.d_shift = q_parts, k_parts, shift
        s.q_rows = q_parts.rearrange("r b (h p) n -> r (b h) p n", p=HD)
        s.k_rows = k_parts.rearrange("r b (h p) n -> r (b h) p n", p=HD)
        s.a_rows = attended.rearrange("b (h p) n -> (b h) p n", p=HD).rearrange("(j h) p n -> j h p n", h=GROUP)
        s.d_attended = attended
        s.d_x1, s.d_h = dram("x1", [TILES, P, DIM]), dram("h", [TILES, P, DIM])
        s.d_u_t = dram("u_t", [P, HALVES, TOKENS])
        s.d_light = dram("light", [TILES, P, DIM])
        s.d_s = dram("route_dbg", [P, 2, TILES]) if debug else None
        s.d_out = out.rearrange("b (t p) d -> (b t) p d", p=P)
        s.ident = sb("ident", [P, P])
        s.passed = {engine.engine: ctx.enter_context(nc.semaphore(f"passed_{name}"))
                    for name, engine in (("pe", nc.tensor), ("dve", nc.vector), ("pool", nc.gpsimd), ("sp", nc.sync))}
        s.power, s.half = sb("power", [P, 16]), sb("half", [P, 16])
        s.token_i, s.weight = sb("token_i", [P, BATCH, ROW_TILES], i32), sb("weight", [P, BATCH, ROW_TILES])
        s.route_s = sb("route_s", [P, 2, TILES])
        with ExitStack() as first:
            def sb1(name, shape, dt=fp32):
                return first.enter_context(nc.sbuf_tensor(name, shape, dt))
            s.heads_of = sb1("heads_of", [P, 8])
            s.norm_sel = sb1("norm_sel", [P, 3, 20], bf16)
            s.zero_row = sb1("zero_row", [P, SEQ], bf16)
            s.norm_max = sb1("norm_max", [20, BATCH * BLOCKS_B])
            s.v_all = sb1("v_all", [P, BATCH * KV, TILES_B, 2 * HD])
            s.k_stack = sb1("k_stack", [P, 2, SEQ], bf16)
            s.w_q, s.w_k, s.w_v = sb1("w_q", [P, HALVES, DIM]), sb1("w_k", [P, HALVES, KVD]), sb1("w_v", [P, HALVES, KVD])
            s.b_q, s.b_k, s.b_v = sb1("b_q", [P, HALVES]), sb1("b_k", [KVD, 1]), sb1("b_v", [P, KVD])
            constants(nc, s)
            s.loose = sb1("loose", [1, 1], i32)
            project(nc, s)
            bound_scores(nc, s)
            largest_scores(nc, s)
            attend(nc, s)
        merge(nc, s)
        s.w_qkv_t, s.wout_l_t = sb("w_qkv_t", [P, HALVES, 3 * 512]), sb("wout_l_t", [P, 4, DIM])
        s.wq_h_t, s.wkv_h_t, s.wout_h_t = sb("wq_h_t", [P, HALVES, 512]), sb("wkv_h_t", [P, HALVES, 2, L_HEADS, L_HD]), sb("wout_h_t", [P, 4, DIM])
        transpose_weights(nc, s)
        local(nc, s)
        route(nc, s)
        heavy(nc, s)


_INS = ["L0_attn_x", "L0_attn_w_q", "L0_attn_b_q", "L0_attn_w_k", "L0_attn_b_k", "L0_attn_w_v", "L0_attn_b_v", "L0_attn_w_o",
        "L0_attn_b_o", "L0_ffn_ln_w", "L0_ffn_ln_b", "L0_ffn_Wqkv", "L0_ffn_Wout_l", "L0_ffn_rt_q", "L0_ffn_rt_kv", "L0_ffn_gamma",
        "L0_ffn_Wq", "L0_ffn_Wkv", "L0_ffn_Wout_h", "L0_ffn_null_kv", "L0_ffn_null_q"]


def kernel(**inputs):
    import numpy as _np
    import concourse.bacc as _bacc
    from concourse import mybir as _mybir
    from concourse.bass_utils import run_bass_kernel_spmd as _run

    nc = _bacc.Bacc("TRN2", target_bir_lowering=False, num_devices=1)
    arrays, args = {}, []
    for name in _INS:
        a = _np.ascontiguousarray(inputs[name])
        arrays[f"in_{name}"] = a
        args.append(nc.dram_tensor(f"in_{name}", a.shape, _mybir.dt.from_np(a.dtype), kind="ExternalInput").ap())
    out = nc.dram_tensor("out", (BATCH, SEQ, DIM), _mybir.dt.float32, kind="ExternalOutput").ap()
    build(nc, args, out)
    r = _run(nc, [arrays], core_ids=[0])
    return r.results[0]["out"]
```

```python
import concourse.bass as bass
import numpy as np
from concourse import mybir
from contextlib import ExitStack

fp32 = mybir.dt.float32
bf16 = mybir.dt.bfloat16
i32 = mybir.dt.int32
ALU = mybir.AluOpType
ACT = mybir.ActivationFunctionType
AX = mybir.AxisListType

BATCH, SEQ, DIM = 4, 2048, 256
TOKENS = BATCH * SEQ
P = 128
TILES = TOKENS // P
TILES_B = SEQ // P
BLOCK = 512
BT = BLOCK // P
BLOCKS_B = SEQ // BLOCK
HALVES = DIM // P
EPS = 1e-5
HEADS, KV, GROUP, HD = 16, 4, 4, 16
KVD = KV * HD
PARTS = 3
Q_PART = (0, 0, 1, 1, 0, 2)
K_PART = (0, 1, 0, 1, 2, 0)
SLOTS = len(Q_PART)
STACK = SLOTS * HD
ROWS = STACK + 2
A_SCALE = 1.0 / float(HD) ** 0.5
FAR = -1e38
GUARD = 50.0


class Steps:

    def __init__(self, sem, per=1, lead=2):
        self.sem, self.per, self.lead = sem, per, lead

    def open(self, eng):
        eng.sem_inc(self.sem, self.lead * self.per)

    def after(self, step):
        return (step + 1 + self.lead) * self.per


def apart(engine, s):
    engine.sem_inc(s.passed[engine.engine], 1)


def inverse_root(pool, s, out, var, power, inverted, step):
    apart(pool, s)
    pool.tensor_scalar(out, var, EPS, None, ALU.add).then_inc(inverted.sem, 1)
    pool.wait_ge(inverted.sem, inverted.after(step - 1) + 1)
    pool.tensor_tensor(out, out, power, ALU.pow).then_inc(inverted.sem, 1)


def constants(nc, s):
    with nc.semaphore("const_filled") as const_filled, nc.semaphore("const_zero_out") as zero_out, \
            nc.semaphore("const_loaded") as loaded, nc.semaphore("rows_filled") as rows_filled, nc.Block() as block:

        @block.gpsimd
        def _(pool):
            pool.memset(s.ident[:], 0.0).then_inc(const_filled, 1)
            pool.memset(s.heads_of[:], 1.0).then_inc(const_filled, 1)
            pool.wait_ge(const_filled, 2)
            pool.affine_select(out=s.ident[:], in_=s.ident[:], compare_op=ALU.not_equal, fill=1.0,
                               base=0, pattern=[[-1, P]], channel_multiplier=1).then_inc(const_filled, 1)
            pool.affine_select(out=s.heads_of[:], in_=s.heads_of[:], compare_op=ALU.is_ge, fill=0.0,
                               base=0, pattern=[[-HD, 8]], channel_multiplier=1).then_inc(const_filled, 1)
            pool.wait_ge(const_filled, 4)
            pool.affine_select(out=s.heads_of[:], in_=s.heads_of[:], compare_op=ALU.is_ge, fill=0.0,
                               base=HD - 1, pattern=[[HD, 8]], channel_multiplier=-1).then_inc(const_filled, 1)
            pool.wait_ge(const_filled, 5)
            pool.memset(s.norm_sel[:], 0.0).then_inc(const_filled, 1)
            pool.wait_ge(const_filled, 6)
            pool.tensor_copy(s.norm_sel[:, 0, 0:8], s.heads_of[:]).then_inc(const_filled, 1)
            pool.tensor_copy(s.norm_sel[:, 1, 8:16], s.heads_of[:]).then_inc(const_filled, 1)
            pool.tensor_copy(s.norm_sel[0:KVD, 2, 16:20], s.heads_of[0:KVD, 0:KV]).then_inc(const_filled, 1)

        @block.vector
        def _(dve):
            dve.memset(s.v_all[:, :, :, HD:], 1.0).then_inc(rows_filled, 1)
            dve.memset(s.k_stack[STACK:ROWS, :, :], 1.0).then_inc(rows_filled, 1)
            dve.memset(s.zero_row[:], 0.0).then_inc(rows_filled, 1)
            dve.memset(s.power[:], -0.5).then_inc(rows_filled, 1)
            dve.memset(s.half[:], 0.5).then_inc(rows_filled, 1)

        @block.sync
        def _(sp):
            sp.dma_start(s.w_q[:], s.d_w_q.rearrange("(k p) n -> p k n", p=P)).then_inc(loaded, 16)
            sp.dma_start(s.w_k[:], s.d_w_k.rearrange("(k p) n -> p k n", p=P)).then_inc(loaded, 16)
            sp.dma_start(s.w_v[:], s.d_w_v.rearrange("(k p) n -> p k n", p=P)).then_inc(loaded, 16)
            sp.dma_start(s.b_q[:], s.d_b_q.rearrange("(k p) -> p k", p=P), allow_slow_non_contiguous=True).then_inc(loaded, 16)
            sp.dma_start(s.b_k[:], s.d_b_k.rearrange("(p k) -> p k", k=1), allow_slow_non_contiguous=True).then_inc(loaded, 16)
            sp.dma_start(s.b_v[:], s.d_b_v.rearrange("(a n) -> a n", a=1).broadcast_to([P, KVD]))\
              .then_inc(loaded, 16)
            sp.wait_ge(rows_filled, 3)
            sp.dma_start(s.d_shift, s.zero_row[:]).then_inc(zero_out, 16)
            sp.wait_ge(loaded, 6 * 16)
            sp.wait_ge(zero_out, 16)


def block_at(b, c, by):
    return b + (c + by) // BLOCKS_B, (c + by) % BLOCKS_B


def over_blocks(eng, before, turn):
    before()
    with eng.Fori(0, BATCH - 1) as b:
        for c in range(BLOCKS_B):
            turn(b, c, lambda by: True)
    for c in range(BLOCKS_B):
        turn(BATCH - 1, c, lambda by, c=c: c + by < BLOCKS_B)


def project(nc, s):
    with ExitStack() as ctx:
        def sb(name, shape, dt=fp32):
            return ctx.enter_context(nc.sbuf_tensor(name, shape, dt))

        def ps(name, shape):
            return ctx.enter_context(nc.psum_tensor(name, shape, fp32))

        def sem(name):
            return ctx.enter_context(nc.semaphore(name))

        x_in = sb("x_in", [P, BLOCKS_B, BT, DIM])
        stats = sb("stats", [P, 2, BT, 6])
        mean_var = sb("mean_var", [P, 2, BT, 2])
        inv = sb("inv", [P, 2, BT])
        x_n = sb("x_n", [P, 2, BT, DIM])
        x_t = sb("x_t", [P, 2, HALVES, BLOCK])
        q_f = sb("q_f", [P, 2, HALVES, BLOCK])
        k_f = sb("k_f", [KVD, 2, BLOCK])
        q_sq = sb("q_sq", [P, HALVES, BLOCK], bf16)
        k_sq = sb("k_sq", [KVD, BLOCK], bf16)
        q_p = sb("q_p", [P, 2, PARTS, HALVES, BLOCK], bf16)
        k_p = sb("k_p", [KVD, 2, PARTS, BLOCK], bf16)
        q_rest = sb("q_rest", [P, HALVES, BLOCK])
        k_rest = sb("k_rest", [KVD, BLOCK])
        p_t = ps("p_t", [P, HALVES, BLOCK])
        p_q = ps("p_q", [P, HALVES, BLOCK])
        p_k = ps("p_k", [P, BLOCK])
        p_v = ps("p_v", [P, BLOCK])
        p_norm = ps("p_norm", [P, BLOCK])

        def steps(name, per=1):
            return Steps(sem(name), per, 4)

        x_loaded = [steps(f"x_loaded_{c}", 16) for c in range(BLOCKS_B)]
        normed, norm_step, inverted = steps("normed"), steps("norm_step", 2), steps("inverted", 2)
        transposed, x_t_ready = steps("transposed"), steps("x_t_ready")
        qk_projected = steps("qk_projected")
        projected, biased, v_ready = steps("projected"), steps("biased"), steps("v_ready")
        q_split, k_split = steps("q_split", 4), steps("k_split", 4)
        q_out = [steps(f"q_out_{u}", 32) for u in range(2)]
        k_out = [steps(f"k_out_{u}", 16) for u in range(2)]
        squared, norms, norms_read = steps("squared"), steps("norms"), steps("norms_read")
        block = ctx.enter_context(nc.Block())

        @block.sync
        def _(sp):
            for made in (*x_loaded, *q_out, *k_out):
                made.open(sp)

            def load(b, c):
                sp.wait_ge(normed.sem, normed.after(b * BLOCKS_B + c - BLOCKS_B))
                sp.dma_start(x_in[:, c], s.d_x[bass.ds(b * TILES_B + BT * c, BT)].rearrange("t p d -> p t d"))\
                  .then_inc(x_loaded[c].sem, 16)

            def store(b, c):
                g, u = b * BLOCKS_B + c, c % 2
                sp.wait_ge(q_split.sem, q_split.after(g))
                for m in range(HALVES):
                    sp.dma_start(s.d_q_parts[:, bass.ds(b * 2 + m, 1), :, bass.ts(c, BLOCK)]
                                 .rearrange("r a p n -> p r (a n)"), q_p[:, u, :, m, :]).then_inc(q_out[u].sem, 16)
                sp.wait_ge(k_split.sem, k_split.after(g))
                sp.dma_start(s.d_k_parts[:, bass.ds(b, 1), :, bass.ts(c, BLOCK)]
                             .rearrange("r a p n -> p r (a n)"), k_p[:, u, :, :]).then_inc(k_out[u].sem, 16)

            def before():
                for c in range(3):
                    load(0, c)

            def turn(b, c, has):
                if has(3):
                    load(*block_at(b, c, 3))
                store(b, c)

            over_blocks(sp, before, turn)
            for u in range(2):
                sp.wait_ge(q_out[u].sem, q_out[u].after(BATCH * BLOCKS_B // 2 - 1))
                sp.wait_ge(k_out[u].sem, k_out[u].after(BATCH * BLOCKS_B // 2 - 1))

        @block.vector
        def _(dve):
            for made in (normed, norm_step, v_ready, q_split, norms_read):
                made.open(dve)

            def statistics(b, c):
                g, u = b * BLOCKS_B + c, c % 2
                dve.wait_ge(x_loaded[c].sem, x_loaded[c].after(b))
                dve.wait_ge(normed.sem, normed.after(g - 2))
                for t in range(BT):
                    last = dve.bn_stats(stats[:, u, t], x_in[:, c, t])
                last.then_inc(norm_step.sem, 1)
                dve.wait_ge(norm_step.sem, norm_step.after(g - 1) + 1)
                apart(dve, s)
                for t in range(BT):
                    last = dve.bn_aggr(mean_var[:, u, t], stats[:, u, t])
                last.then_inc(norm_step.sem, 1)

            def normalise(b, c):
                g, u = b * BLOCKS_B + c, c % 2
                dve.wait_ge(inverted.sem, inverted.after(g))
                dve.wait_ge(transposed.sem, transposed.after(g - 2))
                for t in range(BT):
                    last = dve.tensor_scalar(x_n[:, u, t], x_in[:, c, t], mean_var[:, u, t, 0:1], inv[:, u, t:t + 1],
                                             ALU.subtract, ALU.mult)
                last.then_inc(normed.sem, 1)

            def before():
                statistics(0, 0)
                statistics(0, 1)
                normalise(0, 0)

            def turn(b, c, has):
                g, u = b * BLOCKS_B + c, c % 2
                v = b * (BLOCKS_B // 2) + c // 2
                if has(1):
                    normalise(*block_at(b, c, 1))
                if has(2):
                    statistics(*block_at(b, c, 2))
                dve.wait_ge(biased.sem, biased.after(g))
                dve.wait_ge(q_out[u].sem, q_out[u].after(v - 1))
                dve.tensor_copy(q_p[:, u, 0], q_f[:, u]).then_inc(q_split.sem, 1)
                dve.wait_ge(q_split.sem, q_split.after(g - 1) + 1)
                dve.tensor_tensor(q_rest[:], q_f[:, u], q_p[:, u, 0], ALU.subtract).then_inc(q_split.sem, 1)
                dve.wait_ge(projected.sem, projected.after(g))
                for t in range(BT):
                    out = s.v_all[:, bass.ds(b * KV, KV), BT * c + t, 0:HD]
                    last = dve.tensor_tensor(out, p_v[:, KVD * t:KVD * t + KVD].rearrange("p (k d) -> p k d", k=KV),
                                             s.b_v[:].rearrange("p (k d) -> p k d", k=KV), ALU.add)
                last.then_inc(v_ready.sem, 1)
                dve.wait_ge(q_split.sem, q_split.after(g - 1) + 2)
                dve.tensor_copy(q_p[:, u, 1], q_rest[:]).then_inc(q_split.sem, 1)
                dve.wait_ge(q_split.sem, q_split.after(g - 1) + 3)
                dve.tensor_tensor(q_p[:, u, 2], q_rest[:], q_p[:, u, 1], ALU.subtract).then_inc(q_split.sem, 1)
                dve.wait_ge(norms.sem, norms.after(g))
                dve.tensor_reduce(s.norm_max[:, bass.ds(g, 1)], p_norm[0:20, :], AX.X, ALU.max)\
                   .then_inc(norms_read.sem, 1)

            over_blocks(dve, before, turn)

        @block.gpsimd
        def _(pool):
            k_split.open(pool)
            inverted.open(pool)

            def root(b, c):
                g, u = b * BLOCKS_B + c, c % 2
                pool.wait_ge(norm_step.sem, norm_step.after(g))
                pool.wait_ge(normed.sem, normed.after(g - 2))
                inverse_root(pool, s, inv[:, u], mean_var[:, u, :, 1], s.power[:, 0:BT], inverted, g)

            def before():
                root(0, 0)
                root(0, 1)

            def turn(b, c, has):
                g, u = b * BLOCKS_B + c, c % 2
                if has(2):
                    root(*block_at(b, c, 2))
                pool.wait_ge(biased.sem, biased.after(g))
                pool.wait_ge(k_out[u].sem, k_out[u].after(b * (BLOCKS_B // 2) + c // 2 - 1))
                apart(pool, s)
                pool.tensor_copy(k_p[:, u, 0], k_f[:, u]).then_inc(k_split.sem, 1)
                pool.wait_ge(k_split.sem, k_split.after(g - 1) + 1)
                pool.tensor_tensor(k_rest[:], k_f[:, u], k_p[:, u, 0], ALU.subtract).then_inc(k_split.sem, 1)
                pool.wait_ge(k_split.sem, k_split.after(g - 1) + 2)
                apart(pool, s)
                pool.tensor_copy(k_p[:, u, 1], k_rest[:]).then_inc(k_split.sem, 1)
                pool.wait_ge(k_split.sem, k_split.after(g - 1) + 3)
                pool.tensor_tensor(k_p[:, u, 2], k_rest[:], k_p[:, u, 1], ALU.subtract).then_inc(k_split.sem, 1)

            over_blocks(pool, before, turn)

        @block.scalar
        def _(act):
            for made in (x_t_ready, biased, squared):
                made.open(act)

            def take_x(b, c):
                g, u = b * BLOCKS_B + c, c % 2
                act.wait_ge(transposed.sem, transposed.after(g))
                act.wait_ge(projected.sem, projected.after(g - 2))
                act.activation(x_t[:, u], p_t[:], ACT.Copy).then_inc(x_t_ready.sem, 1)

            def before():
                take_x(0, 0)

            def turn(b, c, has):
                g, u = b * BLOCKS_B + c, c % 2
                act.wait_ge(qk_projected.sem, qk_projected.after(g))
                act.wait_ge(q_split.sem, q_split.after(g - 2))
                act.wait_ge(k_split.sem, k_split.after(g - 2))
                for m in range(HALVES):
                    act.activation(q_f[:, u, m], p_q[:, m, :], ACT.Identity, bias=s.b_q[:, m:m + 1])
                act.activation(k_f[:, u], p_k[0:KVD, :], ACT.Identity, bias=s.b_k[:]).then_inc(biased.sem, 1)
                act.wait_ge(biased.sem, biased.after(g))
                act.wait_ge(norms.sem, norms.after(g - 1))
                act.activation(q_sq[:], q_f[:, u], ACT.Square)
                act.activation(k_sq[:], k_f[:, u], ACT.Square).then_inc(squared.sem, 1)
                if has(1):
                    take_x(*block_at(b, c, 1))

            over_blocks(act, before, turn)

        @block.tensor
        def _(pe):
            for made in (transposed, qk_projected, projected, norms):
                made.open(pe)

            def turn_x(b, c):
                g, u = b * BLOCKS_B + c, c % 2
                pe.wait_ge(normed.sem, normed.after(g))
                pe.wait_ge(x_t_ready.sem, x_t_ready.after(g - 1))
                for t in range(BT):
                    for h in range(HALVES):
                        last = nc.tensor.transpose(p_t[:, h, P * t:P * t + P], x_n[:, u, t, P * h:P * h + P], s.ident[:])
                last.then_inc(transposed.sem, 1)

            def before():
                turn_x(0, 0)

            def turn(b, c, has):
                g, u = b * BLOCKS_B + c, c % 2
                pe.wait_ge(x_t_ready.sem, x_t_ready.after(g))
                pe.wait_ge(biased.sem, biased.after(g - 1))
                for m in range(HALVES):
                    for k in range(HALVES):
                        nc.tensor.matmul(p_q[:, m, :], s.w_q[:, k, P * m:P * m + P], x_t[:, u, k, :],
                                         start=(k == 0), stop=(k == HALVES - 1))
                for k in range(HALVES):
                    last = nc.tensor.matmul(p_k[0:KVD, :], s.w_k[:, k, :], x_t[:, u, k, :],
                                            start=(k == 0), stop=(k == HALVES - 1))
                last.then_inc(qk_projected.sem, 1)
                pe.wait_ge(v_ready.sem, v_ready.after(g - 1))
                for t in range(BT):
                    for k in range(HALVES):
                        last = nc.tensor.matmul(p_v[:, KVD * t:KVD * t + KVD], x_t[:, u, k, P * t:P * t + P],
                                                s.w_v[:, k, :], start=(k == 0), stop=(k == HALVES - 1))
                last.then_inc(projected.sem, 1)
                if has(1):
                    turn_x(*block_at(b, c, 1))
                pe.wait_ge(squared.sem, squared.after(g))
                pe.wait_ge(norms_read.sem, norms_read.after(g - 1))
                nc.tensor.matmul(p_norm[0:20, :], s.norm_sel[:, 0, :], q_sq[:, 0, :], start=True, stop=False)
                nc.tensor.matmul(p_norm[0:20, :], s.norm_sel[:, 1, :], q_sq[:, 1, :], start=False, stop=False)
                nc.tensor.matmul(p_norm[0:20, :], s.norm_sel[0:KVD, 2, :], k_sq[:], start=False, stop=True)\
                  .then_inc(norms.sem, 1)

            over_blocks(pe, before, turn)


def bound_scores(nc, s):
    with nc.sbuf_tensor("norm_all", [20, 1], fp32) as norm_all, nc.sbuf_tensor("norm_top", [1, 4], fp32) as norm_top, \
            nc.psum_tensor("norm_row", [1, 20], fp32) as norm_row, nc.semaphore("bounded") as bounded, \
            nc.semaphore("norm_turned") as turned, nc.Block() as block:

        @block.tensor
        def _(pe):
            pe.wait_ge(bounded, 1)
            nc.tensor.matmul(norm_row[:], norm_all[:], s.ident[0:20, 0:20], start=True, stop=True).then_inc(turned, 1)

        @block.vector
        def _(dve):
            dve.tensor_reduce(norm_all[:], s.norm_max[:], AX.X, ALU.max).then_inc(bounded, 1)
            dve.wait_ge(turned, 1)
            dve.tensor_reduce(norm_top[:, 0:1], norm_row[:, 0:HEADS], AX.X, ALU.max)
            dve.tensor_reduce(norm_top[:, 1:2], norm_row[:, HEADS:], AX.X, ALU.max).then_inc(bounded, 1)
            dve.wait_ge(bounded, 2)
            dve.tensor_tensor(norm_top[:, 2:3], norm_top[:, 0:1], norm_top[:, 1:2], ALU.mult).then_inc(bounded, 1)
            dve.wait_ge(bounded, 3)
            dve.tensor_scalar(norm_top[:, 3:4], norm_top[:, 2:3], (GUARD / A_SCALE) ** 2, None, ALU.is_le).then_inc(bounded, 1)
            dve.wait_ge(bounded, 4)
            dve.tensor_scalar(s.loose[:], norm_top[:, 3:4], -1.0, 1.0, ALU.mult, ALU.add).then_inc(bounded, 1)
            dve.wait_ge(bounded, 5)


def largest_scores(nc, s):
    PAIRS = BATCH * KV
    with ExitStack() as ctx:
        def sb(name, shape, dt=fp32):
            return ctx.enter_context(nc.sbuf_tensor(name, shape, dt))

        def steps(name, per=1, lead=2):
            return Steps(ctx.enter_context(nc.semaphore(name)), per, lead)

        q_stack = sb("m_q_stack", [STACK, GROUP, SEQ], bf16)
        ahead, masked = sb("ahead", [P, P]), sb("m_masked", [P, P])
        found = sb("found", [P, 2, GROUP, TILES_B])
        least = sb("least", [P, GROUP * TILES_B])
        rest = sb("m_rest", [GROUP * TILES_B, P])
        parts = sb("m_parts", [GROUP * TILES_B, 2, P], bf16)
        scores = ctx.enter_context(nc.psum_tensor("m_scores", [P, SEQ], fp32))
        turned = ctx.enter_context(nc.psum_tensor("m_turned", [GROUP * TILES_B, P], fp32))
        jobs = [(h, t) for h in range(GROUP) for t in range(TILES_B)]
        filled = ctx.enter_context(nc.semaphore("m_filled"))
        loaded, stored = steps("m_loaded", 16 * 2 * SLOTS), steps("m_stored", 16)
        scored, masked_done, taken = steps("m_scored"), steps("m_masked_done"), steps("m_taken")
        joined, split, flipped = steps("m_joined", 2), steps("m_split", 3), steps("m_flipped")
        block = ctx.enter_context(nc.Block())

        @block.gpsimd
        def _(pool):
            with pool.If(pool.value_load(s.loose[:], min_val=0, max_val=1) > 0):
                pool.memset(ahead[:], 0.0).then_inc(filled, 1)
                pool.wait_ge(filled, 1)
                pool.affine_select(out=ahead[:], in_=ahead[:], compare_op=ALU.is_ge, fill=FAR, base=0, pattern=[[-1, P]],
                                   channel_multiplier=1).then_inc(filled, 1)
            with pool.Else():
                pass

        @block.sync
        def _(sp):
            with sp.If(sp.value_load(s.loose[:], min_val=0, max_val=1) > 0):
                loaded.open(sp)
                stored.open(sp)
                with sp.Fori(0, PAIRS) as j:
                    sp.wait_ge(joined.sem, joined.after(j - 1))
                    for n in range(SLOTS):
                        rows = slice(HD * n, HD * n + HD)
                        sp.dma_start(s.k_stack[rows, 0, :], s.k_rows[K_PART[n], bass.ds(j, 1)].rearrange("a p n -> p (a n)"))\
                          .then_inc(loaded.sem, 16)
                        sp.dma_start(q_stack[rows], s.q_rows[Q_PART[n], bass.ds(j * GROUP, GROUP)].rearrange("h p n -> p h n"))\
                          .then_inc(loaded.sem, 16)
                    sp.wait_ge(split.sem, split.after(j))
                    sp.dma_start(s.d_shift[:, bass.ds(j * GROUP, GROUP)].rearrange("r h (t n) -> (h t) r n", n=P), parts[:])\
                      .then_inc(stored.sem, 16)
                sp.wait_ge(stored.sem, stored.after(PAIRS - 1))
            with sp.Else():
                pass

        @block.tensor
        def _(pe):
            with pe.If(pe.value_load(s.loose[:], min_val=0, max_val=1) > 0):
                scored.open(pe)
                flipped.open(pe)
                with pe.Fori(0, PAIRS) as j:
                    pe.wait_ge(loaded.sem, loaded.after(j))
                    for n, (h, t) in enumerate(jobs):
                        pe.wait_ge(taken.sem, taken.after(j * len(jobs) + n - 1))
                        keys = P * (t + 1)
                        for at in range(0, keys, BLOCK):
                            width = min(BLOCK, keys - at)
                            last = nc.tensor.matmul(scores[:, at:at + width], q_stack[:, h, P * t:P * t + P],
                                                    s.k_stack[0:STACK, 0, at:at + width], start=True, stop=True)
                        last.then_inc(scored.sem, 1)
                    pe.wait_ge(joined.sem, joined.after(j))
                    pe.wait_ge(split.sem, split.after(j - 1))
                    apart(pe, s)
                    nc.tensor.transpose(turned[:], least[:], s.ident[:]).then_inc(flipped.sem, 1)
            with pe.Else():
                pass

        @block.vector
        def _(dve):
            with dve.If(dve.value_load(s.loose[:], min_val=0, max_val=1) > 0):
                for made in (masked_done, taken, joined, split):
                    made.open(dve)
                dve.wait_ge(filled, 2)
                dve.memset(found[:], FAR).then_inc(filled, 1)
                dve.wait_ge(filled, 3)
                with dve.Fori(0, PAIRS) as j:
                    for n, (h, t) in enumerate(jobs):
                        job = j * len(jobs) + n
                        own = P * t
                        dve.wait_ge(scored.sem, scored.after(job))
                        dve.wait_ge(taken.sem, taken.after(job - 1))
                        dve.tensor_tensor(masked[:], scores[:, own:own + P], ahead[:], ALU.add).then_inc(masked_done.sem, 1)
                        dve.wait_ge(masked_done.sem, masked_done.after(job))
                        if t:
                            dve.tensor_reduce(found[:, 1, h, t:t + 1], scores[:, 0:own], AX.X, ALU.max)
                        dve.tensor_reduce(found[:, 0, h, t:t + 1], masked[:], AX.X, ALU.max).then_inc(taken.sem, 1)
                    dve.wait_ge(taken.sem, taken.after(j * len(jobs) + len(jobs) - 1))
                    dve.wait_ge(flipped.sem, flipped.after(j - 1))
                    dve.tensor_tensor(least[:], found[:, 0].rearrange("p h t -> p (h t)"), found[:, 1].rearrange("p h t -> p (h t)"), ALU.max)\
                       .then_inc(joined.sem, 1)
                    dve.wait_ge(joined.sem, joined.after(j - 1) + 1)
                    dve.tensor_scalar(least[:], least[:], -1.0, None, ALU.mult).then_inc(joined.sem, 1)
                    dve.wait_ge(flipped.sem, flipped.after(j))
                    dve.wait_ge(stored.sem, stored.after(j - 1))
                    dve.tensor_copy(parts[:, 0], turned[:]).then_inc(split.sem, 1)
                    dve.wait_ge(split.sem, split.after(j - 1) + 1)
                    dve.tensor_tensor(rest[:], turned[:], parts[:, 0], ALU.subtract).then_inc(split.sem, 1)
                    dve.wait_ge(split.sem, split.after(j - 1) + 2)
                    dve.tensor_copy(parts[:, 1], rest[:]).then_inc(split.sem, 1)
            with dve.Else():
                pass


def attend(nc, s):
    PAIRS = BATCH * KV
    chunks = [(t, c) for t in reversed(range(BLOCKS_B)) for c in range(BT * t + BT)]
    PER_PAIR = len(chunks)
    BODY = 2 * PER_PAIR
    UNITS = 2 * BODY
    diagonal = {}
    for n in range(BODY):
        t, c = chunks[n % PER_PAIR]
        if c >= BT * t:
            diagonal[n] = len(diagonal)
    DIAGONALS = len(diagonal)
    with ExitStack() as ctx:
        def sb(name, shape, dt=fp32):
            return ctx.enter_context(nc.sbuf_tensor(name, shape, dt))

        def steps(name, per=1, lead=2):
            return Steps(ctx.enter_context(nc.semaphore(name)), per, lead)

        q_stack = sb("q_stack", [P, 2, GROUP, SEQ], bf16)
        values = sb("values", [P, 2, TILES_B, 2 * HD])
        probs = sb("probs", [P, 4, 2, BLOCK])
        den = sb("den", [P, 2, BLOCK])
        o_n = sb("o_n", [P, 2, BLOCK])
        scores = ctx.enter_context(nc.psum_tensor("scores", [P, 3, 2, BLOCK], fp32))
        sums = ctx.enter_context(nc.psum_tensor("sums", [P, 2, BLOCK], fp32))

        loaded = [steps(f"pair_loaded_{u}", 16 * (2 * SLOTS + 2)) for u in range(2)]
        scored, exped = steps("scored"), steps("exped", lead=4)
        masked, summed = steps("masked"), steps("summed", lead=BODY)
        divided = steps("divided", 3)
        a_out = [steps(f"a_out_{u}", 16 * GROUP) for u in range(2)]
        block = ctx.enter_context(nc.Block())

        def body():
            for u in range(2):
                for k, (t, c) in enumerate(chunks):
                    yield u * PER_PAIR + k, u, t, c, P * max(0, c - BT * t)

        @block.sync
        def _(sp):
            for made in (*loaded, *a_out):
                made.open(sp)

            def store(i, u):
                for t in reversed(range(BLOCKS_B)):
                    sp.wait_ge(divided.sem, divided.after(i * 2 * BLOCKS_B + u * BLOCKS_B + (BLOCKS_B - 1 - t)))
                    apart(sp, s)
                    for h in range(GROUP):
                        sp.dma_start(s.a_rows[bass.ds(i * 2 + u, 1), h, :, BLOCK * t:BLOCK * t + BLOCK].rearrange("a p n -> p (a n)"),
                                     o_n[2 * HD * h:2 * HD * h + HD, t % 2]).then_inc(a_out[t % 2].sem, 16)

            def load(i, u):
                j = i * 2 + u
                sp.wait_ge(summed.sem, summed.after(i * BODY + (u - 1) * PER_PAIR - 1))
                for n in range(SLOTS):
                    rows = slice(HD * n, HD * n + HD)
                    sp.dma_start(s.k_stack[rows, u, :], s.k_rows[K_PART[n], bass.ds(j, 1)].rearrange("a p n -> p (a n)"))\
                      .then_inc(loaded[u].sem, 16)
                    sp.dma_start(q_stack[rows, u], s.q_rows[Q_PART[n], bass.ds(j * GROUP, GROUP)].rearrange("h p n -> p h n"))\
                      .then_inc(loaded[u].sem, 16)
                sp.dma_start(q_stack[STACK:ROWS, u], s.d_shift[:, bass.ds(j * GROUP, GROUP), :]).then_inc(loaded[u].sem, 16)
                sp.dma_start(values[:, u], s.v_all[:, bass.ds(j, 1)].rearrange("p a t d -> p (a t) d"))\
                  .then_inc(loaded[u].sem, 16)

            load(0, 0)
            with sp.Fori(0, PAIRS // 2 - 1) as i:
                load(i, 1)
                store(i, 0)
                load(i + 1, 0)
                store(i, 1)
            load(PAIRS // 2 - 1, 1)
            store(PAIRS // 2 - 1, 0)
            store(PAIRS // 2 - 1, 1)
            for u in range(2):
                sp.wait_ge(a_out[u].sem, a_out[u].after(PAIRS * BLOCKS_B // 2 - 1))

        @block.tensor
        def _(pe):
            summed.open(pe)
            scored.open(pe)

            def score(i, n, u, t, c, n0):
                if n % PER_PAIR == 0:
                    pe.wait_ge(loaded[u].sem, loaded[u].after(i))
                for half in range(2):
                    e = 2 * n + half
                    before = e - 3 if e >= 3 else max(x for x in range(UNITS - 3, UNITS) if x % 3 == e) - UNITS
                    pe.wait_ge(exped.sem, exped.after(i * UNITS + before))
                    for h in range(2):
                        last = nc.tensor.matmul(scores[:, e % 3, h, n0:], s.k_stack[0:ROWS, u, P * c:P * c + P],
                                                q_stack[0:ROWS, u, 2 * half + h, BLOCK * t + n0:BLOCK * t + BLOCK],
                                                start=True, stop=True)
                    last.then_inc(scored.sem, 1)

            def weigh(i, n, u, t, c, n0):
                pe.wait_ge(exped.sem, exped.after(i * UNITS + 2 * n + 1))
                if c >= BT * t:
                    pe.wait_ge(masked.sem, masked.after(i * DIAGONALS + diagonal[n]))
                if c == 0:
                    pe.wait_ge(divided.sem, divided.after(i * 2 * BLOCKS_B + u * BLOCKS_B + (BLOCKS_B - 1 - t) - 2))
                for h in range(GROUP):
                    last = nc.tensor.matmul(sums[2 * HD * h:2 * HD * h + 2 * HD, t % 2, n0:], values[:, u, c, :],
                                            probs[:, (2 * n + h // 2) % 4, h % 2, n0:],
                                            start=(c == 0), stop=(c == BT * t + BT - 1), tile_position=(0, 2 * HD * h))
                last.then_inc(summed.sem, 1)

            with pe.Fori(0, PAIRS // 2) as i:
                before = None
                for chunk in body():
                    score(i, *chunk)
                    if before:
                        weigh(i, *before)
                    before = chunk
                weigh(i, *before)

        @block.scalar
        def _(act):
            exped.open(act)
            with act.Fori(0, PAIRS // 2) as i:
                for n, u, t, c, n0 in body():
                    act.wait_ge(summed.sem, summed.after(i * BODY + n - 2))
                    for e in (2 * n, 2 * n + 1):
                        act.wait_ge(scored.sem, scored.after(i * UNITS + e))
                        act.activation(probs[:, e % 4, :, n0:], scores[:, e % 3, :, n0:], ACT.Exp, scale=A_SCALE)\
                           .then_inc(exped.sem, 1)

        @block.gpsimd
        def _(pool):
            masked.open(pool)
            with pool.Fori(0, PAIRS // 2) as i:
                for n, u, t, c, n0 in body():
                    if c < BT * t:
                        continue
                    for e in (2 * n, 2 * n + 1):
                        pool.wait_ge(exped.sem, exped.after(i * UNITS + e))
                        own = probs[:, e % 4, :, n0:n0 + P]
                        apart(pool, s)
                        last = pool.affine_select(out=own, in_=own, compare_op=ALU.is_ge, fill=0.0, base=0,
                                                  pattern=[[0, 2], [1, P]], channel_multiplier=-1)
                    last.then_inc(masked.sem, 1)

        @block.vector
        def _(dve):
            divided.open(dve)
            spread = [HD + r % HD for r in range(2 * HD)]
            with dve.Fori(0, PAIRS // 2) as i:
                for n, u, t, c, n0 in body():
                    if c < BT * t + BT - 1:
                        continue
                    tile = i * 2 * BLOCKS_B + u * BLOCKS_B + (BLOCKS_B - 1 - t)
                    dve.wait_ge(summed.sem, summed.after(i * BODY + n))
                    apart(dve, s)
                    dve.stream_shuffle(den[:, 0], sums[:, t % 2], spread).then_inc(divided.sem, 1)
                    dve.wait_ge(divided.sem, divided.after(tile - 1) + 1)
                    dve.reciprocal(den[:, 1], den[:, 0]).then_inc(divided.sem, 1)
                    dve.wait_ge(divided.sem, divided.after(tile - 1) + 2)
                    dve.wait_ge(a_out[t % 2].sem, a_out[t % 2].after(i * BLOCKS_B + (u * BLOCKS_B + BLOCKS_B - 1 - t) // 2 - 1))
                    dve.tensor_tensor(o_n[:, t % 2], sums[:, t % 2], den[:, 1], ALU.mult).then_inc(divided.sem, 1)



def transpose_weights(nc, s):
    jobs = [(source, target, source.shape[0] // P, source.shape[1] // P) for source, target in (
        (s.d_wqkv, s.w_qkv_t), (s.d_wq_h, s.wq_h_t), (s.d_wkv_h, s.wkv_h_t),
        (s.d_wout_l, s.wout_l_t), (s.d_wout_h, s.wout_h_t))]
    rows = sum(n for _, _, n, _ in jobs)
    with nc.sbuf_tensor("w_rows", [P, rows, 4 * P], fp32) as w_rows, \
            nc.psum_tensor("w_turned", [P, 2, 4, P], fp32) as w_turned, \
            nc.semaphore("w_loaded") as loaded, nc.semaphore("w_turned_done") as turned, \
            nc.semaphore("w_copied") as copied, nc.Block() as block:
        turns, at = [], 0
        for source, target, n, m in jobs:
            for r in range(n):
                turns.append((at, target, r, m))
                at += 1

        @block.sync
        def _(sp):
            at = 0
            for source, _, n, m in jobs:
                sp.dma_start(w_rows[:, at:at + n, 0:m * P], source.rearrange("(r p) n -> p r n", p=P)).then_inc(loaded, 16)
                at += n

        @block.tensor
        def _(pe):
            pe.wait_ge(loaded, 16 * len(jobs))
            for k, (at, _, r, m) in enumerate(turns):
                if k >= 2:
                    pe.wait_ge(copied, k - 1)
                for c in range(m):
                    last = nc.tensor.transpose(w_turned[:, k % 2, c], w_rows[:, at, P * c:P * c + P], s.ident[:])
                last.then_inc(turned, 1)

        @block.vector
        def _(dve):
            for k, (_, target, r, m) in enumerate(turns):
                dve.wait_ge(turned, k + 1)
                if target is s.wkv_h_t:
                    dve.tensor_copy(target[:, :, :, r], w_turned[:, k % 2, 0:m].rearrange("p c (a d) -> p c a d", a=2)).then_inc(copied, 1)
                else:
                    dve.tensor_copy(target[:, :, P * r:P * r + P], w_turned[:, k % 2, 0:m]).then_inc(copied, 1)


def normalise_tiles(dve, out, mean_var, inv, x):
    for t in range(BT):
        last = dve.tensor_scalar(out[:, t], x[:, t], mean_var[:, t, 0:1], inv[:, t:t + 1], ALU.subtract, ALU.mult)
    return last


def merge(nc, s):
    with ExitStack() as ctx:
        def sb(name, shape, dt=fp32):
            return ctx.enter_context(nc.sbuf_tensor(name, shape, dt))

        def steps(name, per=1, lead=4):
            return Steps(ctx.enter_context(nc.semaphore(name)), per, lead)

        a_t = sb("a_t", [P, BLOCKS_B, HALVES, BLOCK])
        x_in = sb("x_in2", [P, BLOCKS_B, BT, DIM])
        y = sb("y", [P, BT, DIM])
        x_1 = sb("x_1", [P, 2, BT, DIM])
        h_n = sb("h_n", [P, 2, BT, DIM])
        u_n = sb("u_n", [P, BT, DIM])
        u_t = sb("u_turned", [P, 2, HALVES, BLOCK])
        stats = sb("stats2", [P, 3, BT, 6])
        mean_var = sb("mean_var2", [P, 3, BT, 2])
        inv, shift = sb("inv2", [P, 3, BT]), sb("u_shift", [P, BT])
        scratch, block_s = sb("route_product", [P, BT, 2, DIM]), sb("block_s", [P, 2, BT])
        w_o, b_o, one = sb("w_o", [P, HALVES, DIM]), sb("b_o", [1, DIM]), sb("one", [1, P])
        ln_w, ln_b = sb("ln_w", [P, HALVES]), sb("ln_b", [P, HALVES])
        rt = sb("rt", [P, 2, DIM])
        p_y = ctx.enter_context(nc.psum_tensor("p_y", [P, 2, BT, DIM], fp32))
        p_u = ctx.enter_context(nc.psum_tensor("p_u", [P, HALVES, BLOCK], fp32))

        w_loaded = ctx.enter_context(nc.semaphore("merge_weights"))
        one_made = ctx.enter_context(nc.semaphore("one_made"))
        loaded = [steps(f"block_loaded_{c}", 32) for c in range(BLOCKS_B)]
        x1_out = [steps(f"x1_out_{u}", 32) for u in range(2)]
        u_out = [steps(f"u_out_{u}", 16) for u in range(2)]
        y_stats = steps("y_stats", 2)
        x1_made = steps("x1_made", 4)
        h_made = steps("h_made", 3)
        multiplied, routed = steps("multiplied"), steps("routed")
        y_root, x1_root, h_root = steps("y_root", 2), steps("x1_root", 2), steps("h_root", 4)
        projected, turned, u_made, u_ready = steps("o_projected"), steps("u_turned_done"), steps("u_made"), steps("u_ready")
        block = ctx.enter_context(nc.Block())

        @block.sync
        def _(sp):
            for m in (*loaded, *x1_out, *u_out):
                m.open(sp)
            sp.dma_start(w_o[:], s.d_w_o.rearrange("(k p) n -> p k n", p=P)).then_inc(w_loaded, 16)
            sp.dma_start(b_o[:], s.d_b_o.rearrange("(a n) -> a n", a=1)).then_inc(w_loaded, 16)
            sp.dma_start(rt[:, 0], s.d_rt_q.broadcast_to([P, DIM])).then_inc(w_loaded, 16)
            sp.dma_start(rt[:, 1], s.d_rt_kv.broadcast_to([P, DIM])).then_inc(w_loaded, 16)
            sp.dma_start(ln_w[:], s.d_ln_w.rearrange("(k p) -> p k", p=P), allow_slow_non_contiguous=True).then_inc(w_loaded, 16)
            sp.dma_start(ln_b[:], s.d_ln_b.rearrange("(k p) -> p k", p=P), allow_slow_non_contiguous=True).then_inc(w_loaded, 16)

            def load(b, c):
                g = b * BLOCKS_B + c
                sp.wait_ge(projected.sem, projected.after(g - BLOCKS_B))
                apart(sp, s)
                sp.wait_ge(x1_made.sem, x1_made.after(g - BLOCKS_B))
                sp.dma_start(a_t[:, c], s.d_attended[bass.ds(b * HALVES, HALVES), :, BLOCK * c:BLOCK * c + BLOCK]
                             .rearrange("k p n -> p k n")).then_inc(loaded[c].sem, 16)
                sp.dma_start(x_in[:, c], s.d_x[bass.ds(b * TILES_B + BT * c, BT)].rearrange("t p d -> p t d"))\
                  .then_inc(loaded[c].sem, 16)

            def before():
                for c in range(3):
                    load(0, c)

            def turn(b, c, has):
                g, u = b * BLOCKS_B + c, c % 2
                if has(3):
                    load(*block_at(b, c, 3))
                tiles = bass.ds(b * TILES_B + BT * c, BT)
                sp.wait_ge(h_made.sem, h_made.after(g - 1) + 1)
                apart(sp, s)
                sp.dma_start(s.d_x1[tiles].rearrange("t p d -> p t d"), x_1[:, u]).then_inc(x1_out[u].sem, 16)
                sp.dma_start(s.d_h[tiles].rearrange("t p d -> p t d"), h_n[:, u]).then_inc(x1_out[u].sem, 16)
                sp.wait_ge(u_ready.sem, u_ready.after(g))
                apart(sp, s)
                sp.dma_start(s.d_u_t[:, :, bass.ds(b * SEQ + BLOCK * c, BLOCK)], u_t[:, u]).then_inc(u_out[u].sem, 16)

            over_blocks(sp, before, turn)
            for u in range(2):
                sp.wait_ge(x1_out[u].sem, x1_out[u].after(BATCH * BLOCKS_B // 2 - 1))
                sp.wait_ge(u_out[u].sem, u_out[u].after(BATCH * BLOCKS_B // 2 - 1))

        @block.tensor
        def _(pe):
            projected.open(pe)
            turned.open(pe)
            pe.wait_ge(w_loaded, 6 * 16)
            pe.wait_ge(one_made, 1)

            def out_projection(b, c):
                g, u = b * BLOCKS_B + c, c % 2
                pe.wait_ge(loaded[c].sem, loaded[c].after(b))
                pe.wait_ge(x1_made.sem, x1_made.after(g - 3) + 1)
                for t in range(BT):
                    for k in range(HALVES):
                        nc.tensor.matmul(p_y[:, u, t], a_t[:, c, k, P * t:P * t + P], w_o[:, k], start=(k == 0), stop=False)
                    last = nc.tensor.matmul(p_y[:, u, t], one[:], b_o[:], start=False, stop=True)
                last.then_inc(projected.sem, 1)

            def before():
                out_projection(0, 0)
                out_projection(0, 1)

            def turn(b, c, has):
                g = b * BLOCKS_B + c
                if has(2):
                    out_projection(*block_at(b, c, 2))
                pe.wait_ge(u_made.sem, u_made.after(g))
                pe.wait_ge(u_ready.sem, u_ready.after(g - 1))
                for t in range(BT):
                    for k in range(HALVES):
                        last = nc.tensor.transpose(p_u[:, k, P * t:P * t + P], u_n[:, t, P * k:P * k + P], s.ident[:])
                last.then_inc(turned.sem, 1)

            over_blocks(pe, before, turn)

        @block.scalar
        def _(act):
            u_made.open(act)
            u_ready.open(act)
            act.wait_ge(w_loaded, 6 * 16)

            def turn(b, c, has):
                g, u, v = b * BLOCKS_B + c, c % 2, b * (BLOCKS_B // 2) + c // 2
                act.wait_ge(h_root.sem, h_root.after(g))
                act.wait_ge(turned.sem, turned.after(g - 1))
                for t in range(BT):
                    last = act.activation(u_n[:, t], h_n[:, u, t], ACT.Identity, scale=inv[:, 2, t:t + 1], bias=shift[:, t:t + 1])
                last.then_inc(u_made.sem, 1)
                act.wait_ge(turned.sem, turned.after(g))
                act.wait_ge(u_out[u].sem, u_out[u].after(v - 1))
                for k in range(HALVES):
                    last = act.activation(u_t[:, u, k], p_u[:, k], ACT.Identity, scale=ln_w[:, k:k + 1], bias=ln_b[:, k:k + 1])
                last.then_inc(u_ready.sem, 1)

            over_blocks(act, lambda: None, turn)

        @block.gpsimd
        def _(pool):
            for made in (y_root, x1_root, h_root):
                made.open(pool)
            pool.memset(one[:], 1.0).then_inc(one_made, 1)

            def y_inverse(b, c):
                g = b * BLOCKS_B + c
                pool.wait_ge(y_stats.sem, y_stats.after(g))
                inverse_root(pool, s, inv[:, 0], mean_var[:, 0, :, 1], s.power[:, 0:BT], y_root, g)

            def x1_inverse(b, c):
                g = b * BLOCKS_B + c
                pool.wait_ge(x1_made.sem, x1_made.after(g))
                inverse_root(pool, s, inv[:, 1], mean_var[:, 1, :, 1], s.power[:, 0:BT], x1_root, g)

            def h_inverse(b, c):
                g = b * BLOCKS_B + c
                pool.wait_ge(h_made.sem, h_made.after(g))
                pool.wait_ge(u_made.sem, u_made.after(g - 1))
                apart(pool, s)
                pool.tensor_scalar(inv[:, 2], mean_var[:, 2, :, 1], EPS, None, ALU.add).then_inc(h_root.sem, 1)
                pool.wait_ge(h_root.sem, h_root.after(g - 1) + 1)
                pool.tensor_tensor(inv[:, 2], inv[:, 2], s.power[:, 0:BT], ALU.pow).then_inc(h_root.sem, 1)
                pool.wait_ge(h_root.sem, h_root.after(g - 1) + 2)
                pool.tensor_tensor(shift[:], mean_var[:, 2, :, 0], inv[:, 2], ALU.mult).then_inc(h_root.sem, 1)
                pool.wait_ge(h_root.sem, h_root.after(g - 1) + 3)
                apart(pool, s)
                pool.tensor_scalar(shift[:], shift[:], -1.0, None, ALU.mult).then_inc(h_root.sem, 1)

            def before():
                y_inverse(0, 0)
                x1_inverse(0, 0)

            def turn(b, c, has):
                if has(1):
                    y_inverse(*block_at(b, c, 1))
                h_inverse(b, c)
                if has(1):
                    x1_inverse(*block_at(b, c, 1))

            over_blocks(pool, before, turn)

        @block.vector
        def _(dve):
            for made in (y_stats, x1_made, h_made, multiplied, routed):
                made.open(dve)
            dve.wait_ge(w_loaded, 6 * 16)

            def statistics(x, n, chain, base):
                dve.wait_ge(chain.sem, base)
                for t in range(BT):
                    last = dve.bn_stats(stats[:, n, t], x[:, t])
                last.then_inc(chain.sem, 1)
                dve.wait_ge(chain.sem, base + 1)
                apart(dve, s)
                for t in range(BT):
                    last = dve.bn_aggr(mean_var[:, n, t], stats[:, n, t])
                last.then_inc(chain.sem, 1)

            def take_y(b, c):
                g, u = b * BLOCKS_B + c, c % 2
                dve.wait_ge(projected.sem, projected.after(g))
                statistics(p_y[:, u], 0, y_stats, y_stats.after(g - 1))

            def make_x1(b, c):
                g, u, v = b * BLOCKS_B + c, c % 2, b * (BLOCKS_B // 2) + c // 2
                base = x1_made.after(g - 1)
                dve.wait_ge(y_root.sem, y_root.after(g))
                normalise_tiles(dve, y, mean_var[:, 0], inv[:, 0], p_y[:, u]).then_inc(x1_made.sem, 1)
                dve.wait_ge(x1_out[u].sem, x1_out[u].after(v - 1))
                dve.wait_ge(loaded[c].sem, loaded[c].after(b))
                dve.wait_ge(x1_made.sem, base + 1)
                dve.tensor_tensor(x_1[:, u], x_in[:, c], y[:], ALU.add).then_inc(x1_made.sem, 1)
                statistics(x_1[:, u], 1, x1_made, base + 2)

            def make_h(b, c):
                g, u = b * BLOCKS_B + c, c % 2
                dve.wait_ge(x1_root.sem, x1_root.after(g))
                dve.wait_ge(u_made.sem, u_made.after(g - 2))
                normalise_tiles(dve, h_n[:, u], mean_var[:, 1], inv[:, 1], x_1[:, u]).then_inc(h_made.sem, 1)
                dve.wait_ge(h_root.sem, h_root.after(g - 1))
                statistics(h_n[:, u], 2, h_made, h_made.after(g - 1) + 1)

            def route_products(b, c):
                g, u = b * BLOCKS_B + c, c % 2
                dve.wait_ge(routed.sem, routed.after(g - 1))
                for t in range(BT):
                    for r in range(2):
                        last = dve.tensor_tensor_reduce(out=scratch[:, t, r], in0=h_n[:, u, t], in1=rt[:, r], scale=1.0, scalar=0.0,
                                                        op0=ALU.mult, op1=ALU.add, accum_out=block_s[:, r, t:t + 1])
                last.then_inc(multiplied.sem, 1)
                dve.wait_ge(multiplied.sem, multiplied.after(g))
                dve.tensor_copy(s.route_s[:, :, bass.ds(g * BT, BT)], block_s[:]).then_inc(routed.sem, 1)

            def before():
                take_y(0, 0)
                make_x1(0, 0)

            def turn(b, c, has):
                if has(1):
                    take_y(*block_at(b, c, 1))
                make_h(b, c)
                if has(1):
                    make_x1(*block_at(b, c, 1))
                route_products(b, c)

            over_blocks(dve, before, turn)
            dve.wait_ge(routed.sem, routed.after(BATCH * BLOCKS_B - 1))


WINDOW, L_HEADS, L_HD = 64, 8, 64
L_INNER = L_HEADS * L_HD
L_SCALE = L_HD ** -0.5
PAIR_CHUNKS = L_INNER // P
HALF_HEADS = L_HEADS // 2
OUTSIDE = -1e30


def local(nc, s):
    with ExitStack() as ctx:
        def sb(name, shape, dt=fp32):
            return ctx.enter_context(nc.sbuf_tensor(name, shape, dt))

        def ps(name, shape):
            return ctx.enter_context(nc.psum_tensor(name, shape, fp32))

        def steps(name, per=1, lead=4):
            return Steps(ctx.enter_context(nc.semaphore(name)), per, lead)

        SLOTS4 = 4
        EVEN, ODD = slice(0, WINDOW), slice(WINDOW, P)
        u_in = sb("u_in", [P, SLOTS4, HALVES, P])
        x1_in = sb("x1_in", [P, SLOTS4, DIM])
        q_pad = sb("q_pad", [P, SLOTS4, L_HEADS, P])
        k_window = sb("k_window", [P, SLOTS4, PAIR_CHUNKS, 2 * P])
        v_main = sb("v_main", [P, SLOTS4, L_HEADS, L_HD])
        v_side = sb("v_side", [P, SLOTS4, L_HEADS, L_HD])
        edge = sb("edge", [P, TILES])
        m_main, m_side = sb("m_main", [P, HALF_HEADS]), sb("m_side", [P, HALF_HEADS])
        m_all, m_edge = sb("m_all", [P, HALF_HEADS]), sb("m_edge", [P, HALF_HEADS])
        z = sb("z", [P, 2, HALF_HEADS, 2 * P])
        probs = sb("l_probs", [P, 2, HALF_HEADS, 2 * P])
        probs_t = sb("probs_t", [P, 2, HALF_HEADS, 2, P])
        den, share = sb("l_den", [P, 2, HALF_HEADS]), sb("l_share", [P, 2, HALF_HEADS])
        diagonal = sb("diagonal", [P, 2, HALF_HEADS, P])
        o_t = sb("o_t", [P, PAIR_CHUNKS, P])
        light = sb("light_rows", [P, 2, DIM])
        y = sb("l_y", [P, DIM])
        stats, mean_var, inv = sb("stats3", [P, 6]), sb("mean_var3", [P, 2]), sb("inv3", [P, 1])
        rows = sb("out_rows", [P, 2, DIM])
        null_q = sb("null_q", [P, DIM])
        p_q, p_k, p_v = ps("p_q3", [P, BLOCK]), ps("p_k3", [P, BLOCK]), ps("p_v3", [P, BLOCK])
        p_s = ps("p_s", [P, HALF_HEADS, 2 * P])
        p_p = ps("p_p", [P, HALF_HEADS, 2, P])
        p_o = ps("p_o", [P, PAIR_CHUNKS, P])
        p_y = p_v[:, 0:DIM]

        filled = ctx.enter_context(nc.semaphore("l_filled"))
        null_loaded = ctx.enter_context(nc.semaphore("null_loaded"))
        u_loaded = [steps(f"u_loaded_{k}", 16, 1) for k in range(SLOTS4)]
        x1_loaded = [steps(f"x1_loaded_{k}", 16, 1) for k in range(SLOTS4)]
        light_out = [steps(f"light_out_{k}", 16, 1) for k in range(2)]
        out_out = [steps(f"out_out_{k}", 16, 1) for k in range(2)]
        qk_done, v_done = steps("qk_done"), steps("v_done")
        q_ready, k_main, k_sides = steps("q_ready"), steps("k_main"), steps("k_sides")
        v_ready, v_sides = steps("v_main_ready"), steps("v_sides_ready")
        scored, z_ready, exped = steps("l_scored"), steps("z_ready"), steps("l_exped")
        diagonal_ready, p_turned, p_ready, summed = steps("diagonal_ready"), steps("p_turned"), steps("p_ready"), steps("l_summed", lead=8)
        o_t_ready, y_done, light_ready = steps("o_t_ready"), steps("y_done"), steps("light_ready")
        G_STEPS, F_STEPS = 4, 4
        g_chain = steps("g_chain", G_STEPS)
        f_chain = steps("f_chain", F_STEPS)
        inverted, rows_ready = steps("inverted3", 2), steps("rows_ready")
        r_chain = steps("r_chain")
        FILLS = 8
        block = ctx.enter_context(nc.Block())
        TURNS = TILES // SLOTS4

        def at(i, k, by):
            return i + (k + by) // SLOTS4, (k + by) % SLOTS4

        def loop(eng, before, turn, after):
            before()
            for k in range(SLOTS4):
                turn(0, k, lambda by, k=k: k + by >= 0)
            with eng.Fori(1, TURNS - 1) as i:
                for k in range(SLOTS4):
                    turn(i, k, lambda by: True)
            for k in range(SLOTS4):
                turn(TURNS - 1, k, lambda by, k=k: k + by < SLOTS4)
            after(*at(TURNS, 0, 0))

        @block.sync
        def _(sp):
            for made in (*u_loaded, *x1_loaded, *light_out, *out_out):
                made.open(sp)
            sp.dma_start(null_q[:], s.d_null_q.rearrange("(a n) -> a n", a=1).broadcast_to([P, DIM])).then_inc(null_loaded, 16)

            def load_u(i, k):
                n = i * SLOTS4 + k
                sp.wait_ge(v_done.sem, v_done.after(n - SLOTS4))
                sp.dma_start(u_in[:, k], s.d_u_t[:, :, bass.ds(n * P, P)]).then_inc(u_loaded[k].sem, 16)

            def load_x1(i, k):
                n = i * SLOTS4 + k
                sp.wait_ge(rows_ready.sem, rows_ready.after(n - SLOTS4))
                sp.dma_start(x1_in[:, k], s.d_x1[bass.ds(n, 1)].rearrange("a p d -> p (a d)")).then_inc(x1_loaded[k].sem, 16)

            def store(i, k):
                m = i * SLOTS4 + k
                sp.wait_ge(light_ready.sem, light_ready.after(m))
                sp.dma_start(s.d_light[bass.ds(m, 1)].rearrange("a p d -> p (a d)"), light[:, k % 2]).then_inc(light_out[k % 2].sem, 16)
                sp.wait_ge(rows_ready.sem, rows_ready.after(m))
                sp.dma_start(s.d_out[bass.ds(m, 1)].rearrange("a p d -> p (a d)"), rows[:, k % 2]).then_inc(out_out[k % 2].sem, 16)

            def turn(i, k, has):
                if has(3):
                    load_u(*at(i, k, 3))
                if has(1):
                    load_x1(*at(i, k, 1))
                if has(-1):
                    store(*at(i, k, -1))

            def before():
                for k in range(3):
                    load_u(0, k)
                load_x1(0, 0)

            def after(i, k):
                store(*at(i, k, -1))
                for k in range(2):
                    sp.wait_ge(light_out[k].sem, light_out[k].after(TILES // 2 - 1))
                    sp.wait_ge(out_out[k].sem, out_out[k].after(TILES // 2 - 1))

            loop(sp, before, turn, after)

        @block.tensor
        def _(pe):
            for made in (qk_done, v_done, scored, p_turned, summed, y_done):
                made.open(pe)
            pe.wait_ge(filled, FILLS)

            def project_qk(i, k):
                n = i * SLOTS4 + k
                pe.wait_ge(u_loaded[k].sem, u_loaded[k].after(i))
                pe.wait_ge(q_ready.sem, q_ready.after(n - 1))
                pe.wait_ge(k_main.sem, k_main.after(n - 1))
                for out, first in ((p_q, 0), (p_k, L_INNER)):
                    for c in range(PAIR_CHUNKS):
                        for h in range(HALVES):
                            last = nc.tensor.matmul(out[:, P * c:P * c + P], s.w_qkv_t[:, h, first + P * c:first + P * c + P],
                                                    u_in[:, k, h], start=(h == 0), stop=(h == HALVES - 1))
                last.then_inc(qk_done.sem, 1)

            def project_v(i, k):
                n = i * SLOTS4 + k
                pe.wait_ge(v_ready.sem, v_ready.after(n - 1))
                pe.wait_ge(v_sides.sem, v_sides.after(n - 1))
                pe.wait_ge(light_ready.sem, light_ready.after(n - 3))
                for h in range(HALVES):
                    last = nc.tensor.matmul(p_v[:], u_in[:, k, h], s.w_qkv_t[:, h, 2 * L_INNER:],
                                            start=(h == 0), stop=(h == HALVES - 1))
                last.then_inc(v_done.sem, 1)

            def score(i, k, g, behind):
                m = i * SLOTS4 + k
                e = 2 * m + g
                pe.wait_ge(q_ready.sem, q_ready.after(m))
                pe.wait_ge(k_sides.sem, k_sides.after(m + 1 if behind else m))
                pe.wait_ge(z_ready.sem, z_ready.after(e - 1))
                for j in range(HALF_HEADS):
                    h = g * HALF_HEADS + j
                    last = nc.tensor.matmul(p_s[:, j], q_pad[:, k, h], k_window[:, k, h // 2], start=True, stop=True)
                last.then_inc(scored.sem, 1)

            def turn_probs(e, g):
                pe.wait_ge(diagonal_ready.sem, diagonal_ready.after(e))
                pe.wait_ge(p_ready.sem, p_ready.after(e - 1))
                for j in range(HALF_HEADS):
                    for side in range(2):
                        last = nc.tensor.matmul(p_p[:, j, side], probs[:, g, j, P * side:P * side + P], diagonal[:, g, j],
                                                start=True, stop=True)
                last.then_inc(p_turned.sem, 1)

            def weigh(e, k, g):
                pe.wait_ge(p_ready.sem, p_ready.after(e))
                apart(pe, s)
                for c in range(2):
                    for a in range(2):
                        j = 2 * c + a
                        h = g * HALF_HEADS + j
                        out = p_o[L_HD * a:L_HD * a + L_HD, 2 * g + c]
                        nc.tensor.matmul(out, v_main[:, k, h], probs_t[:, g, j, 0], start=True, stop=False, tile_position=(0, L_HD * a))
                        last = nc.tensor.matmul(out, v_side[:, k, h], probs_t[:, g, j, 1], start=False, stop=True,
                                                tile_position=(0, L_HD * a))
                last.then_inc(summed.sem, 1)

            def put_out(i, k):
                m = i * SLOTS4 + k
                pe.wait_ge(o_t_ready.sem, o_t_ready.after(m))
                newest = m + 2 if not isinstance(m, int) else min(m + 2, TILES - 1)
                pe.wait_ge(v_ready.sem, v_ready.after(newest))
                pe.wait_ge(v_sides.sem, v_sides.after(newest))
                for c in range(PAIR_CHUNKS):
                    last = nc.tensor.matmul(p_y, o_t[:, c], s.wout_l_t[:, c], start=(c == 0), stop=(c == PAIR_CHUNKS - 1))
                last.then_inc(y_done.sem, 1)

            def turn(i, k, has):
                m = i * SLOTS4 + k
                score(i, k, 1, has(1))
                if has(2):
                    project_qk(*at(i, k, 2))
                turn_probs(2 * m, 0)
                if has(-1):
                    put_out(*at(i, k, -1))
                pe.wait_ge(v_sides.sem, v_sides.after(m + 1 if has(1) else m))
                pe.wait_ge(o_t_ready.sem, o_t_ready.after(m - 1))
                weigh(2 * m, k, 0)
                if has(1):
                    score(*at(i, k, 1), 0, has(2))
                turn_probs(2 * m + 1, 1)
                if has(2):
                    project_v(*at(i, k, 2))
                weigh(2 * m + 1, k, 1)

            def before():
                for k in range(2):
                    project_qk(0, k)
                    project_v(0, k)
                score(0, 0, 0, True)

            def after(i, k):
                put_out(*at(i, k, -1))

            loop(pe, before, turn, after)

        @block.scalar
        def _(act):
            for made in (q_ready, k_main, v_sides, exped, p_ready, o_t_ready, light_ready):
                made.open(act)
            act.wait_ge(filled, FILLS)

            def take_qk(i, k):
                n = i * SLOTS4 + k
                act.wait_ge(qk_done.sem, qk_done.after(n))
                q = p_q[:].rearrange("p (c n) -> p c n", c=PAIR_CHUNKS)
                pairs = q_pad[:, k].rearrange("p (c a) n -> p c a n", a=2)
                act.activation(k_window[:, k, :, 0:P], p_k[:].rearrange("p (c n) -> p c n", c=PAIR_CHUNKS), ACT.Copy)\
                   .then_inc(k_main.sem, 1)
                act.activation(pairs[EVEN, :, 0], q[EVEN], ACT.Copy)
                act.activation(pairs[ODD, :, 1], q[ODD], ACT.Copy).then_inc(q_ready.sem, 1)

            def take_v_sides(i, k):
                act.wait_ge(v_ready.sem, v_ready.after(i * SLOTS4 + k))
                v = p_v[:].rearrange("p (h d) -> p h d", h=L_HEADS)
                act.activation(v_side[EVEN, (k - 1) % SLOTS4], v[EVEN], ACT.Copy)
                act.activation(v_side[ODD, (k + 1) % SLOTS4], v[ODD], ACT.Copy).then_inc(v_sides.sem, 1)

            def exps(e, g):
                act.wait_ge(z_ready.sem, z_ready.after(e))
                act.wait_ge(p_turned.sem, p_turned.after(e - 2))
                for j in range(HALF_HEADS):
                    last = act.activation(probs[:, g, j], z[:, g, j], ACT.Exp, scale=L_SCALE, accum_out=den[:, g, j:j + 1])
                last.then_inc(exped.sem, 1)

            def take_probs(e, g):
                act.wait_ge(p_turned.sem, p_turned.after(e))
                act.wait_ge(summed.sem, summed.after(e - 2))
                act.activation(probs_t[:, g], p_p[:], ACT.Copy).then_inc(p_ready.sem, 1)

            def take_light(i, k):
                m = i * SLOTS4 + k
                act.wait_ge(y_done.sem, y_done.after(m))
                act.wait_ge(light_out[k % 2].sem, light_out[k % 2].after(i * 2 + k // 2 - 1))
                act.wait_ge(f_chain.sem, f_chain.after(m - 2))
                act.activation(light[:, k % 2], p_y, ACT.Copy).then_inc(light_ready.sem, 1)

            def turn(i, k, has):
                m = i * SLOTS4 + k
                if has(2):
                    take_qk(*at(i, k, 2))
                take_probs(2 * m, 0)
                exps(2 * m + 1, 1)
                if has(-1):
                    take_light(*at(i, k, -1))
                take_probs(2 * m + 1, 1)
                if has(1):
                    exps(2 * m + 2, 0)
                if has(2):
                    take_v_sides(*at(i, k, 2))
                act.wait_ge(summed.sem, summed.after(2 * m + 1))
                act.wait_ge(y_done.sem, y_done.after(m - 1))
                act.activation(o_t[:], p_o[:], ACT.Copy).then_inc(o_t_ready.sem, 1)

            def before():
                for k in range(2):
                    take_qk(0, k)
                    take_v_sides(0, k)
                exps(0, 0)

            def after(i, k):
                take_light(*at(i, k, -1))

            loop(act, before, turn, after)

        @block.gpsimd
        def _(pool):
            for made in (k_sides, inverted, rows_ready):
                made.open(pool)
            pool.wait_ge(filled, FILLS)

            def sides(i, k):
                n, prior, following = i * SLOTS4 + k, (k - 1) % SLOTS4, (k + 1) % SLOTS4
                pool.wait_ge(k_main.sem, k_main.after(n))
                apart(pool, s)
                pool.tensor_copy(k_window[:, prior, :, P:P + WINDOW], k_window[:, k, :, 0:WINDOW])
                pool.tensor_copy(k_window[:, following, :, P + WINDOW:], k_window[:, k, :, WINDOW:P]).then_inc(k_sides.sem, 1)

            def finish(i, k):
                m = i * SLOTS4 + k
                pool.wait_ge(f_chain.sem, f_chain.after(m - 1) + 3)
                apart(pool, s)
                pool.tensor_scalar(inv[:], mean_var[:, 1:2], EPS, None, ALU.add).then_inc(inverted.sem, 1)
                pool.wait_ge(inverted.sem, inverted.after(m - 1) + 1)
                pool.tensor_tensor(inv[:], inv[:], s.power[:, 0:1], ALU.pow).then_inc(inverted.sem, 1)
                pool.wait_ge(f_chain.sem, f_chain.after(m))
                pool.wait_ge(x1_loaded[k].sem, x1_loaded[k].after(i))
                pool.wait_ge(out_out[k % 2].sem, out_out[k % 2].after(i * 2 + k // 2 - 1))
                pool.tensor_tensor(rows[:, k % 2], y[:], x1_in[:, k], ALU.add).then_inc(rows_ready.sem, 1)

            def turn(i, k, has):
                if has(2):
                    sides(*at(i, k, 2))
                if has(-1):
                    finish(*at(i, k, -1))

            def before():
                sides(0, 0)
                sides(0, 1)

            def after(i, k):
                finish(*at(i, k, -1))

            loop(pool, before, turn, after)

        @block.vector
        def _(dve):
            for made in (v_ready, z_ready, diagonal_ready, g_chain, f_chain, r_chain):
                made.open(dve)
            fills = [(q_pad[:], 0.0), (k_window[:], 0.0), (v_side[:], 0.0), (z[:], OUTSIDE), (edge[:], 0.0)]
            for out, value in fills:
                dve.memset(out, value).then_inc(filled, 1)
            dve.wait_ge(filled, len(fills))
            by_batch = edge[:].rearrange("p (b t) -> p b t", b=BATCH)
            dve.memset(by_batch[EVEN, :, 0:1], OUTSIDE).then_inc(filled, 1)
            dve.memset(by_batch[ODD, :, TILES_B - 1:TILES_B], OUTSIDE).then_inc(filled, 1)
            dve.wait_ge(null_loaded, 16)
            dve.sem_inc(filled, 1)
            dve.wait_ge(filled, FILLS)

            def take_v(i, k):
                n = i * SLOTS4 + k
                dve.wait_ge(v_done.sem, v_done.after(n))
                dve.wait_ge(summed.sem, summed.after(2 * (n - SLOTS4) + 1))
                dve.tensor_copy(v_main[:, k], p_v[:].rearrange("p (h d) -> p h d", h=L_HEADS)).then_inc(v_ready.sem, 1)

            def wide(x, rows, n):
                return x[rows].rearrange("p (h a) -> p h a", a=1).broadcast_to([rows.stop - rows.start, HALF_HEADS, n])

            def maxima(e, m, g):
                base = g_chain.after(e - 1)
                out_of = edge[:, bass.ds(m, 1)]
                dve.wait_ge(scored.sem, scored.after(e))
                dve.wait_ge(exped.sem, exped.after(e - 2))
                dve.wait_ge(z_ready.sem, z_ready.after(e - 1))
                dve.tensor_reduce(m_main[:], p_s[:, :, 0:P], AX.X, ALU.max)
                dve.tensor_reduce(m_side[EVEN], p_s[EVEN, :, P + WINDOW:], AX.X, ALU.max)
                dve.tensor_reduce(m_side[ODD], p_s[ODD, :, P:P + WINDOW], AX.X, ALU.max).then_inc(g_chain.sem, 1)
                dve.wait_ge(g_chain.sem, base + 1)
                dve.tensor_scalar(m_side[:], m_side[:], out_of, None, ALU.add).then_inc(g_chain.sem, 1)
                dve.wait_ge(g_chain.sem, base + 2)
                dve.tensor_tensor(m_all[:], m_side[:], m_main[:], ALU.max).then_inc(g_chain.sem, 1)
                dve.wait_ge(g_chain.sem, base + 3)
                dve.tensor_scalar(m_edge[:], m_all[:], out_of, None, ALU.subtract).then_inc(g_chain.sem, 1)
                dve.wait_ge(g_chain.sem, base + 4)
                dve.tensor_tensor(z[:, g, :, 0:P], p_s[:, :, 0:P], wide(m_all, slice(0, P), P), ALU.subtract)
                dve.tensor_tensor(z[EVEN, g, :, P + WINDOW:], p_s[EVEN, :, P + WINDOW:], wide(m_edge, EVEN, WINDOW), ALU.subtract)
                dve.tensor_tensor(z[ODD, g, :, P:P + WINDOW], p_s[ODD, :, P:P + WINDOW], wide(m_edge, ODD, WINDOW), ALU.subtract)\
                   .then_inc(z_ready.sem, 1)

            def shares(e, g):
                dve.wait_ge(exped.sem, exped.after(e))
                dve.wait_ge(p_turned.sem, p_turned.after(e - 2))
                dve.reciprocal(share[:, g], den[:, g]).then_inc(r_chain.sem, 1)
                dve.wait_ge(r_chain.sem, r_chain.after(e))
                dve.tensor_tensor(diagonal[:, g], s.ident[:].rearrange("p (a n) -> p a n", a=1).broadcast_to([P, HALF_HEADS, P]),
                                  wide(share[:, g], slice(0, P), P), ALU.mult).then_inc(diagonal_ready.sem, 1)

            def statistics(i, k):
                m = i * SLOTS4 + k
                base = f_chain.after(m - 1)
                dve.wait_ge(light_ready.sem, light_ready.after(m))
                dve.wait_ge(rows_ready.sem, rows_ready.after(m - 1))
                dve.tensor_tensor(y[:], light[:, k % 2], null_q[:], ALU.add).then_inc(f_chain.sem, 1)
                dve.wait_ge(f_chain.sem, base + 1)
                dve.bn_stats(stats[:], y[:]).then_inc(f_chain.sem, 1)
                dve.wait_ge(f_chain.sem, base + 2)
                apart(dve, s)
                dve.bn_aggr(mean_var[:], stats[:]).then_inc(f_chain.sem, 1)

            def normalise(i, k):
                m = i * SLOTS4 + k
                dve.wait_ge(inverted.sem, inverted.after(m))
                dve.tensor_scalar(y[:], y[:], mean_var[:, 0:1], inv[:, 0:1], ALU.subtract, ALU.mult).then_inc(f_chain.sem, 1)

            def turn(i, k, has):
                m = i * SLOTS4 + k
                shares(2 * m, 0)
                maxima(2 * m + 1, m, 1)
                shares(2 * m + 1, 1)
                if has(-1):
                    statistics(*at(i, k, -1))
                if has(1):
                    maxima(2 * m + 2, m + 1, 0)
                if has(-1):
                    normalise(*at(i, k, -1))
                if has(2):
                    take_v(*at(i, k, 2))

            def before():
                take_v(0, 0)
                take_v(0, 1)
                maxima(0, 0, 0)

            def after(i, k):
                statistics(*at(i, k, -1))
                normalise(*at(i, k, -1))

            loop(dve, before, turn, after)


N_Q, N_KV = 128, 256
ITERATIONS = 50
FETCH = 9.0 / 8.0
ROUTES = 2 * BATCH
DRAWN = (N_Q,) * BATCH + (N_KV,) * BATCH
LOWEST = 104.0
FLOAT_BITS = 31
ROW_TILES = 3


def route(nc, s):
    with ExitStack() as ctx:
        def sb(name, shape, dt=fp32):
            return ctx.enter_context(nc.sbuf_tensor(name, shape, dt))

        def ps(name, shape):
            return ctx.enter_context(nc.psum_tensor(name, shape, fp32))

        def steps(name, per=1, lead=2):
            return Steps(ctx.enter_context(nc.semaphore(name)), per, lead)

        T = TILES_B
        s17 = sb("s17", [P, ROUTES, T + 1])
        top = sb("top", [P, ROUTES])
        top8, top_diag = sb("top8", [ROUTES, 1]), sb("top_diag", [ROUTES, ROUTES])
        ones, tri, reset = sb("ones", [P, P]), sb("tri", [P, P], bf16), sb("reset", [P, ROUTES, T])
        ones_b = sb("ones_b", [P, P], bf16)
        log_k, k_of = sb("log_k", [P, ROUTES]), sb("k_of", [P, ROUTES])
        a, c = sb("route_a", [P, ROUTES]), sb("route_c", [P, ROUTES])
        t17, nz17, w17 = sb("t17", [P, ROUTES, T + 1]), sb("nz17", [P, ROUTES, T + 1]), sb("w17", [P, ROUTES, T + 1])
        e, part, log_sum = sb("route_e", [P, ROUTES, T]), sb("route_part", [P, ROUTES]), sb("log_sum", [P, ROUTES])
        x, x_clamped, sc = sb("route_x", [P, ROUTES, T]), sb("x_clamped", [P, ROUTES, T]), sb("route_sc", [P, ROUTES, T])
        bit_f, bit_i = sb("bit_f", [P, 1]), sb("bit_i", [P, 1], i32)
        limit, trial, kept = sb("limit", [P, ROUTES], i32), sb("trial", [P, ROUTES], i32), sb("kept", [P, ROUTES], i32)
        below, tie = sb("below", [P, ROUTES, T]), sb("tie", [P, ROUTES, T], bf16)
        count, few = sb("count", [P, ROUTES]), sb("few", [P, ROUTES])
        scan, order = sb("scan", [P, ROUTES, T]), sb("order", [P, ROUTES, T])
        chosen, chosen_b, place = sb("chosen", [P, ROUTES, T]), sb("chosen_b", [P, ROUTES, T], bf16), sb("place", [P, ROUTES, T])
        number_i, number = sb("number_i", [P, 2, ROUTES, T], i32), sb("number", [P, ROUTES, T, 3], bf16)
        slot_i, slot = sb("slot_i", [P, N_KV], i32), sb("slot", [P, N_KV])
        one_hot = sb("one_hot", [P, 2, T, N_KV], bf16)
        token = sb("token", [P, BATCH, ROW_TILES])
        p_sum, p_tri, p_all = ps("p_sum", [P, 512]), ps("p_tri", [P, 512]), ps("p_all", [P, 512])
        p_number = ps("p_number", [P, BATCH, ROW_TILES, 3])

        d = steps("route_step", lead=2)
        exped, summed, logged = steps("r_exped"), steps("r_summed"), steps("r_logged")
        constants_made = ctx.enter_context(nc.semaphore("r_constants"))
        hot, gathered = steps("hot"), steps("hot_used")
        block = ctx.enter_context(nc.Block())

        def wide(v, n):
            return v.rearrange("p (r a) -> p r a", a=1).broadcast_to([P, ROUTES, n])

        TURN = 6
        BIT_TURN = 8
        START = 5
        SEARCH = START + TURN * (ITERATIONS - 1)
        PREPARE = 4
        SELECT = SEARCH + PREPARE + BIT_TURN * FLOAT_BITS
        SUM_BITS = 2 + ITERATIONS - 1
        SUM_LAST = SUM_BITS + FLOAT_BITS
        numbered = [(b, r, problem) for b in range(BATCH) for r, problem in ((0, BATCH + b), (2, b))]

        @block.gpsimd
        def _(pool):
            pool.memset(ones[:], 1.0).then_inc(constants_made, 1)
            pool.memset(ones_b[:], 1.0).then_inc(constants_made, 1)
            pool.memset(tri[:], 1.0).then_inc(constants_made, 1)
            pool.memset(reset[:], 1.0).then_inc(constants_made, 1)
            pool.iota(number_i[:, 0], pattern=[[0, 2], [T, BATCH], [1, T]], base=0, channel_multiplier=0).then_inc(constants_made, 1)
            pool.iota(number_i[:, 1], pattern=[[0, ROUTES], [0, T]], base=0, channel_multiplier=1).then_inc(constants_made, 1)
            pool.iota(slot_i[:], pattern=[[1, N_KV]], base=0, channel_multiplier=0).then_inc(constants_made, 1)
            pool.wait_ge(constants_made, 7)
            pool.affine_select(out=tri[:], in_=tri[:], compare_op=ALU.is_gt, fill=0.0, base=0, pattern=[[1, P]],
                               channel_multiplier=-1).then_inc(constants_made, 1)
            pool.memset(reset[:, :, 0:1], 0.0).then_inc(constants_made, 1)
            pool.tensor_copy(number[:, :, :, 0], number_i[:, 0]).then_inc(constants_made, 1)
            pool.tensor_copy(number[:, :, :, 1], number_i[:, 1]).then_inc(constants_made, 1)
            pool.tensor_copy(slot[:], slot_i[:]).then_inc(constants_made, 1)

        @block.tensor
        def _(pe):
            summed.open(pe)
            gathered.open(pe)
            pe.wait_ge(constants_made, 12)
            pe.wait_ge(d.sem, d.after(1))
            nc.tensor.transpose(p_sum[0:ROUTES, 0:P], top[:], s.ident[:]).then_inc(summed.sem, 1)
            pe.wait_ge(d.sem, d.after(3))
            nc.tensor.matmul(p_sum[:, 0:ROUTES], ones[0:ROUTES, :], top_diag[:], start=True, stop=True).then_inc(summed.sem, 1)

            def total(step):
                pe.wait_ge(d.sem, d.after(step))
                nc.tensor.matmul(p_sum[:, 0:ROUTES], ones[:], part[:], start=True, stop=True).then_inc(summed.sem, 1)

            with pe.Fori(0, ITERATIONS - 1) as i:
                total(START + i * TURN + 4)
            with pe.Fori(0, FLOAT_BITS) as i:
                total(SEARCH + PREPARE + i * BIT_TURN + 3)
            total(SELECT + 1)
            for n, (step, what) in enumerate(((SELECT + 3, tie), (SELECT + 12, chosen_b))):
                pe.wait_ge(d.sem, d.after(step))
                flat = what[:].rearrange("p r t -> p (r t)")
                nc.tensor.matmul(p_tri[:, 0:ROUTES * T], tri[:], flat, start=True, stop=True)
                nc.tensor.matmul(p_all[:, 0:ROUTES * T], ones_b[:], flat, start=True, stop=True).then_inc(summed.sem, 1)
            for n, (b, r, problem) in enumerate(numbered):
                pe.wait_ge(hot.sem, hot.after(n))
                for j in range(DRAWN[problem] // P):
                    for t in range(T):
                        last = nc.tensor.matmul(p_number[:, b, r + j], one_hot[:, n % 2, t, P * j:P * j + P],
                                                number[:, problem, t], start=(t == 0), stop=(t == T - 1))
                last.then_inc(gathered.sem, 1)

        @block.scalar
        def _(act):
            exped.open(act)
            logged.open(act)
            with act.Fori(0, ITERATIONS - 1) as i:
                act.wait_ge(d.sem, d.after(START + i * TURN + 2))
                act.activation(e[:], w17[:, :, 0:T], ACT.Exp, scale=-1.0).then_inc(exped.sem, 1)
                act.wait_ge(summed.sem, summed.after(2 + i))
                act.activation(log_sum[:], p_sum[:, 0:ROUTES], ACT.Ln).then_inc(logged.sem, 1)
            act.wait_ge(d.sem, d.after(SEARCH + 1))
            act.activation(sc[:], x[:], ACT.Exp, scale=-1.0).then_inc(exped.sem, 1)

        @block.vector
        def _(dve):
            d.open(dve)
            hot.open(dve)

            def step(instruction, at):
                instruction.then_inc(d.sem, 1)
                dve.wait_ge(d.sem, d.after(at))

            scores = s17[:, :, 0:T]
            step(dve.tensor_copy(scores, s.route_s[:].rearrange("p r (b t) -> p (r b) t", b=BATCH)), 0)
            step(dve.tensor_reduce(top[:], scores, AX.X, ALU.max), 1)
            dve.wait_ge(summed.sem, summed.after(0))
            step(dve.tensor_reduce(top8[:], p_sum[0:ROUTES, 0:P], AX.X, ALU.max), 2)
            step(dve.tensor_scalar(top_diag[:], s.ident[0:ROUTES, 0:ROUTES], top8[:], None, ALU.mult), 3)
            dve.wait_ge(summed.sem, summed.after(1))
            for r, k in ((0, N_Q), (1, N_KV)):
                some = slice(r * BATCH, (r + 1) * BATCH)
                log = float(np.log(np.float32(min(k * FETCH, float(SEQ)))))
                dve.memset(log_k[:, some], log)
                dve.memset(k_of[:, some], float(k))
                dve.memset(a[:, some], float(np.float32(log) - np.log(np.float32(SEQ))))
            step(dve.tensor_copy(s17[:, :, T:T + 1], p_sum[:, 0:ROUTES].rearrange("p (r a) -> p r a", a=1)), 4)
            with dve.Fori(0, ITERATIONS - 1) as i:
                base = START + i * TURN
                step(dve.tensor_tensor(t17[:], s17[:], wide(a[:], T + 1), ALU.add), base)
                step(dve.scalar_tensor_tensor(nz17[:], t17[:], 0.0, s17[:], ALU.max, ALU.subtract), base + 1)
                step(dve.tensor_tensor(w17[:], nz17[:], nz17[:, :, T:T + 1].broadcast_to([P, ROUTES, T + 1]), ALU.subtract), base + 2)
                step(dve.tensor_tensor(c[:], log_k[:], nz17[:, :, T], ALU.add), base + 3)
                dve.wait_ge(exped.sem, exped.after(i))
                step(dve.tensor_reduce(part[:], e[:], AX.X, ALU.add), base + 4)
                dve.wait_ge(logged.sem, logged.after(i))
                step(dve.tensor_tensor(a[:], c[:], log_sum[:], ALU.subtract), base + 5)
            step(dve.tensor_tensor(t17[:], s17[:], wide(a[:], T + 1), ALU.add), SEARCH)
            step(dve.tensor_scalar(x[:], t17[:, :, 0:T], -1.0, 0.0, ALU.mult, ALU.max), SEARCH + 1)
            dve.memset(limit[:], 0)
            dve.memset(bit_f[:], float(2 ** (FLOAT_BITS - 1)))
            step(dve.tensor_scalar(x_clamped[:], x[:], LOWEST, None, ALU.min), SEARCH + 2)
            step(dve.tensor_copy(bit_i[:], bit_f[:]), SEARCH + 3)
            with dve.Fori(0, FLOAT_BITS) as i:
                base = SEARCH + PREPARE + i * BIT_TURN
                step(dve.tensor_copy(bit_i[:], bit_f[:]), base)
                step(dve.tensor_tensor(trial[:], limit[:], bit_i[:].broadcast_to([P, ROUTES]), ALU.bitwise_or), base + 1)
                step(dve.tensor_tensor(below[:], x_clamped[:], wide(trial[:].bitcast(fp32), T), ALU.is_lt), base + 2)
                step(dve.tensor_reduce(part[:], below[:], AX.X, ALU.add), base + 3)
                dve.wait_ge(summed.sem, summed.after(SUM_BITS + i))
                step(dve.tensor_tensor(few[:], p_sum[:, 0:ROUTES], k_of[:], ALU.is_lt), base + 4)
                step(dve.tensor_scalar(kept[:], few[:], bit_f[:], None, ALU.mult), base + 5)
                step(dve.tensor_tensor(limit[:], limit[:], kept[:], ALU.bitwise_or), base + 6)
                step(dve.tensor_scalar(bit_f[:], bit_f[:], 0.5, None, ALU.mult), base + 7)
            limit_f = wide(limit[:].bitcast(fp32), T)
            step(dve.tensor_tensor(below[:], x_clamped[:], limit_f, ALU.is_lt), SELECT)
            step(dve.tensor_reduce(part[:], below[:], AX.X, ALU.add), SELECT + 1)
            dve.wait_ge(summed.sem, summed.after(SUM_LAST))
            step(dve.tensor_tensor(count[:], k_of[:], p_sum[:, 0:ROUTES], ALU.subtract), SELECT + 2)
            step(dve.tensor_tensor(tie[:], x_clamped[:], limit_f, ALU.is_equal), SELECT + 3)
            dve.wait_ge(summed.sem, summed.after(SUM_LAST + 1))

            def before(at):
                flat = "p r t -> p (r t)"
                every = p_all[:, 0:ROUTES * T]
                step(dve.tensor_tensor_scan(scan[:].rearrange(flat), reset[:].rearrange(flat), every, 0.0, ALU.mult, ALU.add), at)
                step(dve.tensor_tensor(scan[:].rearrange(flat), scan[:].rearrange(flat), every, ALU.subtract), at + 1)
                step(dve.tensor_tensor(order[:].rearrange(flat), scan[:].rearrange(flat), p_tri[:, 0:ROUTES * T], ALU.add), at + 2)

            dve.wait_ge(constants_made, 12)
            before(SELECT + 4)
            step(dve.tensor_tensor(order[:], order[:], wide(count[:], T), ALU.is_lt), SELECT + 7)
            step(dve.tensor_tensor(order[:], order[:], tie[:], ALU.mult), SELECT + 8)
            step(dve.tensor_tensor(chosen[:], order[:], below[:], ALU.add), SELECT + 9)
            dve.wait_ge(exped.sem, exped.after(ITERATIONS - 1))
            step(dve.tensor_scalar(x[:], sc[:], -1.0, 1.0, ALU.mult, ALU.add), SELECT + 10)
            step(dve.tensor_tensor(sc[:], sc[:], x[:], ALU.add), SELECT + 11)
            step(dve.tensor_copy(chosen_b[:], chosen[:]), SELECT + 12)
            step(dve.tensor_scalar(number[:, :, :, 2], sc[:], -1.0, None, ALU.add), SELECT + 13)
            dve.wait_ge(summed.sem, summed.after(SUM_LAST + 2))
            before(SELECT + 14)
            step(dve.scalar_tensor_tensor(place[:], order[:], 1.0, chosen[:], ALU.add, ALU.mult), SELECT + 17)
            step(dve.tensor_scalar(place[:], place[:], -1.0, None, ALU.add), SELECT + 18)
            for n, (b, r, problem) in enumerate(numbered):
                dve.wait_ge(gathered.sem, gathered.after(n - 2))
                k = DRAWN[problem]
                for t in range(T):
                    last = dve.tensor_scalar(one_hot[:, n % 2, t, 0:k], slot[:, 0:k], place[:, problem, t:t + 1], None, ALU.is_equal)
                last.then_inc(hot.sem, 1)
            dve.wait_ge(gathered.sem, gathered.after(len(numbered) - 1))
            step(dve.tensor_scalar(token[:], p_number[:, :, :, 0], float(P), None, ALU.mult), SELECT + 19)
            step(dve.tensor_tensor(token[:], token[:], p_number[:, :, :, 1], ALU.add), SELECT + 20)
            step(dve.tensor_copy(s.token_i[:], token[:]), SELECT + 21)
            step(dve.tensor_scalar(s.weight[:], p_number[:, :, :, 2], 1.0, None, ALU.add), SELECT + 22)


def heavy(nc, s):
    with ExitStack() as ctx:
        def sb(name, shape, dt=fp32):
            return ctx.enter_context(nc.sbuf_tensor(name, shape, dt))

        def ps(name, shape):
            return ctx.enter_context(nc.psum_tensor(name, shape, fp32))

        def steps(name, per=1, lead=2):
            return Steps(ctx.enter_context(nc.semaphore(name)), per, lead)

        EVEN, ODD = slice(0, L_HD), slice(L_HD, P)
        KEYS, ALL_ROWS = N_KV, N_KV + N_Q
        rows_in = sb("rows_in", [P, BATCH, ROW_TILES, DIM])
        x1_rows, light_rows = sb("x1_rows", [P, BATCH, DIM]), sb("h_light_rows", [P, BATCH, DIM])
        out_rows = sb("h_out_rows", [P, BATCH, DIM])
        gamma = sb("gamma", [P, HALVES])
        null_k, null_v = sb("null_k", [P, PAIR_CHUNKS]), sb("null_v", [P, L_HEADS, L_HD + 1])
        own_rows = sb("own_rows", [P, ROW_TILES, DIM])
        squares, square_sum = sb("squares", [P, ROW_TILES, DIM]), sb("square_sum", [P, ROW_TILES])
        norm, inv_norm = sb("norm", [P, ROW_TILES]), sb("inv_norm", [P, ROW_TILES])
        rms = sb("rms", [P, ROW_TILES, DIM])
        rms_t = sb("rms_t", [P, HALVES, ALL_ROWS])
        q_pad = sb("h_q_pad", [P, L_HEADS, P])
        keys, vals = sb("h_keys", [P, PAIR_CHUNKS, KEYS]), sb("h_vals", [P, 2, L_HEADS, L_HD + 1])
        m, m_null = sb("h_m", [P, HALF_HEADS]), sb("h_m_null", [P, L_HEADS])
        z, z_null = sb("h_z", [P, HALF_HEADS, KEYS]), sb("h_z_null", [P, HALF_HEADS])
        probs, p_null = sb("h_probs", [P, HALF_HEADS, KEYS]), sb("h_p_null", [P, HALF_HEADS])
        probs_t = sb("h_probs_t", [P, HALF_HEADS, 2, P])
        o_null, o_all, den = sb("o_null", [P, HALF_HEADS, L_HD + 1]), sb("o_all", [P, HALF_HEADS, L_HD + 1]), sb("h_den", [P, HALF_HEADS])
        o_n, o_t = sb("h_o_n", [P, L_HEADS, L_HD]), sb("h_o_t", [P, PAIR_CHUNKS, P])
        y = sb("h_y", [P, DIM])
        stats, mean_var, inv = sb("stats4", [P, 6]), sb("mean_var4", [P, 2]), sb("inv4", [P, 1])
        p_rms = ps("p_rms", [P, HALVES, 512])
        p_keys = ps("p_keys", [P, PAIR_CHUNKS, KEYS])
        p_probs = ps("p_probs", [P, HALF_HEADS, 2, P])
        p_q, p_o = ps("h_p_q", [P, 512]), ps("h_p_o", [P, 512])
        p_null_s = p_o[:, 384:384 + L_HEADS]
        sums = p_o[:, 0:HALF_HEADS * (L_HD + 1)].rearrange("p (h d) -> p h d", h=HALF_HEADS)

        loaded, filled = ctx.enter_context(nc.semaphore("h_loaded")), ctx.enter_context(nc.semaphore("h_filled"))
        rows_loaded = ctx.enter_context(nc.semaphore("rows_loaded"))
        scattered = ctx.enter_context(nc.semaphore("scattered"))
        copied = steps("own_copied")
        squared, rooted, rms_chain = steps("squared2"), steps("rooted", 2), steps("rms_chain", 2)
        rms_turned, rms_t_ready, projected, vals_done = steps("rms_turned"), steps("rms_t_ready"), steps("h_projected"), steps("vals_done")
        qk_ready, vals_ready, null_scored = steps("h_qk_ready"), steps("h_vals_ready"), steps("null_scored")
        scored, z_chain, z_ready, exped = steps("h_scored"), steps("z_chain", 3), steps("h_z_ready"), steps("h_exped")
        p_turned, p_ready, summed = steps("h_p_turned"), steps("h_p_ready"), steps("h_summed")
        null_added, o_chain, o_ready = steps("null_weighed"), steps("o_chain", 2), steps("h_o_ready")
        o_turned, o_t_ready, y_done = steps("h_o_turned"), steps("h_o_t_ready"), steps("h_y_done")
        y_chain, inverted, rows_ready = steps("y_chain", 5), steps("inverted4", 2), steps("h_rows_ready")
        m_null_ready = steps("m_null_ready")
        block = ctx.enter_context(nc.Block())

        @block.sync
        def _(sp):
            sp.dma_start(gamma[:], s.d_gamma.rearrange("(k p) -> p k", p=P), allow_slow_non_contiguous=True).then_inc(loaded, 16)
            sp.dma_start(null_k[:], s.d_null_kv[0].rearrange("(c a) d -> (a d) c", a=2), allow_slow_non_contiguous=True).then_inc(loaded, 16)
            sp.wait_ge(filled, 3)
            sp.dma_start(null_v[:, :, 0:L_HD], s.d_null_kv[1:2].broadcast_to([P, L_HEADS, L_HD])).then_inc(loaded, 16)

        @block.gpsimd
        def _(pool):
            for made in (rooted, inverted, rows_ready):
                made.open(pool)
            flat = "t p d -> (t p) d"
            for b in range(BATCH):
                sources = [(rows_in[:, b, r], s.d_h, r) for r in range(ROW_TILES)]
                sources += [(x1_rows[:, b], s.d_x1, 2), (light_rows[:, b], s.d_light, 2)]
                for target, source, r in sources:
                    pool.indirect_dma_start(out=target, out_offset=None, in_=source.rearrange(flat),
                                            in_offset=bass.IndirectOffsetOnAxis(ap=s.token_i[:, b, r:r + 1], axis=0))\
                        .then_inc(rows_loaded, 16)
            with pool.Fori(0, BATCH) as b:
                pool.wait_ge(squared.sem, squared.after(b))
                pool.tensor_tensor(norm[:], square_sum[:], s.half[:, 0:ROW_TILES], ALU.pow).then_inc(rooted.sem, 1)
                pool.wait_ge(rooted.sem, rooted.after(b - 1) + 1)
                apart(pool, s)
                pool.tensor_scalar(norm[:], norm[:], 1e-12, None, ALU.max).then_inc(rooted.sem, 1)
                pool.wait_ge(y_chain.sem, y_chain.after(b - 1) + 4)
                apart(pool, s)
                pool.tensor_scalar(inv[:], mean_var[:, 1:2], EPS, None, ALU.add).then_inc(inverted.sem, 1)
                pool.wait_ge(inverted.sem, inverted.after(b - 1) + 1)
                pool.tensor_tensor(inv[:], inv[:], s.power[:, 0:1], ALU.pow).then_inc(inverted.sem, 1)
                pool.wait_ge(y_chain.sem, y_chain.after(b))
                pool.tensor_tensor(out_rows[:, bass.ds(b, 1)].rearrange("p a d -> p (a d)"), y[:],
                                   x1_rows[:, bass.ds(b, 1)].rearrange("p a d -> p (a d)"), ALU.add).then_inc(rows_ready.sem, 1)
            pool.wait_ge(rows_ready.sem, rows_ready.after(BATCH - 1))
            for b in range(BATCH):
                pool.indirect_dma_start(out=s.d_out.rearrange(flat), out_offset=bass.IndirectOffsetOnAxis(ap=s.token_i[:, b, 2:3], axis=0),
                                        in_=out_rows[:, b], in_offset=None).then_inc(scattered, 16)
            pool.wait_ge(scattered, 16 * BATCH)

        @block.tensor
        def _(pe):
            for made in (rms_turned, projected, vals_done, null_scored, scored, p_turned, summed, o_turned, y_done):
                made.open(pe)
            pe.wait_ge(filled, 3)
            pe.wait_ge(loaded, 48)
            with pe.Fori(0, BATCH) as b:
                pe.wait_ge(rms_chain.sem, rms_chain.after(b))
                pe.wait_ge(y_chain.sem, y_chain.after(b - 2) + 1)
                for r in range(ROW_TILES):
                    for k in range(HALVES):
                        last = nc.tensor.transpose(p_rms[:, k, P * r:P * r + P], rms[:, r, P * k:P * k + P], s.ident[:])
                last.then_inc(rms_turned.sem, 1)
                pe.wait_ge(rms_t_ready.sem, rms_t_ready.after(b))
                for c in range(PAIR_CHUNKS):
                    for k in range(HALVES):
                        nc.tensor.matmul(p_q[:, P * c:P * c + P], s.wq_h_t[:, k, P * c:P * c + P], rms_t[:, k, KEYS:ALL_ROWS],
                                         start=(k == 0), stop=(k == HALVES - 1))
                for c in range(PAIR_CHUNKS):
                    for k in range(HALVES):
                        w = s.wkv_h_t[:, k, 0, 2 * c:2 * c + 2].rearrange("p h d -> p (h d)")
                        last = nc.tensor.matmul(p_keys[:, c], w, rms_t[:, k, 0:KEYS], start=(k == 0), stop=(k == HALVES - 1))
                last.then_inc(projected.sem, 1)
                for r in range(2):
                    for k in range(HALVES):
                        w = s.wkv_h_t[:, k, 1].rearrange("p h d -> p (h d)")
                        last = nc.tensor.matmul(p_rms[:, r], rms_t[:, k, P * r:P * r + P], w, start=(k == 0), stop=(k == HALVES - 1))
                last.then_inc(vals_done.sem, 1)
                pe.wait_ge(qk_ready.sem, qk_ready.after(b))
                for h in range(L_HEADS):
                    last = nc.tensor.matmul(p_null_s[:, h:h + 1], q_pad[:, h], null_k[:, h // 2:h // 2 + 1], start=True, stop=True)
                last.then_inc(null_scored.sem, 1)
                for g in range(2):
                    e = b * 2 + g
                    pe.wait_ge(z_ready.sem, z_ready.after(e - 1))
                    for j in range(HALF_HEADS):
                        h = g * HALF_HEADS + j
                        last = nc.tensor.matmul(p_keys[:, j], q_pad[:, h], keys[:, h // 2], start=True, stop=True)
                    last.then_inc(scored.sem, 1)
                    pe.wait_ge(exped.sem, exped.after(e))
                    pe.wait_ge(p_ready.sem, p_ready.after(e - 1))
                    for j in range(HALF_HEADS):
                        for r in range(2):
                            last = nc.tensor.transpose(p_probs[:, j, r], probs[:, j, P * r:P * r + P], s.ident[:])
                    last.then_inc(p_turned.sem, 1)
                    pe.wait_ge(p_ready.sem, p_ready.after(e))
                    pe.wait_ge(vals_ready.sem, vals_ready.after(b))
                    pe.wait_ge(o_chain.sem, o_chain.after(e - 1))
                    pe.wait_ge(m_null_ready.sem, m_null_ready.after(b))
                    for j in range(HALF_HEADS):
                        h = g * HALF_HEADS + j
                        for r in range(2):
                            last = nc.tensor.matmul(sums[:, j], probs_t[:, j, r], vals[:, r, h], start=(r == 0), stop=(r == 1))
                    last.then_inc(summed.sem, 1)
                pe.wait_ge(o_ready.sem, o_ready.after(b * 2 + 1))
                for c in range(PAIR_CHUNKS):
                    last = nc.tensor.transpose(p_q[:, P * c:P * c + P], o_n[:, 2 * c:2 * c + 2].rearrange("p h d -> p (h d)"), s.ident[:])
                last.then_inc(o_turned.sem, 1)
                pe.wait_ge(o_t_ready.sem, o_t_ready.after(b))
                for c in range(PAIR_CHUNKS):
                    last = nc.tensor.matmul(p_rms[:, 0, 0:DIM], o_t[:, c], s.wout_h_t[:, c], start=(c == 0), stop=(c == PAIR_CHUNKS - 1))
                last.then_inc(y_done.sem, 1)

        @block.scalar
        def _(act):
            for made in (rms_t_ready, qk_ready, exped, p_ready, o_t_ready):
                made.open(act)
            act.wait_ge(loaded, 48)
            act.wait_ge(filled, 3)
            with act.Fori(0, BATCH) as b:
                act.wait_ge(rms_turned.sem, rms_turned.after(b))
                for k in range(HALVES):
                    last = act.activation(rms_t[:, k], p_rms[:, k, 0:ALL_ROWS], ACT.Copy, scale=gamma[:, k:k + 1])
                last.then_inc(rms_t_ready.sem, 1)
                act.wait_ge(projected.sem, projected.after(b))
                q = p_q[:].rearrange("p (c n) -> p c n", c=PAIR_CHUNKS)
                pairs = q_pad[:].rearrange("p (c a) n -> p c a n", a=2)
                act.activation(pairs[EVEN, :, 0], q[EVEN], ACT.Copy)
                act.activation(pairs[ODD, :, 1], q[ODD], ACT.Copy)
                act.activation(keys[:], p_keys[:], ACT.Copy).then_inc(qk_ready.sem, 1)
                for g in range(2):
                    e = b * 2 + g
                    act.wait_ge(z_ready.sem, z_ready.after(e))
                    act.wait_ge(null_added.sem, null_added.after(e - 1))
                    act.activation(p_null[:], z_null[:], ACT.Exp, scale=L_SCALE)
                    act.activation(probs[:], z[:], ACT.Exp, scale=L_SCALE).then_inc(exped.sem, 1)
                    act.wait_ge(p_turned.sem, p_turned.after(e))
                    act.activation(probs_t[:], p_probs[:], ACT.Copy).then_inc(p_ready.sem, 1)
                act.wait_ge(o_turned.sem, o_turned.after(b))
                act.activation(o_t[:], p_q[:].rearrange("p (c n) -> p c n", c=PAIR_CHUNKS), ACT.Copy).then_inc(o_t_ready.sem, 1)

        @block.vector
        def _(dve):
            for made in (copied, squared, rms_chain, vals_ready, m_null_ready, z_chain, z_ready, null_added, o_chain, o_ready, y_chain):
                made.open(dve)
            dve.memset(q_pad[:], 0.0).then_inc(filled, 1)
            dve.memset(vals[:], 1.0).then_inc(filled, 1)
            dve.memset(null_v[:], 1.0).then_inc(filled, 1)
            dve.wait_ge(loaded, 48)
            dve.wait_ge(rows_loaded, 16 * BATCH * 5)

            def wide(x, n):
                return x.rearrange("p (h a) -> p h a", a=1).broadcast_to([P, HALF_HEADS, n])

            with dve.Fori(0, BATCH) as b:
                rows = rows_in[:, bass.ds(b, 1)].rearrange("p a r d -> p (a r) d")
                dve.tensor_copy(own_rows[:], rows).then_inc(copied.sem, 1)
                dve.wait_ge(copied.sem, copied.after(b))
                for r in range(ROW_TILES):
                    last = dve.tensor_tensor_reduce(out=squares[:, r], in0=own_rows[:, r], in1=own_rows[:, r], scale=1.0, scalar=0.0,
                                                    op0=ALU.mult, op1=ALU.add, accum_out=square_sum[:, r:r + 1])
                last.then_inc(squared.sem, 1)
                dve.wait_ge(rooted.sem, rooted.after(b))
                dve.reciprocal(inv_norm[:], norm[:]).then_inc(rms_chain.sem, 1)
                dve.wait_ge(rms_chain.sem, rms_chain.after(b - 1) + 1)
                for r in range(ROW_TILES):
                    last = dve.tensor_scalar(rms[:, r], rows[:, r], inv_norm[:, r:r + 1], float(DIM) ** 0.5, ALU.mult, ALU.mult)
                last.then_inc(rms_chain.sem, 1)
                dve.wait_ge(vals_done.sem, vals_done.after(b))
                for r in range(2):
                    last = dve.tensor_scalar(vals[:, r, :, 0:L_HD], p_rms[:, r].rearrange("p (h d) -> p h d", h=L_HEADS),
                                             s.weight[:, bass.ds(b, 1), r], None, ALU.mult)
                last.then_inc(vals_ready.sem, 1)
                dve.wait_ge(null_scored.sem, null_scored.after(b))
                dve.tensor_copy(m_null[:], p_null_s).then_inc(m_null_ready.sem, 1)
                dve.wait_ge(m_null_ready.sem, m_null_ready.after(b))
                for g in range(2):
                    e = b * 2 + g
                    null_s = m_null[:, HALF_HEADS * g:HALF_HEADS * (g + 1)]
                    dve.wait_ge(scored.sem, scored.after(e))
                    dve.tensor_reduce(m[:], p_keys[:], AX.X, ALU.max).then_inc(z_chain.sem, 1)
                    dve.wait_ge(z_chain.sem, z_chain.after(e - 1) + 1)
                    dve.tensor_tensor(m[:], m[:], null_s, ALU.max).then_inc(z_chain.sem, 1)
                    dve.wait_ge(z_chain.sem, z_chain.after(e - 1) + 2)
                    dve.wait_ge(exped.sem, exped.after(e - 1))
                    dve.tensor_tensor(z_null[:], null_s, m[:], ALU.subtract).then_inc(z_chain.sem, 1)
                    dve.tensor_tensor(z[:], p_keys[:], wide(m[:], KEYS), ALU.subtract).then_inc(z_ready.sem, 1)
                    dve.wait_ge(exped.sem, exped.after(e))
                    dve.tensor_tensor(o_null[:], null_v[:, HALF_HEADS * g:HALF_HEADS * (g + 1)], wide(p_null[:], L_HD + 1), ALU.mult)\
                       .then_inc(null_added.sem, 1)
                    dve.wait_ge(null_added.sem, null_added.after(e))
                    dve.wait_ge(summed.sem, summed.after(e))
                    dve.tensor_tensor(o_all[:], sums, o_null[:], ALU.add).then_inc(o_chain.sem, 1)
                    dve.wait_ge(o_chain.sem, o_chain.after(e - 1) + 1)
                    dve.reciprocal(den[:], o_all[:, :, L_HD]).then_inc(o_chain.sem, 1)
                    dve.wait_ge(o_chain.sem, o_chain.after(e))
                    dve.tensor_tensor(o_n[:, HALF_HEADS * g:HALF_HEADS * (g + 1)], o_all[:, :, 0:L_HD], wide(den[:], L_HD), ALU.mult)\
                       .then_inc(o_ready.sem, 1)
                base = y_chain.after(b - 1)
                dve.wait_ge(y_done.sem, y_done.after(b))
                dve.wait_ge(rows_ready.sem, rows_ready.after(b - 1))
                dve.tensor_scalar(y[:], p_rms[:, 0, 0:DIM], s.weight[:, bass.ds(b, 1), 2], None, ALU.mult).then_inc(y_chain.sem, 1)
                dve.wait_ge(y_chain.sem, base + 1)
                dve.tensor_tensor(y[:], y[:], light_rows[:, bass.ds(b, 1)].rearrange("p a d -> p (a d)"), ALU.add).then_inc(y_chain.sem, 1)
                dve.wait_ge(y_chain.sem, base + 2)
                dve.bn_stats(stats[:], y[:]).then_inc(y_chain.sem, 1)
                dve.wait_ge(y_chain.sem, base + 3)
                apart(dve, s)
                dve.bn_aggr(mean_var[:], stats[:]).then_inc(y_chain.sem, 1)
                dve.wait_ge(inverted.sem, inverted.after(b))
                dve.tensor_scalar(y[:], y[:], mean_var[:, 0:1], inv[:, 0:1], ALU.subtract, ALU.mult).then_inc(y_chain.sem, 1)


class Memory:
    pass


def build(nc, ins, out, debug=None):
    with ExitStack() as ctx:
        s = Memory()
        kind = "ExternalOutput" if debug else "Internal"

        def dram(name, shape, dt=fp32):
            return nc.dram_tensor(name, shape, dt, kind=kind).ap()

        def sb(name, shape, dt=fp32):
            return ctx.enter_context(nc.sbuf_tensor(name, shape, dt))

        (x, s.d_w_q, s.d_b_q, s.d_w_k, s.d_b_k, s.d_w_v, s.d_b_v, s.d_w_o, s.d_b_o, s.d_ln_w, s.d_ln_b, s.d_wqkv,
         s.d_wout_l, s.d_rt_q, s.d_rt_kv, s.d_gamma, s.d_wq_h, s.d_wkv_h, s.d_wout_h, s.d_null_kv, s.d_null_q) = ins
        s.d_x = x.rearrange("b (t p) d -> (b t) p d", p=P)
        q_parts = dram("q_parts", [PARTS, BATCH * HALVES, P, SEQ], bf16)
        k_parts = dram("k_parts", [PARTS, BATCH, KVD, SEQ], bf16)
        shift = dram("shift", [2, BATCH * HEADS, SEQ], bf16)
        attended = dram("attended", [BATCH * HALVES, P, SEQ])
        s.d_q_parts, s.d_k_parts, s.d_shift = q_parts, k_parts, shift
        s.q_rows = q_parts.rearrange("r b (h p) n -> r (b h) p n", p=HD)
        s.k_rows = k_parts.rearrange("r b (h p) n -> r (b h) p n", p=HD)
        s.a_rows = attended.rearrange("b (h p) n -> (b h) p n", p=HD).rearrange("(j h) p n -> j h p n", h=GROUP)
        s.d_attended = attended
        s.d_x1, s.d_h = dram("x1", [TILES, P, DIM]), dram("h", [TILES, P, DIM])
        s.d_u_t = dram("u_t", [P, HALVES, TOKENS])
        s.d_light = dram("light", [TILES, P, DIM])
        s.d_s = dram("route_dbg", [P, 2, TILES]) if debug else None
        s.d_out = out.rearrange("b (t p) d -> (b t) p d", p=P)
        s.ident = sb("ident", [P, P])
        s.passed = {engine.engine: ctx.enter_context(nc.semaphore(f"passed_{name}"))
                    for name, engine in (("pe", nc.tensor), ("dve", nc.vector), ("pool", nc.gpsimd), ("sp", nc.sync))}
        s.power, s.half = sb("power", [P, 16]), sb("half", [P, 16])
        s.token_i, s.weight = sb("token_i", [P, BATCH, ROW_TILES], i32), sb("weight", [P, BATCH, ROW_TILES])
        s.route_s = sb("route_s", [P, 2, TILES])
        with ExitStack() as first:
            def sb1(name, shape, dt=fp32):
                return first.enter_context(nc.sbuf_tensor(name, shape, dt))
            s.heads_of = sb1("heads_of", [P, 8])
            s.norm_sel = sb1("norm_sel", [P, 3, 20], bf16)
            s.zero_row = sb1("zero_row", [P, SEQ], bf16)
            s.norm_max = sb1("norm_max", [20, BATCH * BLOCKS_B])
            s.v_all = sb1("v_all", [P, BATCH * KV, TILES_B, 2 * HD])
            s.k_stack = sb1("k_stack", [P, 2, SEQ], bf16)
            s.w_q, s.w_k, s.w_v = sb1("w_q", [P, HALVES, DIM]), sb1("w_k", [P, HALVES, KVD]), sb1("w_v", [P, HALVES, KVD])
            s.b_q, s.b_k, s.b_v = sb1("b_q", [P, HALVES]), sb1("b_k", [KVD, 1]), sb1("b_v", [P, KVD])
            constants(nc, s)
            s.loose = sb1("loose", [1, 1], i32)
            project(nc, s)
            bound_scores(nc, s)
            largest_scores(nc, s)
            attend(nc, s)
        merge(nc, s)
        s.w_qkv_t, s.wout_l_t = sb("w_qkv_t", [P, HALVES, 3 * 512]), sb("wout_l_t", [P, 4, DIM])
        s.wq_h_t, s.wkv_h_t, s.wout_h_t = sb("wq_h_t", [P, HALVES, 512]), sb("wkv_h_t", [P, HALVES, 2, L_HEADS, L_HD]), sb("wout_h_t", [P, 4, DIM])
        transpose_weights(nc, s)
        local(nc, s)
        route(nc, s)
        heavy(nc, s)


_INS = ["L0_attn_x", "L0_attn_w_q", "L0_attn_b_q", "L0_attn_w_k", "L0_attn_b_k", "L0_attn_w_v", "L0_attn_b_v", "L0_attn_w_o",
        "L0_attn_b_o", "L0_ffn_ln_w", "L0_ffn_ln_b", "L0_ffn_Wqkv", "L0_ffn_Wout_l", "L0_ffn_rt_q", "L0_ffn_rt_kv", "L0_ffn_gamma",
        "L0_ffn_Wq", "L0_ffn_Wkv", "L0_ffn_Wout_h", "L0_ffn_null_kv", "L0_ffn_null_q"]


def kernel(**inputs):
    import numpy as _np
    import concourse.bacc as _bacc
    from concourse import mybir as _mybir
    from concourse.bass_utils import run_bass_kernel_spmd as _run

    nc = _bacc.Bacc("TRN2", target_bir_lowering=False, num_devices=1)
    arrays, args = {}, []
    for name in _INS:
        a = _np.ascontiguousarray(inputs[name])
        arrays[f"in_{name}"] = a
        args.append(nc.dram_tensor(f"in_{name}", a.shape, _mybir.dt.from_np(a.dtype), kind="ExternalInput").ap())
    out = nc.dram_tensor("out", (BATCH, SEQ, DIM), _mybir.dt.float32, kind="ExternalOutput").ap()
    build(nc, args, out)
    r = _run(nc, [arrays], core_ids=[0])
    return r.results[0]["out"]
```

```python
import concourse.bass as bass
import numpy as np
from concourse import mybir
from contextlib import ExitStack

fp32 = mybir.dt.float32
bf16 = mybir.dt.bfloat16
i32 = mybir.dt.int32
ALU = mybir.AluOpType
ACT = mybir.ActivationFunctionType
AX = mybir.AxisListType

BATCH, SEQ, DIM = 4, 2048, 256
TOKENS = BATCH * SEQ
P = 128
TILES = TOKENS // P
TILES_B = SEQ // P
BLOCK = 512
BT = BLOCK // P
BLOCKS_B = SEQ // BLOCK
HALVES = DIM // P
EPS = 1e-5
HEADS, KV, GROUP, HD = 16, 4, 4, 16
KVD = KV * HD
PARTS = 3
Q_PART = (0, 0, 1, 1, 0, 2)
K_PART = (0, 1, 0, 1, 2, 0)
SLOTS = len(Q_PART)
STACK = SLOTS * HD
ROWS = STACK + 2
A_SCALE = 1.0 / float(HD) ** 0.5
FAR = -1e38
BEHIND = -1e30
GUARD = 50.0


class Steps:

    def __init__(self, sem, per=1, lead=2):
        self.sem, self.per, self.lead = sem, per, lead

    def open(self, eng):
        eng.sem_inc(self.sem, self.lead * self.per)

    def after(self, step):
        return (step + 1 + self.lead) * self.per


def apart(engine, s):
    engine.sem_inc(s.passed[engine.engine], 1)


def inverse_root(pool, s, out, var, power, inverted, step):
    apart(pool, s)
    pool.tensor_scalar(out, var, EPS, None, ALU.add).then_inc(inverted.sem, 1)
    pool.wait_ge(inverted.sem, inverted.after(step - 1) + 1)
    pool.tensor_tensor(out, out, power, ALU.pow).then_inc(inverted.sem, 1)


def constants(nc, s):
    with nc.semaphore("const_filled") as const_filled, nc.semaphore("const_zero_out") as zero_out, \
            nc.semaphore("const_loaded") as loaded, nc.semaphore("rows_filled") as rows_filled, nc.Block() as block:

        @block.gpsimd
        def _(pool):
            pool.memset(s.ident[:], 0.0).then_inc(const_filled, 1)
            pool.memset(s.heads_of[:], 1.0).then_inc(const_filled, 1)
            pool.wait_ge(const_filled, 2)
            pool.affine_select(out=s.ident[:], in_=s.ident[:], compare_op=ALU.not_equal, fill=1.0,
                               base=0, pattern=[[-1, P]], channel_multiplier=1).then_inc(const_filled, 1)
            pool.affine_select(out=s.heads_of[:], in_=s.heads_of[:], compare_op=ALU.is_ge, fill=0.0,
                               base=0, pattern=[[-HD, 8]], channel_multiplier=1).then_inc(const_filled, 1)
            pool.wait_ge(const_filled, 4)
            pool.affine_select(out=s.heads_of[:], in_=s.heads_of[:], compare_op=ALU.is_ge, fill=0.0,
                               base=HD - 1, pattern=[[HD, 8]], channel_multiplier=-1).then_inc(const_filled, 1)
            pool.wait_ge(const_filled, 5)
            pool.memset(s.norm_sel[:], 0.0).then_inc(const_filled, 1)
            pool.wait_ge(const_filled, 6)
            pool.tensor_copy(s.norm_sel[:, 0, 0:8], s.heads_of[:]).then_inc(const_filled, 1)
            pool.tensor_copy(s.norm_sel[:, 1, 8:16], s.heads_of[:]).then_inc(const_filled, 1)
            pool.tensor_copy(s.norm_sel[0:KVD, 2, 16:20], s.heads_of[0:KVD, 0:KV]).then_inc(const_filled, 1)
            pool.tensor_copy(s.ident_b[:], s.ident[:]).then_inc(const_filled, 1)
            pool.memset(s.behind[:], 0.0).then_inc(const_filled, 1)
            pool.wait_ge(const_filled, 11)
            pool.affine_select(out=s.behind[:], in_=s.behind[:], compare_op=ALU.is_ge, fill=BEHIND, base=0, pattern=[[1, P]],
                               channel_multiplier=-1).then_inc(const_filled, 1)
            pool.wait_ge(const_filled, 12)

        @block.vector
        def _(dve):
            dve.memset(s.v_all[:, :, :, HD:], 1.0).then_inc(rows_filled, 1)
            dve.memset(s.k_stack[STACK:ROWS, :, :], 1.0).then_inc(rows_filled, 1)
            dve.memset(s.zero_row[:], 0.0).then_inc(rows_filled, 1)
            dve.memset(s.power[:], -0.5).then_inc(rows_filled, 1)
            dve.memset(s.half[:], 0.5).then_inc(rows_filled, 1)

        @block.sync
        def _(sp):
            sp.dma_start(s.w_q[:], s.d_w_q.rearrange("(k p) n -> p k n", p=P)).then_inc(loaded, 16)
            sp.dma_start(s.w_k[:], s.d_w_k.rearrange("(k p) n -> p k n", p=P)).then_inc(loaded, 16)
            sp.dma_start(s.w_v[:], s.d_w_v.rearrange("(k p) n -> p k n", p=P)).then_inc(loaded, 16)
            sp.dma_start(s.b_q[:], s.d_b_q.rearrange("(k p) -> p k", p=P), allow_slow_non_contiguous=True).then_inc(loaded, 16)
            sp.dma_start(s.b_k[:], s.d_b_k.rearrange("(p k) -> p k", k=1), allow_slow_non_contiguous=True).then_inc(loaded, 16)
            sp.dma_start(s.b_v[:], s.d_b_v.rearrange("(a n) -> a n", a=1).broadcast_to([P, KVD]))\
              .then_inc(loaded, 16)
            sp.dma_start(s.w_o[:], s.d_w_o.rearrange("(k p) n -> p k n", p=P)).then_inc(s.later_loaded, 16)
            sp.dma_start(s.b_o[:], s.d_b_o.rearrange("(a n) -> a n", a=1)).then_inc(s.later_loaded, 16)
            sp.dma_start(s.rt[:, 0], s.d_rt_q.broadcast_to([P, DIM])).then_inc(s.later_loaded, 16)
            sp.dma_start(s.rt[:, 1], s.d_rt_kv.broadcast_to([P, DIM])).then_inc(s.later_loaded, 16)
            sp.dma_start(s.ln_w[:], s.d_ln_w.rearrange("(k p) -> p k", p=P), allow_slow_non_contiguous=True).then_inc(s.later_loaded, 16)
            sp.dma_start(s.ln_b[:], s.d_ln_b.rearrange("(k p) -> p k", p=P), allow_slow_non_contiguous=True).then_inc(s.later_loaded, 16)
            sp.wait_ge(rows_filled, 3)
            sp.dma_start(s.d_shift, s.zero_row[:]).then_inc(zero_out, 16)
            sp.wait_ge(loaded, 6 * 16)
            sp.wait_ge(zero_out, 16)


def block_at(b, c, by):
    return b + (c + by) // BLOCKS_B, (c + by) % BLOCKS_B


def over_blocks(eng, before, turn):
    before()
    with eng.Fori(0, BATCH - 1) as b:
        for c in range(BLOCKS_B):
            turn(b, c, lambda by: True)
    for c in range(BLOCKS_B):
        turn(BATCH - 1, c, lambda by, c=c: c + by < BLOCKS_B)


def project(nc, s):
    with ExitStack() as ctx:
        def sb(name, shape, dt=fp32):
            return ctx.enter_context(nc.sbuf_tensor(name, shape, dt))

        def ps(name, shape):
            return ctx.enter_context(nc.psum_tensor(name, shape, fp32))

        def sem(name):
            return ctx.enter_context(nc.semaphore(name))

        x_in = sb("x_in", [P, BLOCKS_B, BT, DIM])
        stats = sb("stats", [P, 2, BT, 6])
        mean_var = sb("mean_var", [P, 2, BT, 2])
        inv = sb("inv", [P, 2, BT])
        x_n = sb("x_n", [P, 2, BT, DIM])
        x_t = sb("x_t", [P, 2, HALVES, BLOCK])
        q_f = sb("q_f", [P, 2, HALVES, BLOCK])
        k_f = sb("k_f", [KVD, 2, BLOCK])
        q_sq = sb("q_sq", [P, HALVES, BLOCK], bf16)
        k_sq = sb("k_sq", [KVD, BLOCK], bf16)
        q_p = sb("q_p", [P, 2, PARTS, HALVES, BLOCK], bf16)
        k_p = sb("k_p", [KVD, 2, PARTS, BLOCK], bf16)
        q_rest = sb("q_rest", [P, HALVES, BLOCK])
        k_rest = sb("k_rest", [KVD, BLOCK])
        p_t = ps("p_t", [P, HALVES, BLOCK])
        p_q = ps("p_q", [P, HALVES, BLOCK])
        p_k = ps("p_k", [P, BLOCK])
        p_v = ps("p_v", [P, BLOCK])
        p_norm = ps("p_norm", [P, BLOCK])

        def steps(name, per=1):
            return Steps(sem(name), per, 4)

        x_loaded = [steps(f"x_loaded_{c}", 16) for c in range(BLOCKS_B)]
        normed, norm_step, inverted = steps("normed"), steps("norm_step", 2), steps("inverted", 2)
        transposed, x_t_ready = steps("transposed"), steps("x_t_ready")
        qk_projected = steps("qk_projected")
        projected, biased, v_ready = steps("projected"), steps("biased"), steps("v_ready")
        q_split, k_split = steps("q_split", 4), steps("k_split", 4)
        q_out = [steps(f"q_out_{u}", 32) for u in range(2)]
        k_out = [steps(f"k_out_{u}", 16) for u in range(2)]
        squared, norms, norms_read = steps("squared"), steps("norms"), steps("norms_read")
        block = ctx.enter_context(nc.Block())

        @block.sync
        def _(sp):
            for made in (*x_loaded, *q_out, *k_out):
                made.open(sp)

            def load(b, c):
                sp.wait_ge(normed.sem, normed.after(b * BLOCKS_B + c - BLOCKS_B))
                sp.dma_start(x_in[:, c], s.d_x[bass.ds(b * TILES_B + BT * c, BT)].rearrange("t p d -> p t d"))\
                  .then_inc(x_loaded[c].sem, 16)

            def store(b, c):
                g, u = b * BLOCKS_B + c, c % 2
                sp.wait_ge(q_split.sem, q_split.after(g))
                for m in range(HALVES):
                    sp.dma_start(s.d_q_parts[:, bass.ds(b * 2 + m, 1), :, bass.ts(c, BLOCK)]
                                 .rearrange("r a p n -> p r (a n)"), q_p[:, u, :, m, :]).then_inc(q_out[u].sem, 16)
                sp.wait_ge(k_split.sem, k_split.after(g))
                sp.dma_start(s.d_k_parts[:, bass.ds(b, 1), :, bass.ts(c, BLOCK)]
                             .rearrange("r a p n -> p r (a n)"), k_p[:, u, :, :]).then_inc(k_out[u].sem, 16)

            def before():
                for c in range(3):
                    load(0, c)

            def turn(b, c, has):
                if has(3):
                    load(*block_at(b, c, 3))
                store(b, c)

            over_blocks(sp, before, turn)
            for u in range(2):
                sp.wait_ge(q_out[u].sem, q_out[u].after(BATCH * BLOCKS_B // 2 - 1))
                sp.wait_ge(k_out[u].sem, k_out[u].after(BATCH * BLOCKS_B // 2 - 1))

        @block.vector
        def _(dve):
            for made in (normed, norm_step, v_ready, q_split, norms_read):
                made.open(dve)

            def statistics(b, c):
                g, u = b * BLOCKS_B + c, c % 2
                dve.wait_ge(x_loaded[c].sem, x_loaded[c].after(b))
                dve.wait_ge(normed.sem, normed.after(g - 2))
                for t in range(BT):
                    last = dve.bn_stats(stats[:, u, t], x_in[:, c, t])
                last.then_inc(norm_step.sem, 1)
                dve.wait_ge(norm_step.sem, norm_step.after(g - 1) + 1)
                apart(dve, s)
                for t in range(BT):
                    last = dve.bn_aggr(mean_var[:, u, t], stats[:, u, t])
                last.then_inc(norm_step.sem, 1)

            def normalise(b, c):
                g, u = b * BLOCKS_B + c, c % 2
                dve.wait_ge(inverted.sem, inverted.after(g))
                dve.wait_ge(transposed.sem, transposed.after(g - 2))
                for t in range(BT):
                    last = dve.tensor_scalar(x_n[:, u, t], x_in[:, c, t], mean_var[:, u, t, 0:1], inv[:, u, t:t + 1],
                                             ALU.subtract, ALU.mult)
                last.then_inc(normed.sem, 1)

            def before():
                statistics(0, 0)
                statistics(0, 1)
                normalise(0, 0)

            def turn(b, c, has):
                g, u = b * BLOCKS_B + c, c % 2
                v = b * (BLOCKS_B // 2) + c // 2
                if has(1):
                    normalise(*block_at(b, c, 1))
                if has(2):
                    statistics(*block_at(b, c, 2))
                dve.wait_ge(biased.sem, biased.after(g))
                dve.wait_ge(q_out[u].sem, q_out[u].after(v - 1))
                dve.tensor_copy(q_p[:, u, 0], q_f[:, u]).then_inc(q_split.sem, 1)
                dve.wait_ge(q_split.sem, q_split.after(g - 1) + 1)
                dve.tensor_tensor(q_rest[:], q_f[:, u], q_p[:, u, 0], ALU.subtract).then_inc(q_split.sem, 1)
                dve.wait_ge(projected.sem, projected.after(g))
                for t in range(BT):
                    out = s.v_all[:, bass.ds(b * KV, KV), BT * c + t, 0:HD]
                    last = dve.tensor_tensor(out, p_v[:, KVD * t:KVD * t + KVD].rearrange("p (k d) -> p k d", k=KV),
                                             s.b_v[:].rearrange("p (k d) -> p k d", k=KV), ALU.add)
                last.then_inc(v_ready.sem, 1)
                dve.wait_ge(q_split.sem, q_split.after(g - 1) + 2)
                dve.tensor_copy(q_p[:, u, 1], q_rest[:]).then_inc(q_split.sem, 1)
                dve.wait_ge(q_split.sem, q_split.after(g - 1) + 3)
                dve.tensor_tensor(q_p[:, u, 2], q_rest[:], q_p[:, u, 1], ALU.subtract).then_inc(q_split.sem, 1)
                dve.wait_ge(norms.sem, norms.after(g))
                dve.tensor_reduce(s.norm_max[:, bass.ds(g, 1)], p_norm[0:20, :], AX.X, ALU.max)\
                   .then_inc(norms_read.sem, 1)

            over_blocks(dve, before, turn)

        @block.gpsimd
        def _(pool):
            k_split.open(pool)
            inverted.open(pool)

            def root(b, c):
                g, u = b * BLOCKS_B + c, c % 2
                pool.wait_ge(norm_step.sem, norm_step.after(g))
                pool.wait_ge(normed.sem, normed.after(g - 2))
                inverse_root(pool, s, inv[:, u], mean_var[:, u, :, 1], s.power[:, 0:BT], inverted, g)

            def before():
                root(0, 0)
                root(0, 1)

            def turn(b, c, has):
                g, u = b * BLOCKS_B + c, c % 2
                if has(2):
                    root(*block_at(b, c, 2))
                pool.wait_ge(biased.sem, biased.after(g))
                pool.wait_ge(k_out[u].sem, k_out[u].after(b * (BLOCKS_B // 2) + c // 2 - 1))
                apart(pool, s)
                pool.tensor_copy(k_p[:, u, 0], k_f[:, u]).then_inc(k_split.sem, 1)
                pool.wait_ge(k_split.sem, k_split.after(g - 1) + 1)
                pool.tensor_tensor(k_rest[:], k_f[:, u], k_p[:, u, 0], ALU.subtract).then_inc(k_split.sem, 1)
                pool.wait_ge(k_split.sem, k_split.after(g - 1) + 2)
                apart(pool, s)
                pool.tensor_copy(k_p[:, u, 1], k_rest[:]).then_inc(k_split.sem, 1)
                pool.wait_ge(k_split.sem, k_split.after(g - 1) + 3)
                pool.tensor_tensor(k_p[:, u, 2], k_rest[:], k_p[:, u, 1], ALU.subtract).then_inc(k_split.sem, 1)

            over_blocks(pool, before, turn)

        @block.scalar
        def _(act):
            for made in (x_t_ready, biased, squared):
                made.open(act)

            def take_x(b, c):
                g, u = b * BLOCKS_B + c, c % 2
                act.wait_ge(transposed.sem, transposed.after(g))
                act.wait_ge(projected.sem, projected.after(g - 2))
                act.activation(x_t[:, u], p_t[:], ACT.Copy).then_inc(x_t_ready.sem, 1)

            def before():
                take_x(0, 0)

            def turn(b, c, has):
                g, u = b * BLOCKS_B + c, c % 2
                act.wait_ge(qk_projected.sem, qk_projected.after(g))
                act.wait_ge(q_split.sem, q_split.after(g - 2))
                act.wait_ge(k_split.sem, k_split.after(g - 2))
                for m in range(HALVES):
                    act.activation(q_f[:, u, m], p_q[:, m, :], ACT.Identity, bias=s.b_q[:, m:m + 1])
                act.activation(k_f[:, u], p_k[0:KVD, :], ACT.Identity, bias=s.b_k[:]).then_inc(biased.sem, 1)
                act.wait_ge(biased.sem, biased.after(g))
                act.wait_ge(norms.sem, norms.after(g - 1))
                act.activation(q_sq[:], q_f[:, u], ACT.Square)
                act.activation(k_sq[:], k_f[:, u], ACT.Square).then_inc(squared.sem, 1)
                if has(1):
                    take_x(*block_at(b, c, 1))

            over_blocks(act, before, turn)

        @block.tensor
        def _(pe):
            for made in (transposed, qk_projected, projected, norms):
                made.open(pe)

            def turn_x(b, c):
                g, u = b * BLOCKS_B + c, c % 2
                pe.wait_ge(normed.sem, normed.after(g))
                pe.wait_ge(x_t_ready.sem, x_t_ready.after(g - 1))
                for t in range(BT):
                    for h in range(HALVES):
                        last = nc.tensor.transpose(p_t[:, h, P * t:P * t + P], x_n[:, u, t, P * h:P * h + P], s.ident[:])
                last.then_inc(transposed.sem, 1)

            def before():
                turn_x(0, 0)

            def turn(b, c, has):
                g, u = b * BLOCKS_B + c, c % 2
                pe.wait_ge(x_t_ready.sem, x_t_ready.after(g))
                pe.wait_ge(biased.sem, biased.after(g - 1))
                for m in range(HALVES):
                    for k in range(HALVES):
                        nc.tensor.matmul(p_q[:, m, :], s.w_q[:, k, P * m:P * m + P], x_t[:, u, k, :],
                                         start=(k == 0), stop=(k == HALVES - 1))
                for k in range(HALVES):
                    last = nc.tensor.matmul(p_k[0:KVD, :], s.w_k[:, k, :], x_t[:, u, k, :],
                                            start=(k == 0), stop=(k == HALVES - 1))
                last.then_inc(qk_projected.sem, 1)
                pe.wait_ge(v_ready.sem, v_ready.after(g - 1))
                for t in range(BT):
                    for k in range(HALVES):
                        last = nc.tensor.matmul(p_v[:, KVD * t:KVD * t + KVD], x_t[:, u, k, P * t:P * t + P],
                                                s.w_v[:, k, :], start=(k == 0), stop=(k == HALVES - 1))
                last.then_inc(projected.sem, 1)
                if has(1):
                    turn_x(*block_at(b, c, 1))
                pe.wait_ge(squared.sem, squared.after(g))
                pe.wait_ge(norms_read.sem, norms_read.after(g - 1))
                nc.tensor.matmul(p_norm[0:20, :], s.norm_sel[:, 0, :], q_sq[:, 0, :], start=True, stop=False)
                nc.tensor.matmul(p_norm[0:20, :], s.norm_sel[:, 1, :], q_sq[:, 1, :], start=False, stop=False)
                nc.tensor.matmul(p_norm[0:20, :], s.norm_sel[0:KVD, 2, :], k_sq[:], start=False, stop=True)\
                  .then_inc(norms.sem, 1)

            over_blocks(pe, before, turn)


def bound_scores(nc, s):
    with nc.sbuf_tensor("norm_all", [20, 1], fp32) as norm_all, nc.sbuf_tensor("norm_top", [1, 4], fp32) as norm_top, \
            nc.psum_tensor("norm_row", [1, 20], fp32) as norm_row, nc.semaphore("bounded") as bounded, \
            nc.semaphore("norm_turned") as turned, nc.Block() as block:

        @block.tensor
        def _(pe):
            pe.wait_ge(bounded, 1)
            nc.tensor.matmul(norm_row[:], norm_all[:], s.ident[0:20, 0:20], start=True, stop=True).then_inc(turned, 1)

        @block.vector
        def _(dve):
            dve.tensor_reduce(norm_all[:], s.norm_max[:], AX.X, ALU.max).then_inc(bounded, 1)
            dve.wait_ge(turned, 1)
            dve.tensor_reduce(norm_top[:, 0:1], norm_row[:, 0:HEADS], AX.X, ALU.max)
            dve.tensor_reduce(norm_top[:, 1:2], norm_row[:, HEADS:], AX.X, ALU.max).then_inc(bounded, 1)
            dve.wait_ge(bounded, 2)
            dve.tensor_tensor(norm_top[:, 2:3], norm_top[:, 0:1], norm_top[:, 1:2], ALU.mult).then_inc(bounded, 1)
            dve.wait_ge(bounded, 3)
            dve.tensor_scalar(norm_top[:, 3:4], norm_top[:, 2:3], (GUARD / A_SCALE) ** 2, None, ALU.is_le).then_inc(bounded, 1)
            dve.wait_ge(bounded, 4)
            dve.tensor_scalar(s.loose[:], norm_top[:, 3:4], -1.0, 1.0, ALU.mult, ALU.add).then_inc(bounded, 1)
            dve.wait_ge(bounded, 5)


def largest_scores(nc, s):
    PAIRS = BATCH * KV
    with ExitStack() as ctx:
        def sb(name, shape, dt=fp32):
            return ctx.enter_context(nc.sbuf_tensor(name, shape, dt))

        def steps(name, per=1, lead=2):
            return Steps(ctx.enter_context(nc.semaphore(name)), per, lead)

        q_stack = sb("m_q_stack", [STACK, GROUP, SEQ], bf16)
        ahead, masked = sb("ahead", [P, P]), sb("m_masked", [P, P])
        found = sb("found", [P, 2, GROUP, TILES_B])
        least = sb("least", [P, GROUP * TILES_B])
        rest = sb("m_rest", [GROUP * TILES_B, P])
        parts = sb("m_parts", [GROUP * TILES_B, 2, P], bf16)
        scores = ctx.enter_context(nc.psum_tensor("m_scores", [P, SEQ], fp32))
        turned = ctx.enter_context(nc.psum_tensor("m_turned", [GROUP * TILES_B, P], fp32))
        jobs = [(h, t) for h in range(GROUP) for t in range(TILES_B)]
        filled = ctx.enter_context(nc.semaphore("m_filled"))
        loaded, stored = steps("m_loaded", 16 * 2 * SLOTS), steps("m_stored", 16)
        scored, masked_done, taken = steps("m_scored"), steps("m_masked_done"), steps("m_taken")
        joined, split, flipped = steps("m_joined", 2), steps("m_split", 3), steps("m_flipped")
        block = ctx.enter_context(nc.Block())

        @block.gpsimd
        def _(pool):
            with pool.If(pool.value_load(s.loose[:], min_val=0, max_val=1) > 0):
                pool.memset(ahead[:], 0.0).then_inc(filled, 1)
                pool.wait_ge(filled, 1)
                pool.affine_select(out=ahead[:], in_=ahead[:], compare_op=ALU.is_ge, fill=FAR, base=0, pattern=[[-1, P]],
                                   channel_multiplier=1).then_inc(filled, 1)
            with pool.Else():
                pass

        @block.sync
        def _(sp):
            with sp.If(sp.value_load(s.loose[:], min_val=0, max_val=1) > 0):
                loaded.open(sp)
                stored.open(sp)
                with sp.Fori(0, PAIRS) as j:
                    sp.wait_ge(joined.sem, joined.after(j - 1))
                    for n in range(SLOTS):
                        rows = slice(HD * n, HD * n + HD)
                        sp.dma_start(s.k_stack[rows, 0, :], s.k_rows[K_PART[n], bass.ds(j, 1)].rearrange("a p n -> p (a n)"))\
                          .then_inc(loaded.sem, 16)
                        sp.dma_start(q_stack[rows], s.q_rows[Q_PART[n], bass.ds(j * GROUP, GROUP)].rearrange("h p n -> p h n"))\
                          .then_inc(loaded.sem, 16)
                    sp.wait_ge(split.sem, split.after(j))
                    sp.dma_start(s.d_shift[:, bass.ds(j * GROUP, GROUP)].rearrange("r h (t n) -> (h t) r n", n=P), parts[:])\
                      .then_inc(stored.sem, 16)
                sp.wait_ge(stored.sem, stored.after(PAIRS - 1))
            with sp.Else():
                pass

        @block.tensor
        def _(pe):
            with pe.If(pe.value_load(s.loose[:], min_val=0, max_val=1) > 0):
                scored.open(pe)
                flipped.open(pe)
                with pe.Fori(0, PAIRS) as j:
                    pe.wait_ge(loaded.sem, loaded.after(j))
                    for n, (h, t) in enumerate(jobs):
                        pe.wait_ge(taken.sem, taken.after(j * len(jobs) + n - 1))
                        keys = P * (t + 1)
                        for at in range(0, keys, BLOCK):
                            width = min(BLOCK, keys - at)
                            last = nc.tensor.matmul(scores[:, at:at + width], q_stack[:, h, P * t:P * t + P],
                                                    s.k_stack[0:STACK, 0, at:at + width], start=True, stop=True)
                        last.then_inc(scored.sem, 1)
                    pe.wait_ge(joined.sem, joined.after(j))
                    pe.wait_ge(split.sem, split.after(j - 1))
                    apart(pe, s)
                    nc.tensor.transpose(turned[:], least[:], s.ident[:]).then_inc(flipped.sem, 1)
            with pe.Else():
                pass

        @block.vector
        def _(dve):
            with dve.If(dve.value_load(s.loose[:], min_val=0, max_val=1) > 0):
                for made in (masked_done, taken, joined, split):
                    made.open(dve)
                dve.wait_ge(filled, 2)
                dve.memset(found[:], FAR).then_inc(filled, 1)
                dve.wait_ge(filled, 3)
                with dve.Fori(0, PAIRS) as j:
                    for n, (h, t) in enumerate(jobs):
                        job = j * len(jobs) + n
                        own = P * t
                        dve.wait_ge(scored.sem, scored.after(job))
                        dve.wait_ge(taken.sem, taken.after(job - 1))
                        dve.tensor_tensor(masked[:], scores[:, own:own + P], ahead[:], ALU.add).then_inc(masked_done.sem, 1)
                        dve.wait_ge(masked_done.sem, masked_done.after(job))
                        if t:
                            dve.tensor_reduce(found[:, 1, h, t:t + 1], scores[:, 0:own], AX.X, ALU.max)
                        dve.tensor_reduce(found[:, 0, h, t:t + 1], masked[:], AX.X, ALU.max).then_inc(taken.sem, 1)
                    dve.wait_ge(taken.sem, taken.after(j * len(jobs) + len(jobs) - 1))
                    dve.wait_ge(flipped.sem, flipped.after(j - 1))
                    dve.tensor_tensor(least[:], found[:, 0].rearrange("p h t -> p (h t)"), found[:, 1].rearrange("p h t -> p (h t)"), ALU.max)\
                       .then_inc(joined.sem, 1)
                    dve.wait_ge(joined.sem, joined.after(j - 1) + 1)
                    dve.tensor_scalar(least[:], least[:], -1.0, None, ALU.mult).then_inc(joined.sem, 1)
                    dve.wait_ge(flipped.sem, flipped.after(j))
                    dve.wait_ge(stored.sem, stored.after(j - 1))
                    dve.tensor_copy(parts[:, 0], turned[:]).then_inc(split.sem, 1)
                    dve.wait_ge(split.sem, split.after(j - 1) + 1)
                    dve.tensor_tensor(rest[:], turned[:], parts[:, 0], ALU.subtract).then_inc(split.sem, 1)
                    dve.wait_ge(split.sem, split.after(j - 1) + 2)
                    dve.tensor_copy(parts[:, 1], rest[:]).then_inc(split.sem, 1)
            with dve.Else():
                pass


def attend(nc, s):
    PAIRS = BATCH * KV
    chunks = [(t, c) for t in reversed(range(BLOCKS_B)) for c in range(BT * t + BT)]
    PER_PAIR = len(chunks)
    BODY = 2 * PER_PAIR
    UNITS = 2 * BODY
    diagonal = {}
    for n in range(BODY):
        t, c = chunks[n % PER_PAIR]
        if c >= BT * t:
            diagonal[n] = len(diagonal)
    DIAGONALS = len(diagonal)
    PROB_SLOTS = 8
    LAG = 2
    with ExitStack() as ctx:
        def sb(name, shape, dt=fp32):
            return ctx.enter_context(nc.sbuf_tensor(name, shape, dt))

        def steps(name, per=1, lead=2):
            return Steps(ctx.enter_context(nc.semaphore(name)), per, lead)

        q_stack = sb("q_stack", [P, 2, GROUP, SEQ], bf16)
        values = sb("values", [P, 2, TILES_B, 2 * HD])
        probs = sb("probs", [P, PROB_SLOTS, 2, BLOCK])
        den = sb("den", [P, 2, BLOCK])
        o_n = sb("o_n", [P, 2, BLOCK])
        scores = ctx.enter_context(nc.psum_tensor("scores", [P, 3, 2, BLOCK], fp32))
        sums = ctx.enter_context(nc.psum_tensor("sums", [P, 2, BLOCK], fp32))

        loaded = [steps(f"pair_loaded_{u}", 16 * (2 * SLOTS + 2)) for u in range(2)]
        scored, exped = steps("scored"), steps("exped", lead=4)
        masked, summed = steps("masked"), steps("summed", lead=BODY)
        divided = steps("divided", 3)
        a_out = [steps(f"a_out_{u}", 16 * GROUP) for u in range(2)]
        block = ctx.enter_context(nc.Block())

        def body():
            for u in range(2):
                for k, (t, c) in enumerate(chunks):
                    yield u * PER_PAIR + k, u, t, c, P * max(0, c - BT * t)

        @block.sync
        def _(sp):
            for made in (*loaded, *a_out):
                made.open(sp)

            def store(i, u):
                for t in reversed(range(BLOCKS_B)):
                    sp.wait_ge(divided.sem, divided.after(i * 2 * BLOCKS_B + u * BLOCKS_B + (BLOCKS_B - 1 - t)))
                    apart(sp, s)
                    for h in range(GROUP):
                        sp.dma_start(s.a_rows[bass.ds(i * 2 + u, 1), h, :, BLOCK * t:BLOCK * t + BLOCK].rearrange("a p n -> p (a n)"),
                                     o_n[2 * HD * h:2 * HD * h + HD, t % 2]).then_inc(a_out[t % 2].sem, 16)

            def load(i, u):
                j = i * 2 + u
                sp.wait_ge(summed.sem, summed.after(i * BODY + (u - 1) * PER_PAIR - 1))
                for n in range(SLOTS):
                    rows = slice(HD * n, HD * n + HD)
                    sp.dma_start(s.k_stack[rows, u, :], s.k_rows[K_PART[n], bass.ds(j, 1)].rearrange("a p n -> p (a n)"))\
                      .then_inc(loaded[u].sem, 16)
                    sp.dma_start(q_stack[rows, u], s.q_rows[Q_PART[n], bass.ds(j * GROUP, GROUP)].rearrange("h p n -> p h n"))\
                      .then_inc(loaded[u].sem, 16)
                sp.dma_start(q_stack[STACK:ROWS, u], s.d_shift[:, bass.ds(j * GROUP, GROUP), :]).then_inc(loaded[u].sem, 16)
                sp.dma_start(values[:, u], s.v_all[:, bass.ds(j, 1)].rearrange("p a t d -> p (a t) d"))\
                  .then_inc(loaded[u].sem, 16)

            load(0, 0)
            with sp.Fori(0, PAIRS // 2 - 1) as i:
                load(i, 1)
                store(i, 0)
                load(i + 1, 0)
                store(i, 1)
            load(PAIRS // 2 - 1, 1)
            store(PAIRS // 2 - 1, 0)
            store(PAIRS // 2 - 1, 1)
            for u in range(2):
                sp.wait_ge(a_out[u].sem, a_out[u].after(PAIRS * BLOCKS_B // 2 - 1))
            sp.wait_ge(s.later_loaded, 6 * 16)

        @block.tensor
        def _(pe):
            summed.open(pe)
            scored.open(pe)

            def score(i, n, u, t, c, n0, loose):
                if n % PER_PAIR == 0:
                    pe.wait_ge(loaded[u].sem, loaded[u].after(i))
                for half in range(2):
                    e = 2 * n + half
                    before = e - 3 if e >= 3 else max(x for x in range(UNITS - 3, UNITS) if x % 3 == e) - UNITS
                    pe.wait_ge(exped.sem, exped.after(i * UNITS + before))
                    for h in range(2):
                        last = nc.tensor.matmul(scores[:, e % 3, h, n0:], s.k_stack[0:ROWS, u, P * c:P * c + P],
                                                q_stack[0:ROWS, u, 2 * half + h, BLOCK * t + n0:BLOCK * t + BLOCK],
                                                start=True, stop=not (loose and c >= BT * t))
                        if loose and c >= BT * t:
                            last = nc.tensor.matmul(scores[:, e % 3, h, n0:n0 + P], s.ident_b[:], s.behind[:], start=False, stop=True)
                    last.then_inc(scored.sem, 1)

            def weigh(i, n, u, t, c, n0, loose):
                pe.wait_ge(exped.sem, exped.after(i * UNITS + 2 * n + 1))
                if c >= BT * t and not loose:
                    pe.wait_ge(masked.sem, masked.after(i * DIAGONALS + diagonal[n]))
                if c == 0:
                    pe.wait_ge(divided.sem, divided.after(i * 2 * BLOCKS_B + u * BLOCKS_B + (BLOCKS_B - 1 - t) - 2))
                for h in range(GROUP):
                    last = nc.tensor.matmul(sums[2 * HD * h:2 * HD * h + 2 * HD, t % 2, n0:], values[:, u, c, :],
                                            probs[:, (2 * n + h // 2) % PROB_SLOTS, h % 2, n0:],
                                            start=(c == 0), stop=(c == BT * t + BT - 1), tile_position=(0, 2 * HD * h))
                last.then_inc(summed.sem, 1)

            def over_pairs(loose):
                with pe.Fori(0, PAIRS // 2) as i:
                    order = list(body())
                    for n, chunk in enumerate(order):
                        score(i, *chunk, loose)
                        if n >= LAG:
                            weigh(i, *order[n - LAG], loose)
                    for chunk in order[-LAG:]:
                        weigh(i, *chunk, loose)

            with pe.If(pe.value_load(s.loose[:], min_val=0, max_val=1) > 0):
                over_pairs(True)
            with pe.Else():
                over_pairs(False)

        @block.scalar
        def _(act):
            exped.open(act)
            with act.Fori(0, PAIRS // 2) as i:
                for n, u, t, c, n0 in body():
                    act.wait_ge(summed.sem, summed.after(i * BODY + n - PROB_SLOTS // 2))
                    for e in (2 * n, 2 * n + 1):
                        act.wait_ge(scored.sem, scored.after(i * UNITS + e))
                        act.activation(probs[:, e % PROB_SLOTS, :, n0:], scores[:, e % 3, :, n0:], ACT.Exp, scale=A_SCALE)\
                           .then_inc(exped.sem, 1)

        @block.gpsimd
        def _(pool):
            masked.open(pool)
            with pool.If(pool.value_load(s.loose[:], min_val=0, max_val=1) > 0):
                pass
            with pool.Else():
                with pool.Fori(0, PAIRS // 2) as i:
                    for n, u, t, c, n0 in body():
                        if c < BT * t:
                            continue
                        for e in (2 * n, 2 * n + 1):
                            pool.wait_ge(exped.sem, exped.after(i * UNITS + e))
                            own = probs[:, e % PROB_SLOTS, :, n0:n0 + P]
                            apart(pool, s)
                            last = pool.affine_select(out=own, in_=own, compare_op=ALU.is_ge, fill=0.0, base=0,
                                                      pattern=[[0, 2], [1, P]], channel_multiplier=-1)
                        last.then_inc(masked.sem, 1)

        @block.vector
        def _(dve):
            divided.open(dve)
            spread = [HD + r % HD for r in range(2 * HD)]
            with dve.Fori(0, PAIRS // 2) as i:
                for n, u, t, c, n0 in body():
                    if c < BT * t + BT - 1:
                        continue
                    tile = i * 2 * BLOCKS_B + u * BLOCKS_B + (BLOCKS_B - 1 - t)
                    dve.wait_ge(summed.sem, summed.after(i * BODY + n))
                    apart(dve, s)
                    dve.stream_shuffle(den[:, 0], sums[:, t % 2], spread).then_inc(divided.sem, 1)
                    dve.wait_ge(divided.sem, divided.after(tile - 1) + 1)
                    dve.reciprocal(den[:, 1], den[:, 0]).then_inc(divided.sem, 1)
                    dve.wait_ge(divided.sem, divided.after(tile - 1) + 2)
                    dve.wait_ge(a_out[t % 2].sem, a_out[t % 2].after(i * BLOCKS_B + (u * BLOCKS_B + BLOCKS_B - 1 - t) // 2 - 1))
                    dve.tensor_tensor(o_n[:, t % 2], sums[:, t % 2], den[:, 1], ALU.mult).then_inc(divided.sem, 1)



def weight_turns(s):
    weights = [(source, target, source.shape[0] // P, source.shape[1] // P) for source, target in (
        (s.d_wqkv, s.w_qkv_t), (s.d_wq_h, s.wq_h_t), (s.d_wkv_h, s.wkv_h_t),
        (s.d_wout_l, s.wout_l_t), (s.d_wout_h, s.wout_h_t))]
    turns = []
    for _, target, n, m in weights:
        for r in range(n):
            turns.append((len(turns), target, r, m))
    return weights, turns


def normalise_tiles(dve, out, mean_var, inv, x):
    for t in range(BT):
        last = dve.tensor_scalar(out[:, t], x[:, t], mean_var[:, t, 0:1], inv[:, t:t + 1], ALU.subtract, ALU.mult)
    return last


def merge(nc, s):
    weights, turns = weight_turns(s)
    PER_BLOCK = -(-len(turns) // BLOCKS_B)
    with ExitStack() as ctx:
        def sb(name, shape, dt=fp32):
            return ctx.enter_context(nc.sbuf_tensor(name, shape, dt))

        def steps(name, per=1, lead=4):
            return Steps(ctx.enter_context(nc.semaphore(name)), per, lead)

        a_t = sb("a_t", [P, BLOCKS_B, HALVES, BLOCK])
        x_in = sb("x_in2", [P, BLOCKS_B, BT, DIM])
        y = sb("y", [P, BT, DIM])
        x_1 = sb("x_1", [P, 2, BT, DIM])
        h_n = sb("h_n", [P, 2, BT, DIM])
        u_n = sb("u_n", [P, BT, DIM])
        u_t = sb("u_turned", [P, 2, HALVES, BLOCK])
        stats = sb("stats2", [P, 3, BT, 6])
        mean_var = sb("mean_var2", [P, 3, BT, 2])
        inv, shift = sb("inv2", [P, 3, BT]), sb("u_shift", [P, BT])
        scratch, block_s = sb("route_product", [P, BT, 2, DIM]), sb("block_s", [P, 2, BT])
        w_o, b_o, ln_w, ln_b, rt = s.w_o, s.b_o, s.ln_w, s.ln_b, s.rt
        one = sb("one", [1, P])
        p_y = ctx.enter_context(nc.psum_tensor("p_y", [P, 2, BT, DIM], fp32))
        p_u = ctx.enter_context(nc.psum_tensor("p_u", [P, HALVES, BLOCK], fp32))

        w_rows = sb("w_rows", [P, len(turns), 4 * P])
        w_turned = ctx.enter_context(nc.psum_tensor("w_turned", [P, 2, 4, P], fp32))
        rows_loaded, w_done = (ctx.enter_context(nc.semaphore(name)) for name in ("w_rows_loaded", "w_turned_done"))
        w_copied = ctx.enter_context(nc.semaphore("w_copied"))
        one_made = ctx.enter_context(nc.semaphore("one_made"))
        loaded = [steps(f"block_loaded_{c}", 32) for c in range(BLOCKS_B)]
        x1_out = [steps(f"x1_out_{u}", 32) for u in range(2)]
        u_out = [steps(f"u_out_{u}", 16) for u in range(2)]
        y_stats = steps("y_stats", 2)
        x1_made = steps("x1_made", 4)
        h_made = steps("h_made", 3)
        multiplied, routed = steps("multiplied"), steps("routed")
        y_root, x1_root, h_root = steps("y_root", 2), steps("x1_root", 2), steps("h_root", 4)
        projected, turned, u_made, u_ready = steps("o_projected"), steps("u_turned_done"), steps("u_made"), steps("u_ready")
        block = ctx.enter_context(nc.Block())

        @block.sync
        def _(sp):
            for m in (*loaded, *x1_out, *u_out):
                m.open(sp)
            def load(b, c):
                g = b * BLOCKS_B + c
                sp.wait_ge(projected.sem, projected.after(g - BLOCKS_B))
                apart(sp, s)
                sp.wait_ge(x1_made.sem, x1_made.after(g - BLOCKS_B))
                sp.dma_start(a_t[:, c], s.d_attended[bass.ds(b * HALVES, HALVES), :, BLOCK * c:BLOCK * c + BLOCK]
                             .rearrange("k p n -> p k n")).then_inc(loaded[c].sem, 16)
                sp.dma_start(x_in[:, c], s.d_x[bass.ds(b * TILES_B + BT * c, BT)].rearrange("t p d -> p t d"))\
                  .then_inc(loaded[c].sem, 16)

            def before():
                for c in range(3):
                    load(0, c)
                at = 0
                for source, _, n, m in weights:
                    sp.dma_start(w_rows[:, at:at + n, 0:m * P], source.rearrange("(r p) n -> p r n", p=P)).then_inc(rows_loaded, 16)
                    at += n

            def turn(b, c, has):
                g, u = b * BLOCKS_B + c, c % 2
                if has(3):
                    load(*block_at(b, c, 3))
                tiles = bass.ds(b * TILES_B + BT * c, BT)
                sp.wait_ge(h_made.sem, h_made.after(g - 1) + 1)
                apart(sp, s)
                sp.dma_start(s.d_x1[tiles].rearrange("t p d -> p t d"), x_1[:, u]).then_inc(x1_out[u].sem, 16)
                sp.dma_start(s.d_h[tiles].rearrange("t p d -> p t d"), h_n[:, u]).then_inc(x1_out[u].sem, 16)
                sp.wait_ge(u_ready.sem, u_ready.after(g))
                apart(sp, s)
                sp.dma_start(s.d_u_t[:, :, bass.ds(b * SEQ + BLOCK * c, BLOCK)], u_t[:, u]).then_inc(u_out[u].sem, 16)

            over_blocks(sp, before, turn)
            for u in range(2):
                sp.wait_ge(x1_out[u].sem, x1_out[u].after(BATCH * BLOCKS_B // 2 - 1))
                sp.wait_ge(u_out[u].sem, u_out[u].after(BATCH * BLOCKS_B // 2 - 1))

        @block.tensor
        def _(pe):
            projected.open(pe)
            turned.open(pe)
            pe.wait_ge(one_made, 1)

            def out_projection(b, c):
                g, u = b * BLOCKS_B + c, c % 2
                pe.wait_ge(loaded[c].sem, loaded[c].after(b))
                pe.wait_ge(x1_made.sem, x1_made.after(g - 3) + 1)
                for t in range(BT):
                    for k in range(HALVES):
                        nc.tensor.matmul(p_y[:, u, t], a_t[:, c, k, P * t:P * t + P], w_o[:, k], start=(k == 0), stop=False)
                    last = nc.tensor.matmul(p_y[:, u, t], one[:], b_o[:], start=False, stop=True)
                last.then_inc(projected.sem, 1)

            def before():
                out_projection(0, 0)
                out_projection(0, 1)

            def turn(b, c, has):
                g = b * BLOCKS_B + c
                if has(2):
                    out_projection(*block_at(b, c, 2))
                pe.wait_ge(u_made.sem, u_made.after(g))
                pe.wait_ge(u_ready.sem, u_ready.after(g - 1))
                for t in range(BT):
                    for k in range(HALVES):
                        last = nc.tensor.transpose(p_u[:, k, P * t:P * t + P], u_n[:, t, P * k:P * k + P], s.ident[:])
                last.then_inc(turned.sem, 1)
                if not has(BLOCKS_B):
                    turn_weights(c)

            def turn_weights(c):
                pe.wait_ge(rows_loaded, 16 * len(weights))
                for k, (row, _, _, m) in enumerate(turns[PER_BLOCK * c:PER_BLOCK * (c + 1)], PER_BLOCK * c):
                    if k >= 2:
                        pe.wait_ge(w_copied, k - 1)
                    for n in range(m):
                        last = nc.tensor.transpose(w_turned[:, k % 2, n], w_rows[:, row, P * n:P * n + P], s.ident[:])
                    last.then_inc(w_done, 1)

            over_blocks(pe, before, turn)

        @block.scalar
        def _(act):
            u_made.open(act)
            u_ready.open(act)

            def turn(b, c, has):
                g, u, v = b * BLOCKS_B + c, c % 2, b * (BLOCKS_B // 2) + c // 2
                act.wait_ge(h_root.sem, h_root.after(g))
                act.wait_ge(turned.sem, turned.after(g - 1))
                for t in range(BT):
                    last = act.activation(u_n[:, t], h_n[:, u, t], ACT.Identity, scale=inv[:, 2, t:t + 1], bias=shift[:, t:t + 1])
                last.then_inc(u_made.sem, 1)
                act.wait_ge(turned.sem, turned.after(g))
                act.wait_ge(u_out[u].sem, u_out[u].after(v - 1))
                for k in range(HALVES):
                    last = act.activation(u_t[:, u, k], p_u[:, k], ACT.Identity, scale=ln_w[:, k:k + 1], bias=ln_b[:, k:k + 1])
                last.then_inc(u_ready.sem, 1)
                if not has(BLOCKS_B):
                    take_weights(c)

            def take_weights(c):
                for k, (_, target, row, m) in enumerate(turns[PER_BLOCK * c:PER_BLOCK * (c + 1)], PER_BLOCK * c):
                    act.wait_ge(w_done, k + 1)
                    out, turned_w = target[:, :, P * row:P * row + P] if target is not s.wkv_h_t else target[:, :, :, row], w_turned[:, k % 2, 0:m]
                    if target is s.wkv_h_t:
                        turned_w = turned_w.rearrange("p c (a d) -> p c a d", a=2)
                    act.activation(out, turned_w, ACT.Copy).then_inc(w_copied, 1)

            over_blocks(act, lambda: None, turn)

        @block.gpsimd
        def _(pool):
            for made in (y_root, x1_root, h_root):
                made.open(pool)
            pool.memset(one[:], 1.0).then_inc(one_made, 1)

            def y_inverse(b, c):
                g = b * BLOCKS_B + c
                pool.wait_ge(y_stats.sem, y_stats.after(g))
                inverse_root(pool, s, inv[:, 0], mean_var[:, 0, :, 1], s.power[:, 0:BT], y_root, g)

            def x1_inverse(b, c):
                g = b * BLOCKS_B + c
                pool.wait_ge(x1_made.sem, x1_made.after(g))
                inverse_root(pool, s, inv[:, 1], mean_var[:, 1, :, 1], s.power[:, 0:BT], x1_root, g)

            def h_inverse(b, c):
                g = b * BLOCKS_B + c
                pool.wait_ge(h_made.sem, h_made.after(g))
                pool.wait_ge(u_made.sem, u_made.after(g - 1))
                apart(pool, s)
                pool.tensor_scalar(inv[:, 2], mean_var[:, 2, :, 1], EPS, None, ALU.add).then_inc(h_root.sem, 1)
                pool.wait_ge(h_root.sem, h_root.after(g - 1) + 1)
                pool.tensor_tensor(inv[:, 2], inv[:, 2], s.power[:, 0:BT], ALU.pow).then_inc(h_root.sem, 1)
                pool.wait_ge(h_root.sem, h_root.after(g - 1) + 2)
                pool.tensor_tensor(shift[:], mean_var[:, 2, :, 0], inv[:, 2], ALU.mult).then_inc(h_root.sem, 1)
                pool.wait_ge(h_root.sem, h_root.after(g - 1) + 3)
                apart(pool, s)
                pool.tensor_scalar(shift[:], shift[:], -1.0, None, ALU.mult).then_inc(h_root.sem, 1)

            def before():
                y_inverse(0, 0)
                x1_inverse(0, 0)

            def turn(b, c, has):
                if has(1):
                    y_inverse(*block_at(b, c, 1))
                h_inverse(b, c)
                if has(1):
                    x1_inverse(*block_at(b, c, 1))

            over_blocks(pool, before, turn)

        @block.vector
        def _(dve):
            for made in (y_stats, x1_made, h_made, multiplied, routed):
                made.open(dve)

            def statistics(x, n, chain, base):
                dve.wait_ge(chain.sem, base)
                for t in range(BT):
                    last = dve.bn_stats(stats[:, n, t], x[:, t])
                last.then_inc(chain.sem, 1)
                dve.wait_ge(chain.sem, base + 1)
                apart(dve, s)
                for t in range(BT):
                    last = dve.bn_aggr(mean_var[:, n, t], stats[:, n, t])
                last.then_inc(chain.sem, 1)

            def take_y(b, c):
                g, u = b * BLOCKS_B + c, c % 2
                dve.wait_ge(projected.sem, projected.after(g))
                statistics(p_y[:, u], 0, y_stats, y_stats.after(g - 1))

            def make_x1(b, c):
                g, u, v = b * BLOCKS_B + c, c % 2, b * (BLOCKS_B // 2) + c // 2
                base = x1_made.after(g - 1)
                dve.wait_ge(y_root.sem, y_root.after(g))
                normalise_tiles(dve, y, mean_var[:, 0], inv[:, 0], p_y[:, u]).then_inc(x1_made.sem, 1)
                dve.wait_ge(x1_out[u].sem, x1_out[u].after(v - 1))
                dve.wait_ge(loaded[c].sem, loaded[c].after(b))
                dve.wait_ge(x1_made.sem, base + 1)
                dve.tensor_tensor(x_1[:, u], x_in[:, c], y[:], ALU.add).then_inc(x1_made.sem, 1)
                statistics(x_1[:, u], 1, x1_made, base + 2)

            def make_h(b, c):
                g, u = b * BLOCKS_B + c, c % 2
                dve.wait_ge(x1_root.sem, x1_root.after(g))
                dve.wait_ge(u_made.sem, u_made.after(g - 2))
                normalise_tiles(dve, h_n[:, u], mean_var[:, 1], inv[:, 1], x_1[:, u]).then_inc(h_made.sem, 1)
                dve.wait_ge(h_root.sem, h_root.after(g - 1))
                statistics(h_n[:, u], 2, h_made, h_made.after(g - 1) + 1)

            def route_products(b, c):
                g, u = b * BLOCKS_B + c, c % 2
                dve.wait_ge(routed.sem, routed.after(g - 1))
                for t in range(BT):
                    for r in range(2):
                        last = dve.tensor_tensor_reduce(out=scratch[:, t, r], in0=h_n[:, u, t], in1=rt[:, r], scale=1.0, scalar=0.0,
                                                        op0=ALU.mult, op1=ALU.add, accum_out=block_s[:, r, t:t + 1])
                last.then_inc(multiplied.sem, 1)
                dve.wait_ge(multiplied.sem, multiplied.after(g))
                dve.tensor_copy(s.route_s[:, :, bass.ds(g * BT, BT)], block_s[:]).then_inc(routed.sem, 1)

            def before():
                take_y(0, 0)
                make_x1(0, 0)

            def turn(b, c, has):
                if has(1):
                    take_y(*block_at(b, c, 1))
                make_h(b, c)
                if has(1):
                    make_x1(*block_at(b, c, 1))
                route_products(b, c)

            over_blocks(dve, before, turn)
            dve.wait_ge(routed.sem, routed.after(BATCH * BLOCKS_B - 1))


N_Q, N_KV = 128, 256
ITERATIONS = 50
FETCH = 9.0 / 8.0
ROUTES = 2 * BATCH
DRAWN = (N_Q,) * BATCH + (N_KV,) * BATCH
LOWEST = 104.0
FLOAT_BITS = 31
ROW_TILES = 3


class Memory:
    pass


SLOTS4 = 4
TURN = 6
START = 9
TURNS_R = ITERATIONS - 1
DESCENT_LOOPS = TURNS_R // SLOTS4
DESCENT_FIRST = SLOTS4 - TURNS_R % SLOTS4


def exponents(r, dve, at):
    T = TILES_B
    dve.tensor_tensor(r.t17[:], r.s17[:], over_problems(r.a[:], T + 1), ALU.add).then_inc(r.made.sem, 1)
    dve.wait_ge(r.made.sem, r.made.after(at))
    dve.scalar_tensor_tensor(r.nz17[:], r.t17[:], 0.0, r.s17[:], ALU.max, ALU.subtract).then_inc(r.made.sem, 1)
    dve.wait_ge(r.made.sem, r.made.after(at + 1))
    dve.tensor_tensor(r.w17[:], r.nz17[:], r.nz17[:, :, T:].broadcast_to([P, ROUTES, T + 1]), ALU.subtract).then_inc(r.made.sem, 1)
    dve.tensor_tensor(r.c[:], r.log_k[:], r.nz17[:, :, T], ALU.add).then_inc(r.made.sem, 1)
    dve.wait_ge(r.made.sem, r.made.after(at + 3))


def route_start(nc, s, ctx):
    def sb(name, shape, dt=fp32):
        return ctx.enter_context(nc.sbuf_tensor(name, shape, dt))

    def steps(name, per=1, lead=2):
        return Steps(ctx.enter_context(nc.semaphore(name)), per, lead)

    T = TILES_B
    r = s.r = Memory()
    r.s17, r.t17, r.nz17, r.w17 = (sb(name, [P, ROUTES, T + 1]) for name in ("s17", "t17", "nz17", "w17"))
    r.log_k, r.k_of = sb("log_k", [P, ROUTES]), sb("k_of", [P, ROUTES])
    r.a, r.c = sb("route_a", [P, ROUTES]), sb("route_c", [P, ROUTES])
    r.e, r.part, r.log_sum = sb("route_e", [P, ROUTES, T]), sb("route_part", [P, ROUTES]), sb("log_sum", [P, ROUTES])
    r.ones = sb("ones", [P, P])
    r.made = steps("route_step")
    r.exped, r.summed, r.logged = steps("r_exped"), steps("r_summed"), steps("r_logged")
    with nc.sbuf_tensor("top", [P, ROUTES], fp32) as top, nc.sbuf_tensor("top8", [ROUTES, 1], fp32) as top8, \
            nc.sbuf_tensor("top_diag", [ROUTES, ROUTES], fp32) as top_diag, nc.psum_tensor("p_top", [P, 512], fp32) as p_sum, \
            nc.semaphore("ones_made") as ones_made, nc.Block() as block:

        @block.gpsimd
        def _(pool):
            pool.memset(r.ones[:], 1.0).then_inc(ones_made, 1)

        @block.scalar
        def _(act):
            r.exped.open(act)
            r.logged.open(act)
            act.wait_ge(r.made.sem, r.made.after(START - 2))
            act.activation(r.e[:], r.w17[:, :, 0:T], ACT.Exp, scale=-1.0).then_inc(r.exped.sem, 1)

        @block.tensor
        def _(pe):
            r.summed.open(pe)
            pe.wait_ge(ones_made, 1)
            pe.wait_ge(r.made.sem, r.made.after(1))
            nc.tensor.transpose(p_sum[0:ROUTES, 0:P], top[:], s.ident[:]).then_inc(r.summed.sem, 1)
            pe.wait_ge(r.made.sem, r.made.after(3))
            nc.tensor.matmul(p_sum[:, 0:ROUTES], r.ones[0:ROUTES, :], top_diag[:], start=True, stop=True).then_inc(r.summed.sem, 1)

        @block.vector
        def _(dve):
            r.made.open(dve)

            def step(instruction, at):
                instruction.then_inc(r.made.sem, 1)
                dve.wait_ge(r.made.sem, r.made.after(at))

            scores = r.s17[:, :, 0:T]
            step(dve.tensor_copy(scores, s.route_s[:].rearrange("p r (b t) -> p (r b) t", b=BATCH)), 0)
            step(dve.tensor_reduce(top[:], scores, AX.X, ALU.max), 1)
            dve.wait_ge(r.summed.sem, r.summed.after(0))
            step(dve.tensor_reduce(top8[:], p_sum[0:ROUTES, 0:P], AX.X, ALU.max), 2)
            step(dve.tensor_scalar(top_diag[:], s.ident[0:ROUTES, 0:ROUTES], top8[:], None, ALU.mult), 3)
            dve.wait_ge(r.summed.sem, r.summed.after(1))
            for n, k in ((0, N_Q), (1, N_KV)):
                some = slice(n * BATCH, (n + 1) * BATCH)
                log = float(np.log(np.float32(min(k * FETCH, float(SEQ)))))
                dve.memset(r.log_k[:, some], log)
                dve.memset(r.k_of[:, some], float(k))
                dve.memset(r.a[:, some], float(np.float32(log) - np.log(np.float32(SEQ))))
            step(dve.tensor_copy(r.s17[:, :, T:T + 1], p_sum[:, 0:ROUTES].rearrange("p (r a) -> p r a", a=1)), 4)
            exponents(r, dve, 5)


def over_problems(v, n):
    return v.rearrange("p (r a) -> p r a", a=1).broadcast_to([P, ROUTES, n])


WINDOW, L_HEADS, L_HD = 64, 8, 64
L_INNER = L_HEADS * L_HD
L_SCALE = L_HD ** -0.5
PAIR_CHUNKS = L_INNER // P
HALF_HEADS = L_HEADS // 2
OUTSIDE = -1e30


def local(nc, s):
    r = s.r
    with ExitStack() as ctx:
        def sb(name, shape, dt=fp32):
            return ctx.enter_context(nc.sbuf_tensor(name, shape, dt))

        def ps(name, shape):
            return ctx.enter_context(nc.psum_tensor(name, shape, fp32))

        def steps(name, per=1, lead=4):
            return Steps(ctx.enter_context(nc.semaphore(name)), per, lead)

        EVEN, ODD = slice(0, WINDOW), slice(WINDOW, P)
        u_in = sb("u_in", [P, SLOTS4, HALVES, P])
        x1_in = sb("x1_in", [P, SLOTS4, DIM])
        q_pad = sb("q_pad", [P, SLOTS4, L_HEADS, P])
        k_window = sb("k_window", [P, SLOTS4, PAIR_CHUNKS, 2 * P])
        v_main = sb("v_main", [P, SLOTS4, L_HEADS, L_HD])
        v_side = sb("v_side", [P, SLOTS4, L_HEADS, L_HD])
        edge = sb("edge", [P, TILES])
        m_main, m_side = sb("m_main", [P, HALF_HEADS]), sb("m_side", [P, HALF_HEADS])
        m_all, m_edge = sb("m_all", [P, HALF_HEADS]), sb("m_edge", [P, HALF_HEADS])
        z = sb("z", [P, 2, HALF_HEADS, 2 * P])
        probs = sb("l_probs", [P, 2, HALF_HEADS, 2 * P])
        probs_t = sb("probs_t", [P, 2, HALF_HEADS, 2, P])
        den, share = sb("l_den", [P, 2, HALF_HEADS]), sb("l_share", [P, 2, HALF_HEADS])
        diagonal = sb("diagonal", [P, 2, HALF_HEADS, P])
        o_t = sb("o_t", [P, PAIR_CHUNKS, P])
        light = sb("light_rows", [P, 2, DIM])
        y = sb("l_y", [P, DIM])
        stats, mean_var, inv = sb("stats3", [P, 6]), sb("mean_var3", [P, 2]), sb("inv3", [P, 1])
        rows = sb("out_rows", [P, 2, DIM])
        null_q = sb("null_q", [P, DIM])
        p_q, p_k, p_v = ps("p_q3", [P, BLOCK]), ps("p_k3", [P, BLOCK]), ps("p_v3", [P, BLOCK])
        p_s = ps("p_s", [P, HALF_HEADS, 2 * P])
        p_p = ps("p_p", [P, HALF_HEADS, 2, P])
        p_o = ps("p_o", [P, PAIR_CHUNKS, P])
        p_y, p_log = p_v[:, 0:DIM], p_v[:, DIM:DIM + ROUTES]

        filled = ctx.enter_context(nc.semaphore("l_filled"))
        null_loaded = ctx.enter_context(nc.semaphore("null_loaded"))
        u_loaded = [steps(f"u_loaded_{k}", 16, 1) for k in range(SLOTS4)]
        x1_loaded = [steps(f"x1_loaded_{k}", 16, 1) for k in range(SLOTS4)]
        light_out = [steps(f"light_out_{k}", 16, 1) for k in range(2)]
        out_out = [steps(f"out_out_{k}", 16, 1) for k in range(2)]
        qk_done, v_done = steps("qk_done"), steps("v_done")
        q_ready, k_main, k_sides = steps("q_ready"), steps("k_main"), steps("k_sides")
        v_ready, v_sides = steps("v_main_ready"), steps("v_sides_ready")
        scored, z_ready, exped = steps("l_scored"), steps("z_ready"), steps("l_exped")
        diagonal_ready, p_turned, p_ready, summed = steps("diagonal_ready"), steps("p_turned"), steps("p_ready"), steps("l_summed", lead=8)
        o_t_ready, y_done, light_ready = steps("o_t_ready"), steps("y_done"), steps("light_ready")
        G_STEPS, F_STEPS = 4, 4
        g_chain = steps("g_chain", G_STEPS)
        f_chain = steps("f_chain", F_STEPS)
        inverted, rows_ready = steps("inverted3", 2), steps("rows_ready")
        r_chain = steps("r_chain")
        pool_filled = ctx.enter_context(nc.semaphore("l_pool_filled"))
        FILLS = 12
        block = ctx.enter_context(nc.Block())
        TURNS = TILES // SLOTS4

        def at(i, k, by):
            return i + (k + by) // SLOTS4, (k + by) % SLOTS4

        def loop(eng, before, turn, after):
            before()
            for k in range(SLOTS4):
                turn(0, k, lambda by, k=k: k + by >= 0, k >= DESCENT_FIRST)
            with eng.Fori(1, 1 + DESCENT_LOOPS) as i:
                for k in range(SLOTS4):
                    turn(i, k, lambda by: True, True)
            with eng.Fori(1 + DESCENT_LOOPS, TURNS - 1) as i:
                for k in range(SLOTS4):
                    turn(i, k, lambda by: True, False)
            for k in range(SLOTS4):
                turn(TURNS - 1, k, lambda by, k=k: k + by < SLOTS4, False)
            after(*at(TURNS, 0, 0))

        @block.sync
        def _(sp):
            for made in (*u_loaded, *x1_loaded, *light_out, *out_out):
                made.open(sp)
            sp.dma_start(null_q[:], s.d_null_q.rearrange("(a n) -> a n", a=1).broadcast_to([P, DIM])).then_inc(null_loaded, 16)

            def load_u(i, k):
                n = i * SLOTS4 + k
                sp.wait_ge(v_done.sem, v_done.after(n - SLOTS4))
                sp.dma_start(u_in[:, k], s.d_u_t[:, :, bass.ds(n * P, P)]).then_inc(u_loaded[k].sem, 16)

            def load_x1(i, k):
                n = i * SLOTS4 + k
                sp.wait_ge(rows_ready.sem, rows_ready.after(n - SLOTS4))
                sp.dma_start(x1_in[:, k], s.d_x1[bass.ds(n, 1)].rearrange("a p d -> p (a d)")).then_inc(x1_loaded[k].sem, 16)

            def store(i, k):
                m = i * SLOTS4 + k
                sp.wait_ge(light_ready.sem, light_ready.after(m))
                sp.dma_start(s.d_light[bass.ds(m, 1)].rearrange("a p d -> p (a d)"), light[:, k % 2]).then_inc(light_out[k % 2].sem, 16)
                sp.wait_ge(rows_ready.sem, rows_ready.after(m))
                sp.dma_start(s.d_out[bass.ds(m, 1)].rearrange("a p d -> p (a d)"), rows[:, k % 2]).then_inc(out_out[k % 2].sem, 16)

            def turn(i, k, has, descends):
                if has(3):
                    load_u(*at(i, k, 3))
                if has(1):
                    load_x1(*at(i, k, 1))
                if has(-1):
                    store(*at(i, k, -1))

            def before():
                for k in range(3):
                    load_u(0, k)
                load_x1(0, 0)

            def after(i, k):
                store(*at(i, k, -1))
                for k in range(2):
                    sp.wait_ge(light_out[k].sem, light_out[k].after(TILES // 2 - 1))
                    sp.wait_ge(out_out[k].sem, out_out[k].after(TILES // 2 - 1))

            loop(sp, before, turn, after)

        @block.tensor
        def _(pe):
            for made in (qk_done, v_done, scored, p_turned, summed, y_done):
                made.open(pe)
            pe.wait_ge(filled, FILLS)
            pe.wait_ge(pool_filled, SLOTS4)

            def project_qk(i, k):
                n = i * SLOTS4 + k
                pe.wait_ge(u_loaded[k].sem, u_loaded[k].after(i))
                pe.wait_ge(q_ready.sem, q_ready.after(n - 1))
                pe.wait_ge(k_main.sem, k_main.after(n - 1))
                for out, first in ((p_q, 0), (p_k, L_INNER)):
                    for c in range(PAIR_CHUNKS):
                        for h in range(HALVES):
                            last = nc.tensor.matmul(out[:, P * c:P * c + P], s.w_qkv_t[:, h, first + P * c:first + P * c + P],
                                                    u_in[:, k, h], start=(h == 0), stop=(h == HALVES - 1))
                last.then_inc(qk_done.sem, 1)

            def project_v(i, k):
                n = i * SLOTS4 + k
                pe.wait_ge(v_ready.sem, v_ready.after(n - 1))
                pe.wait_ge(v_sides.sem, v_sides.after(n - 1))
                pe.wait_ge(light_ready.sem, light_ready.after(n - 3))
                for h in range(HALVES):
                    last = nc.tensor.matmul(p_v[:], u_in[:, k, h], s.w_qkv_t[:, h, 2 * L_INNER:],
                                            start=(h == 0), stop=(h == HALVES - 1))
                last.then_inc(v_done.sem, 1)

            def score(i, k, g, behind):
                m = i * SLOTS4 + k
                e = 2 * m + g
                pe.wait_ge(q_ready.sem, q_ready.after(m))
                pe.wait_ge(k_sides.sem, k_sides.after(m + 1 if behind else m))
                pe.wait_ge(z_ready.sem, z_ready.after(e - 1))
                for j in range(HALF_HEADS):
                    h = g * HALF_HEADS + j
                    last = nc.tensor.matmul(p_s[:, j], q_pad[:, k, h], k_window[:, k, h // 2], start=True, stop=True)
                last.then_inc(scored.sem, 1)

            def turn_probs(e, g):
                pe.wait_ge(diagonal_ready.sem, diagonal_ready.after(e))
                pe.wait_ge(p_ready.sem, p_ready.after(e - 1))
                for j in range(HALF_HEADS):
                    for side in range(2):
                        last = nc.tensor.matmul(p_p[:, j, side], probs[:, g, j, P * side:P * side + P], diagonal[:, g, j],
                                                start=True, stop=True)
                last.then_inc(p_turned.sem, 1)

            def weigh(e, k, g):
                pe.wait_ge(p_ready.sem, p_ready.after(e))
                apart(pe, s)
                for c in range(2):
                    for a in range(2):
                        j = 2 * c + a
                        h = g * HALF_HEADS + j
                        out = p_o[L_HD * a:L_HD * a + L_HD, 2 * g + c]
                        nc.tensor.matmul(out, v_main[:, k, h], probs_t[:, g, j, 0], start=True, stop=False, tile_position=(0, L_HD * a))
                        last = nc.tensor.matmul(out, v_side[:, k, h], probs_t[:, g, j, 1], start=False, stop=True,
                                                tile_position=(0, L_HD * a))
                last.then_inc(summed.sem, 1)

            def put_out(i, k, descends):
                m = i * SLOTS4 + k
                pe.wait_ge(o_t_ready.sem, o_t_ready.after(m))
                newest = m + 2 if not isinstance(m, int) else min(m + 2, TILES - 1)
                pe.wait_ge(v_ready.sem, v_ready.after(newest))
                pe.wait_ge(v_sides.sem, v_sides.after(newest))
                if descends:
                    pe.wait_ge(r.made.sem, r.made.after(START + (m + 1 - DESCENT_FIRST) * TURN))
                    nc.tensor.matmul(p_log, r.ones[:], r.part[:], start=True, stop=True).then_inc(r.summed.sem, 1)
                for c in range(PAIR_CHUNKS):
                    last = nc.tensor.matmul(p_y, o_t[:, c], s.wout_l_t[:, c], start=(c == 0), stop=(c == PAIR_CHUNKS - 1))
                last.then_inc(y_done.sem, 1)

            def turn(i, k, has, descends):
                m = i * SLOTS4 + k
                score(i, k, 1, has(1))
                if has(2):
                    project_qk(*at(i, k, 2))
                turn_probs(2 * m, 0)
                if has(-1):
                    put_out(*at(i, k, -1), descends)
                pe.wait_ge(v_sides.sem, v_sides.after(m + 1 if has(1) else m))
                pe.wait_ge(o_t_ready.sem, o_t_ready.after(m - 1))
                weigh(2 * m, k, 0)
                if has(1):
                    score(*at(i, k, 1), 0, has(2))
                turn_probs(2 * m + 1, 1)
                if descends:
                    pe.wait_ge(r.logged.sem, r.logged.after(m - DESCENT_FIRST))
                if has(2):
                    project_v(*at(i, k, 2))
                weigh(2 * m + 1, k, 1)

            def before():
                for k in range(2):
                    project_qk(0, k)
                    project_v(0, k)
                score(0, 0, 0, True)

            def after(i, k):
                put_out(*at(i, k, -1), False)

            loop(pe, before, turn, after)

        @block.scalar
        def _(act):
            for made in (q_ready, k_main, v_sides, exped, p_ready, o_t_ready, light_ready):
                made.open(act)
            act.wait_ge(filled, FILLS)

            def take_qk(i, k):
                n = i * SLOTS4 + k
                act.wait_ge(qk_done.sem, qk_done.after(n))
                q = p_q[:].rearrange("p (c n) -> p c n", c=PAIR_CHUNKS)
                pairs = q_pad[:, k].rearrange("p (c a) n -> p c a n", a=2)
                act.activation(k_window[:, k, :, 0:P], p_k[:].rearrange("p (c n) -> p c n", c=PAIR_CHUNKS), ACT.Copy)\
                   .then_inc(k_main.sem, 1)
                act.activation(pairs[EVEN, :, 0], q[EVEN], ACT.Copy)
                act.activation(pairs[ODD, :, 1], q[ODD], ACT.Copy).then_inc(q_ready.sem, 1)

            def take_v_sides(i, k):
                act.wait_ge(v_ready.sem, v_ready.after(i * SLOTS4 + k))
                v = p_v[:].rearrange("p (h d) -> p h d", h=L_HEADS)
                act.activation(v_side[EVEN, (k - 1) % SLOTS4], v[EVEN], ACT.Copy)
                act.activation(v_side[ODD, (k + 1) % SLOTS4], v[ODD], ACT.Copy).then_inc(v_sides.sem, 1)

            def exps(e, g):
                act.wait_ge(z_ready.sem, z_ready.after(e))
                act.wait_ge(p_turned.sem, p_turned.after(e - 2))
                for j in range(HALF_HEADS):
                    last = act.activation(probs[:, g, j], z[:, g, j], ACT.Exp, scale=L_SCALE, accum_out=den[:, g, j:j + 1])
                last.then_inc(exped.sem, 1)

            def take_probs(e, g):
                act.wait_ge(p_turned.sem, p_turned.after(e))
                act.wait_ge(summed.sem, summed.after(e - 2))
                act.activation(probs_t[:, g], p_p[:], ACT.Copy).then_inc(p_ready.sem, 1)

            def take_light(i, k):
                m = i * SLOTS4 + k
                act.wait_ge(y_done.sem, y_done.after(m))
                act.wait_ge(light_out[k % 2].sem, light_out[k % 2].after(i * 2 + k // 2 - 1))
                act.wait_ge(f_chain.sem, f_chain.after(m - 2))
                act.activation(light[:, k % 2], p_y, ACT.Copy).then_inc(light_ready.sem, 1)

            def turn(i, k, has, descends):
                m = i * SLOTS4 + k
                if has(2):
                    take_qk(*at(i, k, 2))
                take_probs(2 * m, 0)
                exps(2 * m + 1, 1)
                if has(-1):
                    take_light(*at(i, k, -1))
                if descends:
                    act.wait_ge(r.summed.sem, r.summed.after(2 + m - DESCENT_FIRST))
                    act.activation(r.log_sum[:], p_log, ACT.Ln).then_inc(r.logged.sem, 1)
                take_probs(2 * m + 1, 1)
                if has(1):
                    exps(2 * m + 2, 0)
                if has(2):
                    take_v_sides(*at(i, k, 2))
                act.wait_ge(summed.sem, summed.after(2 * m + 1))
                act.wait_ge(y_done.sem, y_done.after(m - 1))
                act.activation(o_t[:], p_o[:], ACT.Copy).then_inc(o_t_ready.sem, 1)
                if descends:
                    act.wait_ge(r.made.sem, r.made.after(START + (m - DESCENT_FIRST) * TURN + 4))
                    act.activation(r.e[:], r.w17[:, :, 0:TILES_B], ACT.Exp, scale=-1.0).then_inc(r.exped.sem, 1)

            def before():
                for k in range(2):
                    take_qk(0, k)
                    take_v_sides(0, k)
                exps(0, 0)

            def after(i, k):
                take_light(*at(i, k, -1))

            loop(act, before, turn, after)

        @block.gpsimd
        def _(pool):
            for made in (k_sides, inverted, rows_ready):
                made.open(pool)
            for k in range(SLOTS4):
                pool.memset(q_pad[:, k].rearrange("p (c a) n -> p c a n", a=2)[ODD, :, 0], 0.0).then_inc(pool_filled, 1)
            pool.wait_ge(pool_filled, SLOTS4)
            pool.wait_ge(filled, FILLS)

            def sides(i, k):
                n, prior, following = i * SLOTS4 + k, (k - 1) % SLOTS4, (k + 1) % SLOTS4
                pool.wait_ge(k_main.sem, k_main.after(n))
                apart(pool, s)
                pool.tensor_copy(k_window[:, prior, :, P:P + WINDOW], k_window[:, k, :, 0:WINDOW])
                pool.tensor_copy(k_window[:, following, :, P + WINDOW:], k_window[:, k, :, WINDOW:P]).then_inc(k_sides.sem, 1)

            def finish(i, k):
                m = i * SLOTS4 + k
                pool.wait_ge(f_chain.sem, f_chain.after(m - 1) + 3)
                apart(pool, s)
                pool.tensor_scalar(inv[:], mean_var[:, 1:2], EPS, None, ALU.add).then_inc(inverted.sem, 1)
                pool.wait_ge(inverted.sem, inverted.after(m - 1) + 1)
                pool.tensor_tensor(inv[:], inv[:], s.power[:, 0:1], ALU.pow).then_inc(inverted.sem, 1)
                pool.wait_ge(f_chain.sem, f_chain.after(m))
                pool.wait_ge(x1_loaded[k].sem, x1_loaded[k].after(i))
                pool.wait_ge(out_out[k % 2].sem, out_out[k % 2].after(i * 2 + k // 2 - 1))
                pool.tensor_tensor(rows[:, k % 2], y[:], x1_in[:, k], ALU.add).then_inc(rows_ready.sem, 1)

            def turn(i, k, has, descends):
                if has(2):
                    sides(*at(i, k, 2))
                if has(-1):
                    finish(*at(i, k, -1))

            def before():
                sides(0, 0)
                sides(0, 1)

            def after(i, k):
                finish(*at(i, k, -1))

            loop(pool, before, turn, after)

        @block.vector
        def _(dve):
            for made in (v_ready, z_ready, diagonal_ready, g_chain, f_chain, r_chain):
                made.open(dve)
            pairs = q_pad[:].rearrange("p s (c a) n -> p s c a n", a=2)
            fills = [(pairs[EVEN, k, :, 1], 0.0) for k in range(SLOTS4)] + [
                (k_window[:, 0, :, P + WINDOW:], 0.0), (v_side[ODD, 0], 0.0), (edge[:], 0.0),
                (z[EVEN, :, :, P:P + WINDOW], OUTSIDE), (z[ODD, :, :, P + WINDOW:], OUTSIDE)]
            for out, value in fills:
                dve.memset(out, value).then_inc(filled, 1)
            dve.wait_ge(filled, len(fills))
            by_batch = edge[:].rearrange("p (b t) -> p b t", b=BATCH)
            dve.memset(by_batch[EVEN, :, 0:1], OUTSIDE).then_inc(filled, 1)
            dve.memset(by_batch[ODD, :, TILES_B - 1:TILES_B], OUTSIDE).then_inc(filled, 1)
            dve.wait_ge(null_loaded, 16)
            dve.sem_inc(filled, 1)
            dve.wait_ge(filled, FILLS)

            def take_v(i, k):
                n = i * SLOTS4 + k
                dve.wait_ge(v_done.sem, v_done.after(n))
                dve.wait_ge(summed.sem, summed.after(2 * (n - SLOTS4) + 1))
                dve.tensor_copy(v_main[:, k], p_v[:].rearrange("p (h d) -> p h d", h=L_HEADS)).then_inc(v_ready.sem, 1)

            def wide(x, rows, n):
                return x[rows].rearrange("p (h a) -> p h a", a=1).broadcast_to([rows.stop - rows.start, HALF_HEADS, n])

            def maxima(e, m, g):
                base = g_chain.after(e - 1)
                out_of = edge[:, bass.ds(m, 1)]
                dve.wait_ge(scored.sem, scored.after(e))
                dve.wait_ge(exped.sem, exped.after(e - 2))
                dve.wait_ge(z_ready.sem, z_ready.after(e - 1))
                dve.tensor_reduce(m_main[:], p_s[:, :, 0:P], AX.X, ALU.max)
                dve.tensor_reduce(m_side[EVEN], p_s[EVEN, :, P + WINDOW:], AX.X, ALU.max)
                dve.tensor_reduce(m_side[ODD], p_s[ODD, :, P:P + WINDOW], AX.X, ALU.max).then_inc(g_chain.sem, 1)
                dve.wait_ge(g_chain.sem, base + 1)
                dve.tensor_scalar(m_side[:], m_side[:], out_of, None, ALU.add).then_inc(g_chain.sem, 1)
                dve.wait_ge(g_chain.sem, base + 2)
                dve.tensor_tensor(m_all[:], m_side[:], m_main[:], ALU.max).then_inc(g_chain.sem, 1)
                dve.wait_ge(g_chain.sem, base + 3)
                dve.tensor_scalar(m_edge[:], m_all[:], out_of, None, ALU.subtract).then_inc(g_chain.sem, 1)
                dve.wait_ge(g_chain.sem, base + 4)
                dve.tensor_tensor(z[:, g, :, 0:P], p_s[:, :, 0:P], wide(m_all, slice(0, P), P), ALU.subtract)
                dve.tensor_tensor(z[EVEN, g, :, P + WINDOW:], p_s[EVEN, :, P + WINDOW:], wide(m_edge, EVEN, WINDOW), ALU.subtract)
                dve.tensor_tensor(z[ODD, g, :, P:P + WINDOW], p_s[ODD, :, P:P + WINDOW], wide(m_edge, ODD, WINDOW), ALU.subtract)\
                   .then_inc(z_ready.sem, 1)

            def shares(e, g):
                dve.wait_ge(exped.sem, exped.after(e))
                dve.wait_ge(p_turned.sem, p_turned.after(e - 2))
                dve.reciprocal(share[:, g], den[:, g]).then_inc(r_chain.sem, 1)
                dve.wait_ge(r_chain.sem, r_chain.after(e))
                dve.tensor_tensor(diagonal[:, g], s.ident[:].rearrange("p (a n) -> p a n", a=1).broadcast_to([P, HALF_HEADS, P]),
                                  wide(share[:, g], slice(0, P), P), ALU.mult).then_inc(diagonal_ready.sem, 1)

            def statistics(i, k):
                m = i * SLOTS4 + k
                base = f_chain.after(m - 1)
                dve.wait_ge(light_ready.sem, light_ready.after(m))
                dve.wait_ge(rows_ready.sem, rows_ready.after(m - 1))
                dve.tensor_tensor(y[:], light[:, k % 2], null_q[:], ALU.add).then_inc(f_chain.sem, 1)
                dve.wait_ge(f_chain.sem, base + 1)
                dve.bn_stats(stats[:], y[:]).then_inc(f_chain.sem, 1)
                dve.wait_ge(f_chain.sem, base + 2)
                apart(dve, s)
                dve.bn_aggr(mean_var[:], stats[:]).then_inc(f_chain.sem, 1)

            def normalise(i, k):
                m = i * SLOTS4 + k
                dve.wait_ge(inverted.sem, inverted.after(m))
                dve.tensor_scalar(y[:], y[:], mean_var[:, 0:1], inv[:, 0:1], ALU.subtract, ALU.mult).then_inc(f_chain.sem, 1)

            def step(instruction, at):
                instruction.then_inc(r.made.sem, 1)
                dve.wait_ge(r.made.sem, r.made.after(at))

            def turn(i, k, has, descends):
                m = i * SLOTS4 + k
                descent = m - DESCENT_FIRST
                base = START + descent * TURN
                shares(2 * m, 0)
                maxima(2 * m + 1, m, 1)
                if descends:
                    dve.wait_ge(r.exped.sem, r.exped.after(descent))
                    step(dve.tensor_reduce(r.part[:], r.e[:], AX.X, ALU.add), base)
                shares(2 * m + 1, 1)
                if has(-1):
                    statistics(*at(i, k, -1))
                if has(1):
                    maxima(2 * m + 2, m + 1, 0)
                if descends:
                    dve.wait_ge(r.logged.sem, r.logged.after(descent))
                    step(dve.tensor_tensor(r.a[:], r.c[:], r.log_sum[:], ALU.subtract), base + 1)
                    exponents(r, dve, base + 2)
                if has(-1):
                    normalise(*at(i, k, -1))
                if has(2):
                    take_v(*at(i, k, 2))

            def before():
                take_v(0, 0)
                take_v(0, 1)
                maxima(0, 0, 0)

            def after(i, k):
                statistics(*at(i, k, -1))
                normalise(*at(i, k, -1))

            loop(dve, before, turn, after)


def route(nc, s):
    r = s.r
    with ExitStack() as ctx:
        def sb(name, shape, dt=fp32):
            return ctx.enter_context(nc.sbuf_tensor(name, shape, dt))

        def ps(name, shape):
            return ctx.enter_context(nc.psum_tensor(name, shape, fp32))

        def steps(name, per=1, lead=2):
            return Steps(ctx.enter_context(nc.semaphore(name)), per, lead)

        T = TILES_B
        tri, reset = sb("tri", [P, P], bf16), sb("reset", [P, ROUTES, T])
        k_of, part, ones = r.k_of, r.part, r.ones
        ones_b = sb("ones_b", [P, P], bf16)
        x, x_clamped, sc = sb("route_x", [P, ROUTES, T]), sb("x_clamped", [P, ROUTES, T]), sb("route_sc", [P, ROUTES, T])
        digits, digits_i = sb("digits", [P, ROUTES, 3]), sb("digits_i", [P, ROUTES, 3], i32)
        unit = sb("unit", [P, 1])
        limit, trial, kept = sb("limit", [P, ROUTES], i32), sb("trial", [P, ROUTES, 3], i32), sb("kept", [P, ROUTES], i32)
        below, tie = sb("below", [P, ROUTES, T]), sb("tie", [P, ROUTES, T], bf16)
        below3, part3, few3 = sb("below3", [P, ROUTES, 3, T]), sb("part3", [P, ROUTES, 3]), sb("few3", [P, ROUTES, 3])
        count, few = sb("count", [P, ROUTES]), sb("few", [P, ROUTES])
        next_digit = ctx.enter_context(nc.semaphore("next_digit"))
        scan, order = sb("scan", [P, ROUTES, T]), sb("order", [P, ROUTES, T])
        chosen, chosen_b, place = sb("chosen", [P, ROUTES, T]), sb("chosen_b", [P, ROUTES, T], bf16), sb("place", [P, ROUTES, T])
        number_i, number = sb("number_i", [P, 2, ROUTES, T], i32), sb("number", [P, ROUTES, T, 3], bf16)
        slot_i, slot = sb("slot_i", [P, N_KV], i32), sb("slot", [P, N_KV], bf16)
        one_hot = sb("one_hot", [P, 2, T, N_KV], bf16)
        token = sb("token", [P, BATCH, ROW_TILES])
        p_sum, p_tri, p_all = ps("p_sum", [P, 512]), ps("p_tri", [P, 512]), ps("p_all", [P, 512])
        p_number = ps("p_number", [P, BATCH, ROW_TILES, 3])

        d, exped, summed = r.made, r.exped, r.summed
        constants_made = ctx.enter_context(nc.semaphore("r_constants"))
        hot, gathered = steps("hot"), steps("hot_used")
        block = ctx.enter_context(nc.Block())

        wide = over_problems
        DIGIT_TURNS, DIGIT_TURN = (FLOAT_BITS - 1) // 2, 7
        SEARCH = START + TURN * (ITERATIONS - 1)
        PREPARE = 5
        LAST_BIT = SEARCH + PREPARE + DIGIT_TURN * DIGIT_TURNS
        SELECT = LAST_BIT + 7
        SUM_BITS = 2 + ITERATIONS - 1
        SUM_LAST = SUM_BITS + DIGIT_TURNS + 1
        numbered = [(b, row, problem) for b in range(BATCH) for row, problem in ((0, BATCH + b), (2, b))]

        @block.gpsimd
        def _(pool):
            pool.memset(ones_b[:], 1.0).then_inc(constants_made, 1)
            pool.memset(tri[:], 1.0).then_inc(constants_made, 1)
            pool.memset(reset[:], 1.0).then_inc(constants_made, 1)
            pool.iota(number_i[:, 0], pattern=[[0, 2], [T, BATCH], [1, T]], base=0, channel_multiplier=0).then_inc(constants_made, 1)
            pool.iota(number_i[:, 1], pattern=[[0, ROUTES], [0, T]], base=0, channel_multiplier=1).then_inc(constants_made, 1)
            pool.iota(slot_i[:], pattern=[[1, N_KV]], base=0, channel_multiplier=0).then_inc(constants_made, 1)
            pool.wait_ge(constants_made, 6)
            pool.affine_select(out=tri[:], in_=tri[:], compare_op=ALU.is_gt, fill=0.0, base=0, pattern=[[1, P]],
                               channel_multiplier=-1).then_inc(constants_made, 1)
            pool.memset(reset[:, :, 0:1], 0.0).then_inc(constants_made, 1)
            pool.tensor_copy(number[:, :, :, 0], number_i[:, 0]).then_inc(constants_made, 1)
            pool.tensor_copy(number[:, :, :, 1], number_i[:, 1]).then_inc(constants_made, 1)
            pool.tensor_copy(slot[:], slot_i[:]).then_inc(constants_made, 1)

        @block.tensor
        def _(pe):
            gathered.open(pe)
            pe.wait_ge(constants_made, 11)

            def total(step):
                pe.wait_ge(d.sem, d.after(step))
                nc.tensor.matmul(p_sum[:, 0:ROUTES], ones[:], part[:], start=True, stop=True).then_inc(summed.sem, 1)

            with pe.Fori(0, DIGIT_TURNS) as i:
                pe.wait_ge(d.sem, d.after(SEARCH + PREPARE + i * DIGIT_TURN + 2))
                nc.tensor.matmul(p_sum[:, 0:3 * ROUTES], ones[:], part3[:].rearrange("p r j -> p (r j)"), start=True, stop=True)\
                  .then_inc(summed.sem, 1)
            total(LAST_BIT + 3)
            total(SELECT + 1)
            for n, (step, what) in enumerate(((SELECT + 3, tie), (SELECT + 12, chosen_b))):
                pe.wait_ge(d.sem, d.after(step))
                flat = what[:].rearrange("p r t -> p (r t)")
                nc.tensor.matmul(p_tri[:, 0:ROUTES * T], tri[:], flat, start=True, stop=True)
                nc.tensor.matmul(p_all[:, 0:ROUTES * T], ones_b[:], flat, start=True, stop=True).then_inc(summed.sem, 1)
            for n, (b, row, problem) in enumerate(numbered):
                pe.wait_ge(hot.sem, hot.after(n))
                for j in range(DRAWN[problem] // P):
                    for t in range(T):
                        last = nc.tensor.matmul(p_number[:, b, row + j], one_hot[:, n % 2, t, P * j:P * j + P],
                                                number[:, problem, t], start=(t == 0), stop=(t == T - 1))
                last.then_inc(gathered.sem, 1)

        @block.scalar
        def _(act):
            act.wait_ge(d.sem, d.after(SEARCH + 1))
            act.activation(sc[:], x[:], ACT.Exp, scale=-1.0).then_inc(exped.sem, 1)

        @block.vector
        def _(dve):
            hot.open(dve)

            def step(instruction, at):
                instruction.then_inc(d.sem, 1)
                dve.wait_ge(d.sem, d.after(at))

            step(dve.tensor_tensor(r.t17[:], r.s17[:], wide(r.a[:], T + 1), ALU.add), SEARCH)
            step(dve.tensor_scalar(x[:], r.t17[:, :, 0:T], -1.0, 0.0, ALU.mult, ALU.max), SEARCH + 1)
            dve.memset(limit[:], 0)
            for j in range(3):
                dve.memset(digits[:, :, j:j + 1], float((j + 1) * 2 ** (FLOAT_BITS - 2)))
            dve.memset(unit[:], float(2 ** (FLOAT_BITS - 2)))
            step(dve.tensor_scalar(x_clamped[:], x[:], LOWEST, None, ALU.min), SEARCH + 2)
            step(dve.tensor_copy(digits_i[:], digits[:]), SEARCH + 3)
            step(dve.tensor_scalar(digits[:], digits[:], 0.25, None, ALU.mult), SEARCH + 4)
            with dve.Fori(0, DIGIT_TURNS) as i:
                base = SEARCH + PREPARE + i * DIGIT_TURN
                step(dve.tensor_tensor(trial[:], limit[:].rearrange("p (r a) -> p r a", a=1).broadcast_to([P, ROUTES, 3]),
                                       digits_i[:], ALU.bitwise_or), base)
                step(dve.tensor_tensor(below3[:], x_clamped[:].rearrange("p r (a t) -> p r a t", a=1).broadcast_to([P, ROUTES, 3, T]),
                                       trial[:].bitcast(fp32).rearrange("p r (j a) -> p r j a", a=1).broadcast_to([P, ROUTES, 3, T]),
                                       ALU.is_lt), base + 1)
                step(dve.tensor_reduce(part3[:], below3[:], AX.X, ALU.add), base + 2)
                dve.tensor_copy(digits_i[:], digits[:]).then_inc(next_digit, 1)
                dve.wait_ge(summed.sem, summed.after(SUM_BITS + i))
                step(dve.tensor_tensor(few3[:], p_sum[:, 0:3 * ROUTES].rearrange("p (r j) -> p r j", j=3),
                                       k_of[:].rearrange("p (r a) -> p r a", a=1).broadcast_to([P, ROUTES, 3]), ALU.is_lt), base + 3)
                step(dve.tensor_reduce(few[:], few3[:], AX.X, ALU.add), base + 4)
                step(dve.tensor_scalar(kept[:], few[:], unit[:, 0:1], None, ALU.mult), base + 5)
                dve.tensor_scalar(unit[:], unit[:], 0.25, None, ALU.mult).then_inc(next_digit, 1)
                dve.wait_ge(next_digit, i * 3 + 2)
                dve.tensor_scalar(digits[:], digits[:], 0.25, None, ALU.mult).then_inc(next_digit, 1)
                step(dve.tensor_tensor(limit[:], limit[:], kept[:], ALU.bitwise_or), base + 6)
                dve.wait_ge(next_digit, i * 3 + 3)
            step(dve.memset(trial[:], 1), LAST_BIT)
            step(dve.tensor_tensor(trial[:, :, 0], limit[:], trial[:, :, 1], ALU.bitwise_or), LAST_BIT + 1)
            last_trial = trial[:, :, 0:1].bitcast(fp32).broadcast_to([P, ROUTES, T])
            step(dve.tensor_tensor(below[:], x_clamped[:], last_trial, ALU.is_lt), LAST_BIT + 2)
            step(dve.tensor_reduce(part[:], below[:], AX.X, ALU.add), LAST_BIT + 3)
            dve.wait_ge(summed.sem, summed.after(SUM_BITS + DIGIT_TURNS))
            step(dve.tensor_tensor(few[:], p_sum[:, 0:ROUTES], k_of[:], ALU.is_lt), LAST_BIT + 4)
            step(dve.tensor_copy(kept[:], few[:]), LAST_BIT + 5)
            step(dve.tensor_tensor(limit[:], limit[:], kept[:], ALU.bitwise_or), LAST_BIT + 6)
            limit_f = wide(limit[:].bitcast(fp32), T)
            step(dve.tensor_tensor(below[:], x_clamped[:], limit_f, ALU.is_lt), SELECT)
            step(dve.tensor_reduce(part[:], below[:], AX.X, ALU.add), SELECT + 1)
            dve.wait_ge(summed.sem, summed.after(SUM_LAST))
            step(dve.tensor_tensor(count[:], k_of[:], p_sum[:, 0:ROUTES], ALU.subtract), SELECT + 2)
            step(dve.tensor_tensor(tie[:], x_clamped[:], limit_f, ALU.is_equal), SELECT + 3)
            dve.wait_ge(summed.sem, summed.after(SUM_LAST + 1))

            def before(at):
                flat = "p r t -> p (r t)"
                every = p_all[:, 0:ROUTES * T]
                step(dve.tensor_tensor_scan(scan[:].rearrange(flat), reset[:].rearrange(flat), every, 0.0, ALU.mult, ALU.add), at)
                step(dve.tensor_tensor(scan[:].rearrange(flat), scan[:].rearrange(flat), every, ALU.subtract), at + 1)
                step(dve.tensor_tensor(order[:].rearrange(flat), scan[:].rearrange(flat), p_tri[:, 0:ROUTES * T], ALU.add), at + 2)

            dve.wait_ge(constants_made, 11)
            before(SELECT + 4)
            step(dve.tensor_tensor(order[:], order[:], wide(count[:], T), ALU.is_lt), SELECT + 7)
            step(dve.tensor_tensor(order[:], order[:], tie[:], ALU.mult), SELECT + 8)
            step(dve.tensor_tensor(chosen[:], order[:], below[:], ALU.add), SELECT + 9)
            dve.wait_ge(exped.sem, exped.after(ITERATIONS))
            step(dve.tensor_scalar(x[:], sc[:], -1.0, 1.0, ALU.mult, ALU.add), SELECT + 10)
            step(dve.tensor_tensor(sc[:], sc[:], x[:], ALU.add), SELECT + 11)
            step(dve.tensor_copy(chosen_b[:], chosen[:]), SELECT + 12)
            step(dve.tensor_scalar(number[:, :, :, 2], sc[:], -1.0, None, ALU.add), SELECT + 13)
            dve.wait_ge(summed.sem, summed.after(SUM_LAST + 2))
            before(SELECT + 14)
            step(dve.scalar_tensor_tensor(place[:], order[:], 1.0, chosen[:], ALU.add, ALU.mult), SELECT + 17)
            step(dve.tensor_scalar(place[:], place[:], -1.0, None, ALU.add), SELECT + 18)
            for n, (b, row, problem) in enumerate(numbered):
                dve.wait_ge(gathered.sem, gathered.after(n - 2))
                k = DRAWN[problem]
                for t in range(T):
                    last = dve.tensor_scalar(one_hot[:, n % 2, t, 0:k], slot[:, 0:k], place[:, problem, t:t + 1], None, ALU.is_equal)
                last.then_inc(hot.sem, 1)
            dve.wait_ge(gathered.sem, gathered.after(len(numbered) - 1))
            step(dve.tensor_scalar(token[:], p_number[:, :, :, 0], float(P), None, ALU.mult), SELECT + 19)
            step(dve.tensor_tensor(token[:], token[:], p_number[:, :, :, 1], ALU.add), SELECT + 20)
            step(dve.tensor_copy(s.token_i[:], token[:]), SELECT + 21)
            step(dve.tensor_scalar(s.weight[:], p_number[:, :, :, 2], 1.0, None, ALU.add), SELECT + 22)


def heavy(nc, s):
    with ExitStack() as ctx:
        def sb(name, shape, dt=fp32):
            return ctx.enter_context(nc.sbuf_tensor(name, shape, dt))

        def ps(name, shape):
            return ctx.enter_context(nc.psum_tensor(name, shape, fp32))

        def steps(name, per=1, lead=4):
            return Steps(ctx.enter_context(nc.semaphore(name)), per, lead)

        EVEN, ODD = slice(0, L_HD), slice(L_HD, P)
        KEYS, ALL_ROWS = N_KV, N_KV + N_Q
        rows_in = sb("rows_in", [P, BATCH, ROW_TILES, DIM])
        x1_rows, light_rows = sb("x1_rows", [P, BATCH, DIM]), sb("h_light_rows", [P, BATCH, DIM])
        out_rows = sb("h_out_rows", [P, BATCH, DIM])
        gamma = sb("gamma", [P, HALVES])
        null_k, null_v = sb("null_k", [P, PAIR_CHUNKS]), sb("null_v", [P, L_HEADS, L_HD + 1])
        own_rows = sb("own_rows", [P, ROW_TILES, DIM])
        squares, square_sum = sb("squares", [P, ROW_TILES, DIM]), sb("square_sum", [P, ROW_TILES])
        norm, inv_norm = sb("norm", [P, ROW_TILES]), sb("inv_norm", [P, ROW_TILES])
        rms = sb("rms", [P, ROW_TILES, DIM])
        rms_t = sb("rms_t", [P, HALVES, ALL_ROWS])
        q_pad = sb("h_q_pad", [P, L_HEADS, P])
        keys, vals = sb("h_keys", [P, PAIR_CHUNKS, KEYS]), sb("h_vals", [P, 2, L_HEADS, L_HD + 1])
        m, m_null = sb("h_m", [P, HALF_HEADS]), sb("h_m_null", [P, L_HEADS])
        z, z_null = sb("h_z", [P, HALF_HEADS, KEYS]), sb("h_z_null", [P, HALF_HEADS])
        probs, p_null = sb("h_probs", [P, HALF_HEADS, KEYS]), sb("h_p_null", [P, HALF_HEADS])
        probs_t = sb("h_probs_t", [P, HALF_HEADS, 2, P])
        o_null, o_all, den = sb("o_null", [P, HALF_HEADS, L_HD + 1]), sb("o_all", [P, HALF_HEADS, L_HD + 1]), sb("h_den", [P, HALF_HEADS])
        o_n, o_t = sb("h_o_n", [P, L_HEADS, L_HD]), sb("h_o_t", [P, PAIR_CHUNKS, P])
        y = sb("h_y", [P, DIM])
        stats, mean_var, inv = sb("stats4", [P, 6]), sb("mean_var4", [P, 2]), sb("inv4", [P, 1])
        p_rms = ps("p_rms", [P, HALVES, 512])
        p_keys = p_rms[:].rearrange("p k (c n) -> p (k c) n", c=2)
        p_scores = ps("p_scores", [P, HALF_HEADS, KEYS])
        p_probs = ps("p_probs", [P, HALF_HEADS, 2, P])
        p_q, p_o = ps("h_p_q", [P, 512]), ps("h_p_o", [P, 512])
        p_null_s = p_o[:, 384:384 + L_HEADS]
        sums = p_o[:, 0:HALF_HEADS * (L_HD + 1)].rearrange("p (h d) -> p h d", h=HALF_HEADS)

        loaded, filled = ctx.enter_context(nc.semaphore("h_loaded")), ctx.enter_context(nc.semaphore("h_filled"))
        first_loaded, rows_loaded = (ctx.enter_context(nc.semaphore(name)) for name in ("first_rows_loaded", "rows_loaded"))
        scattered = ctx.enter_context(nc.semaphore("scattered"))
        copied = steps("own_copied")
        squared, rooted, rms_chain = steps("squared2"), steps("rooted", 2), steps("rms_chain", 2)
        rms_turned, rms_t_ready, projected, vals_done = steps("rms_turned"), steps("rms_t_ready"), steps("h_projected"), steps("vals_done")
        keys_done, keys_ready = steps("h_keys_done"), steps("h_keys_ready")
        qk_ready, vals_ready, null_scored = steps("h_qk_ready"), steps("h_vals_ready"), steps("null_scored")
        scored, z_chain, z_ready, exped = steps("h_scored"), steps("z_chain", 3), steps("h_z_ready"), steps("h_exped")
        p_turned, p_ready, summed = steps("h_p_turned"), steps("h_p_ready"), steps("h_summed")
        null_added, o_chain, o_ready = steps("null_weighed"), steps("o_chain", 2), steps("h_o_ready")
        o_turned, o_t_ready, y_done = steps("h_o_turned"), steps("h_o_t_ready"), steps("h_y_done")
        y_chain, inverted, rows_ready = steps("y_chain", 5), steps("inverted4", 2), steps("h_rows_ready")
        m_null_ready = steps("m_null_ready")
        block = ctx.enter_context(nc.Block())

        @block.sync
        def _(sp):
            sp.dma_start(gamma[:], s.d_gamma.rearrange("(k p) -> p k", p=P), allow_slow_non_contiguous=True).then_inc(loaded, 16)
            sp.dma_start(null_k[:], s.d_null_kv[0].rearrange("(c a) d -> (a d) c", a=2), allow_slow_non_contiguous=True).then_inc(loaded, 16)
            sp.wait_ge(filled, 3)
            sp.dma_start(null_v[:, :, 0:L_HD], s.d_null_kv[1:2].broadcast_to([P, L_HEADS, L_HD])).then_inc(loaded, 16)

        @block.gpsimd
        def _(pool):
            for made in (rooted, inverted, rows_ready):
                made.open(pool)
            flat = "t p d -> (t p) d"

            def gather(b, gathered):
                sources = [(rows_in[:, b, r], s.d_h, r) for r in range(ROW_TILES)]
                sources += [(x1_rows[:, b], s.d_x1, 2), (light_rows[:, b], s.d_light, 2)]
                for target, source, r in sources:
                    pool.indirect_dma_start(out=target, out_offset=None, in_=source.rearrange(flat),
                                            in_offset=bass.IndirectOffsetOnAxis(ap=s.token_i[:, b, r:r + 1], axis=0))\
                        .then_inc(gathered, 16)

            def root(b):
                pool.wait_ge(squared.sem, squared.after(b))
                pool.tensor_tensor(norm[:], square_sum[:], s.half[:, 0:ROW_TILES], ALU.pow).then_inc(rooted.sem, 1)
                pool.wait_ge(rooted.sem, rooted.after(b - 1) + 1)
                apart(pool, s)
                pool.tensor_scalar(norm[:], norm[:], 1e-12, None, ALU.max).then_inc(rooted.sem, 1)

            def finish(b):
                pool.wait_ge(y_chain.sem, y_chain.after(b - 1) + 4)
                apart(pool, s)
                pool.tensor_scalar(inv[:], mean_var[:, 1:2], EPS, None, ALU.add).then_inc(inverted.sem, 1)
                pool.wait_ge(inverted.sem, inverted.after(b - 1) + 1)
                pool.tensor_tensor(inv[:], inv[:], s.power[:, 0:1], ALU.pow).then_inc(inverted.sem, 1)
                pool.wait_ge(y_chain.sem, y_chain.after(b))
                pool.tensor_tensor(out_rows[:, bass.ds(b, 1)].rearrange("p a d -> p (a d)"), y[:],
                                   x1_rows[:, bass.ds(b, 1)].rearrange("p a d -> p (a d)"), ALU.add).then_inc(rows_ready.sem, 1)

            gather(0, first_loaded)
            root(0)
            for b in range(1, BATCH):
                gather(b, rows_loaded)
            with pool.Fori(0, BATCH - 1) as b:
                root(b + 1)
                finish(b)
            finish(BATCH - 1)
            pool.wait_ge(rows_ready.sem, rows_ready.after(BATCH - 1))
            for b in range(BATCH):
                pool.indirect_dma_start(out=s.d_out.rearrange(flat), out_offset=bass.IndirectOffsetOnAxis(ap=s.token_i[:, b, 2:3], axis=0),
                                        in_=out_rows[:, b], in_offset=None).then_inc(scattered, 16)
            pool.wait_ge(scattered, 16 * BATCH)

        @block.tensor
        def _(pe):
            for made in (rms_turned, keys_done, projected, vals_done, null_scored, scored, p_turned, summed, o_turned, y_done):
                made.open(pe)
            pe.wait_ge(filled, 3)
            pe.wait_ge(loaded, 48)

            def turn_rows(b):
                pe.wait_ge(rms_chain.sem, rms_chain.after(b))
                pe.wait_ge(y_chain.sem, y_chain.after(b - 3) + 1)
                for r in range(ROW_TILES):
                    for k in range(HALVES):
                        last = nc.tensor.transpose(p_rms[:, k, P * r:P * r + P], rms[:, r, P * k:P * k + P], s.ident[:])
                last.then_inc(rms_turned.sem, 1)

            def project(b):
                pe.wait_ge(rms_t_ready.sem, rms_t_ready.after(b))
                for c in range(PAIR_CHUNKS):
                    for k in range(HALVES):
                        w = s.wkv_h_t[:, k, 0, 2 * c:2 * c + 2].rearrange("p h d -> p (h d)")
                        last = nc.tensor.matmul(p_keys[:, c], w, rms_t[:, k, 0:KEYS], start=(k == 0), stop=(k == HALVES - 1))
                last.then_inc(keys_done.sem, 1)
                pe.wait_ge(o_t_ready.sem, o_t_ready.after(b - 1))
                for c in range(PAIR_CHUNKS):
                    for k in range(HALVES):
                        last = nc.tensor.matmul(p_q[:, P * c:P * c + P], s.wq_h_t[:, k, P * c:P * c + P], rms_t[:, k, KEYS:ALL_ROWS],
                                                start=(k == 0), stop=(k == HALVES - 1))
                last.then_inc(projected.sem, 1)
                pe.wait_ge(keys_ready.sem, keys_ready.after(b))
                for r in range(2):
                    for k in range(HALVES):
                        w = s.wkv_h_t[:, k, 1].rearrange("p h d -> p (h d)")
                        last = nc.tensor.matmul(p_rms[:, r], rms_t[:, k, P * r:P * r + P], w, start=(k == 0), stop=(k == HALVES - 1))
                last.then_inc(vals_done.sem, 1)
                pe.wait_ge(qk_ready.sem, qk_ready.after(b))
                pe.wait_ge(o_chain.sem, o_chain.after(b * 2 - 1))
                for h in range(L_HEADS):
                    last = nc.tensor.matmul(p_null_s[:, h:h + 1], q_pad[:, h], null_k[:, h // 2:h // 2 + 1], start=True, stop=True)
                last.then_inc(null_scored.sem, 1)

            def score(b, g):
                e = b * 2 + g
                pe.wait_ge(z_ready.sem, z_ready.after(e - 1))
                for j in range(HALF_HEADS):
                    h = g * HALF_HEADS + j
                    last = nc.tensor.matmul(p_scores[:, j], q_pad[:, h], keys[:, h // 2], start=True, stop=True)
                last.then_inc(scored.sem, 1)

            def turn_probs(b, g):
                e = b * 2 + g
                pe.wait_ge(exped.sem, exped.after(e))
                pe.wait_ge(p_ready.sem, p_ready.after(e - 1))
                for j in range(HALF_HEADS):
                    for r in range(2):
                        last = nc.tensor.transpose(p_probs[:, j, r], probs[:, j, P * r:P * r + P], s.ident[:])
                last.then_inc(p_turned.sem, 1)

            def weigh(b, g):
                e = b * 2 + g
                pe.wait_ge(p_ready.sem, p_ready.after(e))
                pe.wait_ge(vals_ready.sem, vals_ready.after(b))
                pe.wait_ge(o_chain.sem, o_chain.after(e - 1))
                pe.wait_ge(m_null_ready.sem, m_null_ready.after(b))
                for j in range(HALF_HEADS):
                    h = g * HALF_HEADS + j
                    for r in range(2):
                        last = nc.tensor.matmul(sums[:, j], probs_t[:, j, r], vals[:, r, h], start=(r == 0), stop=(r == 1))
                last.then_inc(summed.sem, 1)

            def turn_sums(b):
                pe.wait_ge(o_ready.sem, o_ready.after(b * 2 + 1))
                for c in range(PAIR_CHUNKS):
                    last = nc.tensor.transpose(p_q[:, P * c:P * c + P], o_n[:, 2 * c:2 * c + 2].rearrange("p h d -> p (h d)"), s.ident[:])
                last.then_inc(o_turned.sem, 1)

            def put_out(b, newest):
                pe.wait_ge(o_t_ready.sem, o_t_ready.after(b))
                pe.wait_ge(vals_ready.sem, vals_ready.after(newest))
                for c in range(PAIR_CHUNKS):
                    last = nc.tensor.matmul(p_rms[:, 0, 0:DIM], o_t[:, c], s.wout_h_t[:, c], start=(c == 0), stop=(c == PAIR_CHUNKS - 1))
                last.then_inc(y_done.sem, 1)

            def attention(b):
                turn_probs(b, 0)
                score(b, 1)
                weigh(b, 0)
                turn_probs(b, 1)
                weigh(b, 1)

            turn_rows(0)
            project(0)
            score(0, 0)
            with pe.Fori(0, BATCH - 1) as b:
                attention(b)
                turn_rows(b + 1)
                turn_sums(b)
                project(b + 1)
                score(b + 1, 0)
                put_out(b, b + 1)
            attention(BATCH - 1)
            turn_sums(BATCH - 1)
            put_out(BATCH - 1, BATCH - 1)

        @block.scalar
        def _(act):
            for made in (rms_t_ready, keys_ready, qk_ready, exped, p_ready, o_t_ready):
                made.open(act)
            act.wait_ge(loaded, 48)
            act.wait_ge(filled, 3)

            def take_rows(b):
                act.wait_ge(rms_turned.sem, rms_turned.after(b))
                for k in range(HALVES):
                    last = act.activation(rms_t[:, k], p_rms[:, k, 0:ALL_ROWS], ACT.Copy, scale=gamma[:, k:k + 1])
                last.then_inc(rms_t_ready.sem, 1)

            def take_projections(b):
                act.wait_ge(keys_done.sem, keys_done.after(b))
                act.activation(keys[:], p_keys, ACT.Copy).then_inc(keys_ready.sem, 1)
                act.wait_ge(projected.sem, projected.after(b))
                q = p_q[:].rearrange("p (c n) -> p c n", c=PAIR_CHUNKS)
                pairs = q_pad[:].rearrange("p (c a) n -> p c a n", a=2)
                act.activation(pairs[EVEN, :, 0], q[EVEN], ACT.Copy)
                act.activation(pairs[ODD, :, 1], q[ODD], ACT.Copy).then_inc(qk_ready.sem, 1)

            def exps(b, g):
                e = b * 2 + g
                act.wait_ge(z_ready.sem, z_ready.after(e))
                act.wait_ge(p_turned.sem, p_turned.after(e - 1))
                act.wait_ge(null_added.sem, null_added.after(e - 1))
                act.activation(p_null[:], z_null[:], ACT.Exp, scale=L_SCALE)
                act.activation(probs[:], z[:], ACT.Exp, scale=L_SCALE).then_inc(exped.sem, 1)

            def take_probs(b, g):
                e = b * 2 + g
                act.wait_ge(p_turned.sem, p_turned.after(e))
                act.wait_ge(summed.sem, summed.after(e - 1))
                act.activation(probs_t[:], p_probs[:], ACT.Copy).then_inc(p_ready.sem, 1)

            def take_sums(b):
                act.wait_ge(o_turned.sem, o_turned.after(b))
                act.wait_ge(y_done.sem, y_done.after(b - 1))
                act.activation(o_t[:], p_q[:].rearrange("p (c n) -> p c n", c=PAIR_CHUNKS), ACT.Copy).then_inc(o_t_ready.sem, 1)

            def attention(b):
                take_probs(b, 0)
                exps(b, 1)
                take_probs(b, 1)

            take_rows(0)
            take_projections(0)
            exps(0, 0)
            with act.Fori(0, BATCH - 1) as b:
                attention(b)
                take_rows(b + 1)
                take_sums(b)
                take_projections(b + 1)
                exps(b + 1, 0)
            attention(BATCH - 1)
            take_sums(BATCH - 1)

        @block.vector
        def _(dve):
            for made in (copied, squared, rms_chain, vals_ready, m_null_ready, z_chain, z_ready, null_added, o_chain, o_ready, y_chain):
                made.open(dve)
            dve.memset(q_pad[:], 0.0).then_inc(filled, 1)
            dve.memset(vals[:], 1.0).then_inc(filled, 1)
            dve.memset(null_v[:], 1.0).then_inc(filled, 1)
            dve.wait_ge(loaded, 48)
            dve.wait_ge(first_loaded, 16 * 5)

            def wide(x, n):
                return x.rearrange("p (h a) -> p h a", a=1).broadcast_to([P, HALF_HEADS, n])

            def normalise(b):
                rows = rows_in[:, bass.ds(b, 1)].rearrange("p a r d -> p (a r) d")
                dve.tensor_copy(own_rows[:], rows).then_inc(copied.sem, 1)
                dve.wait_ge(copied.sem, copied.after(b))
                for r in range(ROW_TILES):
                    last = dve.tensor_tensor_reduce(out=squares[:, r], in0=own_rows[:, r], in1=own_rows[:, r], scale=1.0, scalar=0.0,
                                                    op0=ALU.mult, op1=ALU.add, accum_out=square_sum[:, r:r + 1])
                last.then_inc(squared.sem, 1)
                dve.wait_ge(rooted.sem, rooted.after(b))
                dve.reciprocal(inv_norm[:], norm[:]).then_inc(rms_chain.sem, 1)
                dve.wait_ge(rms_chain.sem, rms_chain.after(b - 1) + 1)
                dve.wait_ge(rms_turned.sem, rms_turned.after(b - 1))
                for r in range(ROW_TILES):
                    last = dve.tensor_scalar(rms[:, r], own_rows[:, r], inv_norm[:, r:r + 1], float(DIM) ** 0.5, ALU.mult, ALU.mult)
                last.then_inc(rms_chain.sem, 1)

            def take_values(b):
                dve.wait_ge(vals_done.sem, vals_done.after(b))
                dve.wait_ge(summed.sem, summed.after(b * 2 - 1))
                for r in range(2):
                    last = dve.tensor_scalar(vals[:, r, :, 0:L_HD], p_rms[:, r].rearrange("p (h d) -> p h d", h=L_HEADS),
                                             s.weight[:, bass.ds(b, 1), r], None, ALU.mult)
                last.then_inc(vals_ready.sem, 1)
                dve.wait_ge(null_scored.sem, null_scored.after(b))
                dve.tensor_copy(m_null[:], p_null_s).then_inc(m_null_ready.sem, 1)
                dve.wait_ge(m_null_ready.sem, m_null_ready.after(b))

            def maxima(b, g):
                e = b * 2 + g
                null_s = m_null[:, HALF_HEADS * g:HALF_HEADS * (g + 1)]
                dve.wait_ge(scored.sem, scored.after(e))
                dve.tensor_reduce(m[:], p_scores[:], AX.X, ALU.max).then_inc(z_chain.sem, 1)
                dve.wait_ge(z_chain.sem, z_chain.after(e - 1) + 1)
                dve.tensor_tensor(m[:], m[:], null_s, ALU.max).then_inc(z_chain.sem, 1)
                dve.wait_ge(z_chain.sem, z_chain.after(e - 1) + 2)
                dve.wait_ge(exped.sem, exped.after(e - 1))
                dve.tensor_tensor(z_null[:], null_s, m[:], ALU.subtract).then_inc(z_chain.sem, 1)
                dve.tensor_tensor(z[:], p_scores[:], wide(m[:], KEYS), ALU.subtract).then_inc(z_ready.sem, 1)

            def weigh_null(b, g):
                e = b * 2 + g
                dve.wait_ge(exped.sem, exped.after(e))
                dve.wait_ge(o_chain.sem, o_chain.after(e - 1))
                dve.tensor_tensor(o_null[:], null_v[:, HALF_HEADS * g:HALF_HEADS * (g + 1)], wide(p_null[:], L_HD + 1), ALU.mult)\
                   .then_inc(null_added.sem, 1)

            def divide(b, g):
                e = b * 2 + g
                dve.wait_ge(null_added.sem, null_added.after(e))
                dve.wait_ge(summed.sem, summed.after(e))
                dve.tensor_tensor(o_all[:], sums, o_null[:], ALU.add).then_inc(o_chain.sem, 1)
                dve.wait_ge(o_chain.sem, o_chain.after(e - 1) + 1)
                dve.reciprocal(den[:], o_all[:, :, L_HD]).then_inc(o_chain.sem, 1)
                dve.wait_ge(o_chain.sem, o_chain.after(e))
                dve.wait_ge(o_turned.sem, o_turned.after(b - 1))
                dve.tensor_tensor(o_n[:, HALF_HEADS * g:HALF_HEADS * (g + 1)], o_all[:, :, 0:L_HD], wide(den[:], L_HD), ALU.mult)\
                   .then_inc(o_ready.sem, 1)

            def finish(b):
                base = y_chain.after(b - 1)
                dve.wait_ge(y_done.sem, y_done.after(b))
                dve.wait_ge(rows_ready.sem, rows_ready.after(b - 1))
                dve.tensor_scalar(y[:], p_rms[:, 0, 0:DIM], s.weight[:, bass.ds(b, 1), 2], None, ALU.mult).then_inc(y_chain.sem, 1)
                dve.wait_ge(y_chain.sem, base + 1)
                dve.tensor_tensor(y[:], y[:], light_rows[:, bass.ds(b, 1)].rearrange("p a d -> p (a d)"), ALU.add).then_inc(y_chain.sem, 1)
                dve.wait_ge(y_chain.sem, base + 2)
                dve.bn_stats(stats[:], y[:]).then_inc(y_chain.sem, 1)
                dve.wait_ge(y_chain.sem, base + 3)
                apart(dve, s)
                dve.bn_aggr(mean_var[:], stats[:]).then_inc(y_chain.sem, 1)
                dve.wait_ge(inverted.sem, inverted.after(b))
                dve.tensor_scalar(y[:], y[:], mean_var[:, 0:1], inv[:, 0:1], ALU.subtract, ALU.mult).then_inc(y_chain.sem, 1)

            def attention(b):
                weigh_null(b, 0)
                maxima(b, 1)
                divide(b, 0)
                weigh_null(b, 1)

            normalise(0)
            take_values(0)
            maxima(0, 0)
            dve.wait_ge(rows_loaded, 16 * 5 * (BATCH - 1))
            with dve.Fori(0, BATCH - 1) as b:
                attention(b)
                normalise(b + 1)
                divide(b, 1)
                take_values(b + 1)
                maxima(b + 1, 0)
                finish(b)
            attention(BATCH - 1)
            divide(BATCH - 1, 1)
            finish(BATCH - 1)


def build(nc, ins, out, debug=None):
    with ExitStack() as ctx:
        s = Memory()
        kind = "ExternalOutput" if debug else "Internal"

        def dram(name, shape, dt=fp32):
            return nc.dram_tensor(name, shape, dt, kind=kind).ap()

        def sb(name, shape, dt=fp32):
            return ctx.enter_context(nc.sbuf_tensor(name, shape, dt))

        (x, s.d_w_q, s.d_b_q, s.d_w_k, s.d_b_k, s.d_w_v, s.d_b_v, s.d_w_o, s.d_b_o, s.d_ln_w, s.d_ln_b, s.d_wqkv,
         s.d_wout_l, s.d_rt_q, s.d_rt_kv, s.d_gamma, s.d_wq_h, s.d_wkv_h, s.d_wout_h, s.d_null_kv, s.d_null_q) = ins
        s.d_x = x.rearrange("b (t p) d -> (b t) p d", p=P)
        q_parts = dram("q_parts", [PARTS, BATCH * HALVES, P, SEQ], bf16)
        k_parts = dram("k_parts", [PARTS, BATCH, KVD, SEQ], bf16)
        shift = dram("shift", [2, BATCH * HEADS, SEQ], bf16)
        attended = dram("attended", [BATCH * HALVES, P, SEQ])
        s.d_q_parts, s.d_k_parts, s.d_shift = q_parts, k_parts, shift
        s.q_rows = q_parts.rearrange("r b (h p) n -> r (b h) p n", p=HD)
        s.k_rows = k_parts.rearrange("r b (h p) n -> r (b h) p n", p=HD)
        s.a_rows = attended.rearrange("b (h p) n -> (b h) p n", p=HD).rearrange("(j h) p n -> j h p n", h=GROUP)
        s.d_attended = attended
        s.d_x1, s.d_h = dram("x1", [TILES, P, DIM]), dram("h", [TILES, P, DIM])
        s.d_u_t = dram("u_t", [P, HALVES, TOKENS])
        s.d_light = dram("light", [TILES, P, DIM])
        s.d_out = out.rearrange("b (t p) d -> (b t) p d", p=P)
        s.ident = sb("ident", [P, P])
        s.passed = {engine.engine: ctx.enter_context(nc.semaphore(f"passed_{name}"))
                    for name, engine in (("pe", nc.tensor), ("dve", nc.vector), ("pool", nc.gpsimd), ("sp", nc.sync))}
        s.power, s.half = sb("power", [P, 16]), sb("half", [P, 16])
        s.w_o, s.b_o, s.rt = sb("w_o", [P, HALVES, DIM]), sb("b_o", [1, DIM]), sb("rt", [P, 2, DIM])
        s.ln_w, s.ln_b = sb("ln_w", [P, HALVES]), sb("ln_b", [P, HALVES])
        s.later_loaded = ctx.enter_context(nc.semaphore("later_loaded"))
        s.token_i, s.weight = sb("token_i", [P, BATCH, ROW_TILES], i32), sb("weight", [P, BATCH, ROW_TILES])
        s.route_s = sb("route_s", [P, 2, TILES])
        with ExitStack() as first:
            def sb1(name, shape, dt=fp32):
                return first.enter_context(nc.sbuf_tensor(name, shape, dt))
            s.heads_of = sb1("heads_of", [P, 8])
            s.norm_sel = sb1("norm_sel", [P, 3, 20], bf16)
            s.zero_row = sb1("zero_row", [P, SEQ], bf16)
            s.ident_b, s.behind = sb1("ident_b", [P, P], bf16), sb1("behind", [P, P], bf16)
            s.norm_max = sb1("norm_max", [20, BATCH * BLOCKS_B])
            s.v_all = sb1("v_all", [P, BATCH * KV, TILES_B, 2 * HD])
            s.k_stack = sb1("k_stack", [P, 2, SEQ], bf16)
            s.w_q, s.w_k, s.w_v = sb1("w_q", [P, HALVES, DIM]), sb1("w_k", [P, HALVES, KVD]), sb1("w_v", [P, HALVES, KVD])
            s.b_q, s.b_k, s.b_v = sb1("b_q", [P, HALVES]), sb1("b_k", [KVD, 1]), sb1("b_v", [P, KVD])
            constants(nc, s)
            s.loose = sb1("loose", [1, 1], i32)
            project(nc, s)
            bound_scores(nc, s)
            largest_scores(nc, s)
            attend(nc, s)
        s.w_qkv_t, s.wout_l_t = sb("w_qkv_t", [P, HALVES, 3 * 512]), sb("wout_l_t", [P, 4, DIM])
        s.wq_h_t, s.wkv_h_t, s.wout_h_t = sb("wq_h_t", [P, HALVES, 512]), sb("wkv_h_t", [P, HALVES, 2, L_HEADS, L_HD]), sb("wout_h_t", [P, 4, DIM])
        merge(nc, s)
        route_start(nc, s, ctx)
        local(nc, s)
        route(nc, s)
        heavy(nc, s)


_INS = ["L0_attn_x", "L0_attn_w_q", "L0_attn_b_q", "L0_attn_w_k", "L0_attn_b_k", "L0_attn_w_v", "L0_attn_b_v", "L0_attn_w_o",
        "L0_attn_b_o", "L0_ffn_ln_w", "L0_ffn_ln_b", "L0_ffn_Wqkv", "L0_ffn_Wout_l", "L0_ffn_rt_q", "L0_ffn_rt_kv", "L0_ffn_gamma",
        "L0_ffn_Wq", "L0_ffn_Wkv", "L0_ffn_Wout_h", "L0_ffn_null_kv", "L0_ffn_null_q"]


def kernel(**inputs):
    import numpy as _np
    import concourse.bacc as _bacc
    from concourse import mybir as _mybir
    from concourse.bass_utils import run_bass_kernel_spmd as _run

    nc = _bacc.Bacc("TRN2", target_bir_lowering=False, num_devices=1)
    arrays, args = {}, []
    for name in _INS:
        a = _np.ascontiguousarray(inputs[name])
        arrays[f"in_{name}"] = a
        args.append(nc.dram_tensor(f"in_{name}", a.shape, _mybir.dt.from_np(a.dtype), kind="ExternalInput").ap())
    out = nc.dram_tensor("out", (BATCH, SEQ, DIM), _mybir.dt.float32, kind="ExternalOutput").ap()
    build(nc, args, out)
    r = _run(nc, [arrays], core_ids=[0])
    return r.results[0]["out"]
```
